# Optimizing a Trainium2 kernel written in Bass

```python
import numpy as np
import jax
import jax.numpy as jnp

def _softmax(x, axis=-1):
    return jax.nn.softmax(x, axis=axis)

def _gelu(x):
    return jax.nn.gelu(x, approximate=True)

def _silu(x):
    return jax.nn.silu(x)

def _sigmoid(x):
    return jax.nn.sigmoid(x)

def _layernorm(x, axis=-1, eps=1e-05):
    m = jnp.mean(x, axis=axis, keepdims=True)
    v = jnp.var(x, axis=axis, keepdims=True)
    return (x - m) / jnp.sqrt(v + eps)

def _scatter_add(tgt, idx, src, axis=0):
    return tgt.at[idx].add(src)

def _segment_sum(src, seg, n):
    return jax.ops.segment_sum(src, seg, n)
kernel_name = 'mk_seq_postln_d1_jaxref_r4_0086e5'

def setup_inputs(seed: int=0):
    np.random.seed(seed)
    _w = jnp.asarray

    def _L0_attn_setup():
        import jax, jax.numpy as jnp
        import numpy as np
        import math
        B, L, E, H, K = (4, 256, 256, 16, 64)
        D = E // H

        def _attend(q, in_proj_weight, in_proj_bias, out_w, out_b, rel_pe):
            b, l, e = q.shape
            h, d = (H, D)
            qkv = q @ in_proj_weight.T + in_proj_bias
            qh, kh, vh = jnp.split(qkv, 3, axis=-1)
            qh = qh.reshape(b, l, h, d).transpose(0, 2, 1, 3)
            kh = kh.reshape(b, l, h, d).transpose(0, 2, 1, 3)
            vh = vh.reshape(b, l, h, d).transpose(0, 2, 1, 3)
            qh = qh / math.sqrt(d)
            scores = jnp.einsum('bhid,bhjd->bhij', qh, kh)
            pos = jnp.arange(l)
            rel = jnp.clip(pos[None, :] - pos[:, None], -K, K) + K
            bias_r = jnp.einsum('bhid,rd->bhir', qh, rel_pe)
            bias = jnp.take_along_axis(bias_r, jnp.broadcast_to(rel[None, None], (b, h, l, l)), axis=-1)
            attn = jax.nn.softmax(scores + bias, axis=-1)
            out = jnp.einsum('bhij,bhjd->bhid', attn, vh)
            out = out.transpose(0, 2, 1, 3).reshape(b, l, e)
            return out @ out_w.T + out_b
        key = jax.random.key(seed)
        ks = jax.random.split(key, 4)
        s = 1.0 / math.sqrt(E)
        return {'q': jax.random.normal(ks[0], (B, L, E), dtype=jnp.float32), 'in_proj_weight': jax.random.normal(ks[1], (3 * E, E), dtype=jnp.float32) * s, 'in_proj_bias': jnp.zeros((3 * E,), dtype=jnp.float32), 'out_w': jax.random.normal(ks[2], (E, E), dtype=jnp.float32) * s, 'out_b': jnp.zeros((E,), dtype=jnp.float32), 'rel_pe': jax.random.normal(ks[3], (2 * K + 1, D), dtype=jnp.float32) * (1.0 / math.sqrt(D))}
    _L0_attn_in = _L0_attn_setup()

    def _L0_ffn_setup():
        import jax, jax.numpy as jnp
        import numpy as np
        DIM = 256
        DEPTH = 2
        HEADS = 8
        DIM_HEAD = 64
        WINDOW = 128
        INNER = HEADS * DIM_HEAD
        HID = int(DIM * 4 * 2 / 3)
        B, N = (2, 2048)
        QK_SCALE = 8.0

        def shift_token(t):
            t1, t2 = jnp.split(t, 2, axis=-1)
            t2 = jnp.pad(t2, ((0, 0), (1, 0), (0, 0)))[:, :-1]
            return jnp.concatenate([t1, t2], axis=-1)

        def l2norm(t):
            return t / jnp.clip(jnp.linalg.norm(t, axis=-1, keepdims=True), 1e-12)

        def rotate_half(x):
            x1, x2 = jnp.split(x, 2, axis=-1)
            return jnp.concatenate([-x2, x1], axis=-1)

        def rotary_xpos(q, k):
            n = q.shape[-2]
            half_idx = jnp.arange(0, DIM_HEAD, 2, dtype=jnp.float32)
            inv_freq = 1.0 / 10000.0 ** (half_idx / DIM_HEAD)
            t = jnp.arange(n, dtype=jnp.float32)
            freqs = t[:, None] * inv_freq[None, :]
            freqs = jnp.concatenate([freqs, freqs], axis=-1)
            base = (half_idx + 0.4 * DIM_HEAD) / (1.4 * DIM_HEAD)
            power = (t - n // 2) / float(WINDOW // 2)
            scale = base[None, :] ** power[:, None]
            scale = jnp.concatenate([scale, scale], axis=-1)
            cos, sin = (jnp.cos(freqs), jnp.sin(freqs))
            q = q * cos * scale + rotate_half(q) * sin * scale
            k = k * cos / scale + rotate_half(k) * sin / scale
            return (q, k)

        def local_attention(q, k, v):
            b, h, n, d = q.shape
            w = n // WINDOW
            bq = q.reshape(b, h, w, WINDOW, d) * QK_SCALE
            bk = k.reshape(b, h, w, WINDOW, d)
            bv = v.reshape(b, h, w, WINDOW, d)

            def look_around(t):
                p = jnp.pad(t, ((0, 0), (0, 0), (1, 0), (0, 0), (0, 0)))
                return jnp.concatenate([p[:, :, :w], p[:, :, 1:]], axis=3)
            bk, bv = (look_around(bk), look_around(bv))
            bt = jnp.arange(n).reshape(w, WINDOW)
            btp = jnp.pad(bt, ((1, 0), (0, 0)), constant_values=-1)
            btk = jnp.concatenate([btp[:w], btp[1:]], axis=1)
            sim = jnp.einsum('bhwid,bhwjd->bhwij', bq, bk)
            i = bt[:, :, None]
            j = btk[:, None, :]
            mask = (i < j) | (i > j + WINDOW) | (j == -1)
            sim = jnp.where(mask, -jnp.finfo(sim.dtype).max, sim)
            attn = jax.nn.softmax(sim, axis=-1)
            out = jnp.einsum('bhwij,bhwjd->bhwid', attn, bv)
            return out.reshape(b, h, n, d)

        def _layer(x, wqkv, qs, ksc, wo, lg, lb, w1, b1, w2, b2):
            b, n, _ = x.shape
            h = shift_token(x)
            qkv = h @ wqkv
            q, k, v = jnp.split(qkv, 3, axis=-1)
            to_heads = lambda t: t.reshape(b, n, HEADS, DIM_HEAD).transpose(0, 2, 1, 3)
            q, k, v = (to_heads(q), to_heads(k), to_heads(v))
            q = l2norm(q) * qs
            k = l2norm(k) * ksc
            q, k = rotary_xpos(q, k)
            o = local_attention(q, k, v)
            o = o.transpose(0, 2, 1, 3).reshape(b, n, INNER)
            x = x + o @ wo
            h = shift_token(x)
            mu = h.mean(-1, keepdims=True)
            var = h.var(-1, keepdims=True)
            h = (h - mu) / jnp.sqrt(var + 1e-05) * lg + lb
            h = h @ w1 + b1
            a, g = jnp.split(h, 2, axis=-1)
            h = a * jax.nn.gelu(g, approximate=False)
            x = x + h @ w2 + b2
            return x
        key = jax.random.key(seed)
        ks = jax.random.split(key, 6)
        return {'x': jax.random.normal(ks[0], (B, N, DIM), jnp.float32), 'wqkv': jax.random.normal(ks[1], (DEPTH, DIM, 3 * INNER), jnp.float32) * 0.02, 'q_scale': jnp.ones((DEPTH, DIM_HEAD), jnp.float32), 'k_scale': jnp.ones((DEPTH, DIM_HEAD), jnp.float32), 'wo': jax.random.normal(ks[2], (DEPTH, INNER, DIM), jnp.float32) * 0.02, 'ln_g': jnp.ones((DEPTH, DIM), jnp.float32), 'ln_b': jnp.zeros((DEPTH, DIM), jnp.float32), 'w1': jax.random.normal(ks[3], (DEPTH, DIM, 2 * HID), jnp.float32) * 0.02, 'b1': jnp.zeros((DEPTH, 2 * HID), jnp.float32), 'w2': jax.random.normal(ks[4], (DEPTH, HID, DIM), jnp.float32) * 0.02, 'b2': jnp.zeros((DEPTH, DIM), jnp.float32)}
    _L0_ffn_in = _L0_ffn_setup()
    _d = {'L0_attn_q': _L0_attn_in['q'], 'L0_attn_in_proj_weight': _L0_attn_in['in_proj_weight'], 'L0_attn_in_proj_bias': _L0_attn_in['in_proj_bias'], 'L0_attn_out_w': _L0_attn_in['out_w'], 'L0_attn_out_b': _L0_attn_in['out_b'], 'L0_attn_rel_pe': _L0_attn_in['rel_pe'], 'L0_ffn_wqkv': _L0_ffn_in['wqkv'], 'L0_ffn_q_scale': _L0_ffn_in['q_scale'], 'L0_ffn_k_scale': _L0_ffn_in['k_scale'], 'L0_ffn_wo': _L0_ffn_in['wo'], 'L0_ffn_ln_g': _L0_ffn_in['ln_g'], 'L0_ffn_ln_b': _L0_ffn_in['ln_b'], 'L0_ffn_w1': _L0_ffn_in['w1'], 'L0_ffn_b1': _L0_ffn_in['b1'], 'L0_ffn_w2': _L0_ffn_in['w2'], 'L0_ffn_b2': _L0_ffn_in['b2']}
    _x0 = _d['L0_attn_q']
    _d['L0_attn_q'] = jax.random.normal(jax.random.fold_in(jax.random.key(seed), 1), (1, 4096, 256), dtype=_x0.dtype)
    del _x0
    return _d

def reference(L0_attn_q, L0_attn_in_proj_weight, L0_attn_in_proj_bias, L0_attn_out_w, L0_attn_out_b, L0_attn_rel_pe, L0_ffn_wqkv, L0_ffn_q_scale, L0_ffn_k_scale, L0_ffn_wo, L0_ffn_ln_g, L0_ffn_ln_b, L0_ffn_w1, L0_ffn_b1, L0_ffn_w2, L0_ffn_b2):

    def _L0_attn_ref(q, in_proj_weight, in_proj_bias, out_w, out_b, rel_pe):
        import jax, jax.numpy as jnp
        import numpy as np
        import math
        B, L, E, H, K = (4, 256, 256, 16, 64)
        D = E // H

        def _attend(q, in_proj_weight, in_proj_bias, out_w, out_b, rel_pe):
            b, l, e = q.shape
            h, d = (H, D)
            qkv = q @ in_proj_weight.T + in_proj_bias
            qh, kh, vh = jnp.split(qkv, 3, axis=-1)
            qh = qh.reshape(b, l, h, d).transpose(0, 2, 1, 3)
            kh = kh.reshape(b, l, h, d).transpose(0, 2, 1, 3)
            vh = vh.reshape(b, l, h, d).transpose(0, 2, 1, 3)
            qh = qh / math.sqrt(d)
            scores = jnp.einsum('bhid,bhjd->bhij', qh, kh)
            pos = jnp.arange(l)
            rel = jnp.clip(pos[None, :] - pos[:, None], -K, K) + K
            bias_r = jnp.einsum('bhid,rd->bhir', qh, rel_pe)
            bias = jnp.take_along_axis(bias_r, jnp.broadcast_to(rel[None, None], (b, h, l, l)), axis=-1)
            attn = jax.nn.softmax(scores + bias, axis=-1)
            out = jnp.einsum('bhij,bhjd->bhid', attn, vh)
            out = out.transpose(0, 2, 1, 3).reshape(b, l, e)
            return out @ out_w.T + out_b
        return _attend(q, in_proj_weight, in_proj_bias, out_w, out_b, rel_pe)

    def _L0_ffn_ref(x, wqkv, q_scale, k_scale, wo, ln_g, ln_b, w1, b1, w2, b2):
        import jax, jax.numpy as jnp
        import numpy as np
        DIM = 256
        DEPTH = 2
        HEADS = 8
        DIM_HEAD = 64
        WINDOW = 128
        INNER = HEADS * DIM_HEAD
        HID = int(DIM * 4 * 2 / 3)
        B, N = (2, 2048)
        QK_SCALE = 8.0

        def shift_token(t):
            t1, t2 = jnp.split(t, 2, axis=-1)
            t2 = jnp.pad(t2, ((0, 0), (1, 0), (0, 0)))[:, :-1]
            return jnp.concatenate([t1, t2], axis=-1)

        def l2norm(t):
            return t / jnp.clip(jnp.linalg.norm(t, axis=-1, keepdims=True), 1e-12)

        def rotate_half(x):
            x1, x2 = jnp.split(x, 2, axis=-1)
            return jnp.concatenate([-x2, x1], axis=-1)

        def rotary_xpos(q, k):
            n = q.shape[-2]
            half_idx = jnp.arange(0, DIM_HEAD, 2, dtype=jnp.float32)
            inv_freq = 1.0 / 10000.0 ** (half_idx / DIM_HEAD)
            t = jnp.arange(n, dtype=jnp.float32)
            freqs = t[:, None] * inv_freq[None, :]
            freqs = jnp.concatenate([freqs, freqs], axis=-1)
            base = (half_idx + 0.4 * DIM_HEAD) / (1.4 * DIM_HEAD)
            power = (t - n // 2) / float(WINDOW // 2)
            scale = base[None, :] ** power[:, None]
            scale = jnp.concatenate([scale, scale], axis=-1)
            cos, sin = (jnp.cos(freqs), jnp.sin(freqs))
            q = q * cos * scale + rotate_half(q) * sin * scale
            k = k * cos / scale + rotate_half(k) * sin / scale
            return (q, k)

        def local_attention(q, k, v):
            b, h, n, d = q.shape
            w = n // WINDOW
            bq = q.reshape(b, h, w, WINDOW, d) * QK_SCALE
            bk = k.reshape(b, h, w, WINDOW, d)
            bv = v.reshape(b, h, w, WINDOW, d)

            def look_around(t):
                p = jnp.pad(t, ((0, 0), (0, 0), (1, 0), (0, 0), (0, 0)))
                return jnp.concatenate([p[:, :, :w], p[:, :, 1:]], axis=3)
            bk, bv = (look_around(bk), look_around(bv))
            bt = jnp.arange(n).reshape(w, WINDOW)
            btp = jnp.pad(bt, ((1, 0), (0, 0)), constant_values=-1)
            btk = jnp.concatenate([btp[:w], btp[1:]], axis=1)
            sim = jnp.einsum('bhwid,bhwjd->bhwij', bq, bk)
            i = bt[:, :, None]
            j = btk[:, None, :]
            mask = (i < j) | (i > j + WINDOW) | (j == -1)
            sim = jnp.where(mask, -jnp.finfo(sim.dtype).max, sim)
            attn = jax.nn.softmax(sim, axis=-1)
            out = jnp.einsum('bhwij,bhwjd->bhwid', attn, bv)
            return out.reshape(b, h, n, d)

        def _layer(x, wqkv, qs, ksc, wo, lg, lb, w1, b1, w2, b2):
            b, n, _ = x.shape
            h = shift_token(x)
            qkv = h @ wqkv
            q, k, v = jnp.split(qkv, 3, axis=-1)
            to_heads = lambda t: t.reshape(b, n, HEADS, DIM_HEAD).transpose(0, 2, 1, 3)
            q, k, v = (to_heads(q), to_heads(k), to_heads(v))
            q = l2norm(q) * qs
            k = l2norm(k) * ksc
            q, k = rotary_xpos(q, k)
            o = local_attention(q, k, v)
            o = o.transpose(0, 2, 1, 3).reshape(b, n, INNER)
            x = x + o @ wo
            h = shift_token(x)
            mu = h.mean(-1, keepdims=True)
            var = h.var(-1, keepdims=True)
            h = (h - mu) / jnp.sqrt(var + 1e-05) * lg + lb
            h = h @ w1 + b1
            a, g = jnp.split(h, 2, axis=-1)
            h = a * jax.nn.gelu(g, approximate=False)
            x = x + h @ w2 + b2
            return x
        for l in range(DEPTH):
            x = _layer(x, wqkv[l], q_scale[l], k_scale[l], wo[l], ln_g[l], ln_b[l], w1[l], b1[l], w2[l], b2[l])
        return x
    x = L0_attn_q
    x = _layernorm(x + _L0_attn_ref(x, L0_attn_in_proj_weight, L0_attn_in_proj_bias, L0_attn_out_w, L0_attn_out_b, L0_attn_rel_pe), axis=-1)
    x = _layernorm(x + _L0_ffn_ref(x, L0_ffn_wqkv, L0_ffn_q_scale, L0_ffn_k_scale, L0_ffn_wo, L0_ffn_ln_g, L0_ffn_ln_b, L0_ffn_w1, L0_ffn_b1, L0_ffn_w2, L0_ffn_b2), axis=-1)
    return x

_drawn_inputs = setup_inputs


def setup_inputs(seed=0):
    import zlib

    import numpy as np

    out = dict(_drawn_inputs(seed))
    spreads = {'L0_attn_in_proj_bias': (0.0, 0.1),
     'L0_attn_out_b': (0.0, 0.1),
     'L0_ffn_q_scale': (1.0, 0.6),
     'L0_ffn_k_scale': (1.0, 0.6),
     'L0_ffn_ln_g': (1.0, 0.6),
     'L0_ffn_ln_b': (0.0, 0.8),
     'L0_ffn_b1': (0.0, 0.8),
     'L0_ffn_b2': (0.0, 0.1)}
    factors = {'L0_attn_rel_pe': 3.681, 'L0_ffn_wqkv': 2.685, 'L0_ffn_wo': 2.7}
    for name, (base, spread) in spreads.items():
        noise = np.random.default_rng([zlib.crc32(name.encode()), seed]).standard_normal(out[name].shape)
        drawn = base * np.exp(spread * noise) if base else spread * noise
        out[name] = jnp.asarray(drawn.astype(out[name].dtype))
    for name, factor in factors.items():
        out[name] = (out[name] * factor).astype(out[name].dtype)
    return out
```

```python
from contextlib import ExitStack

import concourse.bass as bass
from concourse import mybir

F32 = mybir.dt.float32
BF16 = mybir.dt.bfloat16
ACT = mybir.ActivationFunctionType
ALU = mybir.AluOpType
AX = mybir.AxisListType

P = 128
N = 4096
E = 256
KE = E // P
TILES = N // P
LN_EPS = 1e-5

HEADS = 16
D = E // HEADS
CLIP = 64
GROUP = P // D
CH = 512
CHUNKS = N // CH
TPC = CH // P
Q_PARTS = (0, 0, 0, 1, 1, 2)
K_RUNS = (3, 2, 1)
TERMS = len(Q_PARTS)
ROWS = TERMS * D
MROWS = 2
VW = D + 1
WIN_TILES = TILES + TPC - 1
SLAB = 2 * P
PAD = CLIP
PAIRS = TILES // 2
QUADS = TILES // 4
BLOCK_U = SLAB // CHUNKS
BLOCK_W = BLOCK_U - 1 + P
UG = BLOCK_U // 2


def project_heads(nc, x_T, w_in_T, b_in, pe_edges, q_stack, k_parts, v_wide):
    with ExitStack() as ctx:
        sb = lambda name, shape, dt=F32: ctx.enter_context(nc.sbuf_tensor(name, shape, dt))
        sem = lambda name: ctx.enter_context(nc.semaphore(name))
        weights = sb("in_weights", [P, KE, 3 * E])
        v_bias = sb("v_bias", [1, E])
        ones_row = sb("ones_row", [1, P])
        qk_bias = sb("qk_bias", [P, 4])
        edges = sb("edges", [P, 2])
        bias = sb("unit_bias", [P, 6])
        x_in = sb("x_in", [P, 2, KE, CH])
        exact = sb("exact", [P, 6, CH])
        rest = sb("rest", [P, 2, CH])
        part = sb("part", [P, 3, 6, CH], BF16)
        v_stage = sb("v_stage", [P, HEADS, TPC, VW])
        unit_ps = [ctx.enter_context(nc.psum_tensor(f"unit_ps{u}", [P, CH], F32)) for u in range(4)]
        value_ps = [ctx.enter_context(nc.psum_tensor(f"value_ps{u}", [P, 2, E], F32)) for u in range(2)]

        consts_in = sem("consts_in")
        x_loaded = [sem(f"x_loaded{i}") for i in range(2)]
        ones_set = sem("ones_set")
        bias_made = sem("bias_made")
        units_done = sem("units_done")
        values_done = sem("values_done")
        exact_done = sem("exact_done")
        hi_done = sem("hi_done")
        rest_done = sem("rest_done")
        mid_done = sem("mid_done")
        low_done = sem("low_done")
        v_staged = sem("v_staged")
        v_stored = sem("v_stored")
        parts_stored = [sem(f"parts_stored{v}") for v in range(6)]
        VARIANTS = ((0, 0), (1, 1), (2, 2), (2, 3), (3, 4), (3, 5))
        UNIT_READ = (1, 2, 4, 6)
        Q_STORES, K_STORES = TERMS, 3

        block = ctx.enter_context(nc.Block())

        @block.gpsimd
        def _(pool):
            with pool.Fori(0, CHUNKS // 2) as m:
                for par in range(2):
                    n = m * 2 + par
                    pool.wait_ge(values_done, m * 2 if par == 0 else m * 2)
                    pool.dma_start(x_in[:, par, :, :],
                                   x_T.rearrange("(k p) n -> p k n", p=P)[:, :, bass.ds(n * CH, CH)]
                                   ).then_inc(x_loaded[par], 16)

        @block.sync
        def _(sp):
            sp.dma_start(weights[:], w_in_T.rearrange("(k p) n -> p k n", p=P)).then_inc(consts_in, 16)
            sp.dma_start(qk_bias[:], b_in[0:2 * E].rearrange("(u p) -> p u", p=P),
                         allow_slow_non_contiguous=True).then_inc(consts_in, 16)
            sp.dma_start(edges[:], pe_edges.rearrange("e p -> p e"),
                         allow_slow_non_contiguous=True).then_inc(consts_in, 16)
            sp.dma_start(v_bias[:], b_in[2 * E:3 * E].rearrange("(a n) -> a n", a=1)).then_inc(consts_in, 16)
            with sp.Fori(0, CHUNKS) as n:
                col = n * CH
                for v, (unit, _) in enumerate(VARIANTS):
                    sp.wait_ge(low_done, n * 6 + v + 1)
                    heads = slice(GROUP * (unit % 2), GROUP * (unit % 2 + 1))
                    if unit < 2:
                        for t, which in enumerate(Q_PARTS):
                            sp.dma_start(q_stack[heads, t * D:(t + 1) * D, bass.ds(col, CH)],
                                         part[:, which, v, :]).then_inc(parts_stored[v], 16)
                    else:
                        side = col if v in (2, 4) else col + N
                        for which in range(3):
                            sp.dma_start(k_parts[heads, which * D:(which + 1) * D, bass.ds(side, CH)],
                                         part[:, which, v, :]).then_inc(parts_stored[v], 16)
                sp.wait_ge(v_staged, n + 2)
                for again in range(2):
                    sp.dma_start(v_wide.rearrange("h p (t e) -> p h t e", e=VW)
                                 [:, :, bass.ds(n * TPC + again * TILES, TPC), :],
                                 v_stage[:]).then_inc(v_stored, 16)
            for v in range(6):
                sp.wait_ge(parts_stored[v], 16 * CHUNKS * (Q_STORES if v < 2 else K_STORES))
            sp.wait_ge(v_stored, 32 * CHUNKS)

        @block.tensor
        def _(pe):
            pe.wait_ge(consts_in, 64)
            pe.wait_ge(ones_set, 2)
            with pe.Fori(0, CHUNKS // 2) as m:
                for par in range(2):
                    n = m * 2 + par
                    pe.wait_ge(x_loaded[par], m * 16 + 16)
                    for u in range(4):
                        pe.wait_ge(exact_done, n * 6 + UNIT_READ[u])
                        for k in range(KE):
                            mm = pe.matmul(unit_ps[u][:], weights[:, k, u * P:(u + 1) * P],
                                           x_in[:, par, k, :], start=k == 0, stop=k == KE - 1)
                        mm.then_inc(units_done, 1)
                    pe.wait_ge(v_staged, n + 1)
                    for t in range(TPC):
                        out = value_ps[t // 2][:, t % 2, :]
                        for k in range(KE):
                            pe.matmul(out, x_in[:, par, k, t * P:(t + 1) * P],
                                      weights[:, k, 2 * E:3 * E], start=k == 0, stop=False)
                        mm = pe.matmul(out, ones_row[:], v_bias[:], start=False, stop=True)
                    mm.then_inc(values_done, 1)

        @block.scalar
        def _(act):
            act.preload_act_table(ACT.Identity)
            act.sem_inc(exact_done, 6)
            act.sem_inc(v_staged, 1)
            act.wait_ge(bias_made, 1)
            act.wait_ge(ones_set, 2)
            with act.Fori(0, CHUNKS) as n:
                for v, (unit, b) in enumerate(VARIANTS):
                    act.wait_ge(units_done, n * 4 + unit + 1)
                    act.wait_ge(rest_done, n * 6 + v + 1)
                    act.activation(exact[:, v, :], unit_ps[unit][:], ACT.Identity,
                                   bias=bias[:, b:b + 1], scale=D ** -0.5 if unit < 2 else 1.0
                                   ).then_inc(exact_done, 1)
                    act.wait_ge(exact_done, n * 6 + v + 7)
                    act.wait_ge(parts_stored[v], n * (16 * (Q_STORES if v < 2 else K_STORES)))
                    act.activation(part[:, 0, v, :], exact[:, v, :], ACT.Identity).then_inc(hi_done, 1)
                act.wait_ge(values_done, n + 1)
                act.wait_ge(v_stored, n * 32)
                for half in range(2):
                    ins = act.activation(v_stage[:, :, 2 * half:2 * half + 2, 0:D],
                                         value_ps[half][:].rearrange("p t (h d) -> p h t d", d=D),
                                         ACT.Identity)
                ins.then_inc(v_staged, 1)

        @block.vector
        def _(dve):
            dve.memset(ones_row[:], 1.0).then_inc(ones_set, 1)
            dve.memset(v_stage[:], 1.0).then_inc(ones_set, 1)
            dve.sem_inc(rest_done, 6)
            dve.wait_ge(consts_in, 64)
            dve.tensor_scalar(bias[:, 0:2], qk_bias[:, 0:2], D ** -0.5, None, ALU.mult)
            for unit in range(2):
                for side in range(2):
                    ins = dve.tensor_tensor(bias[:, 2 + 2 * unit + side:3 + 2 * unit + side],
                                            qk_bias[:, 2 + unit:3 + unit], edges[:, 1 - side:2 - side],
                                            ALU.add)
            ins.then_inc(bias_made, 1)
            with dve.Fori(0, CHUNKS) as n:
                for v in range(6):
                    dve.wait_ge(hi_done, n * 6 + v + 1)
                    dve.tensor_tensor(rest[:, v % 2, :], exact[:, v, :], part[:, 0, v, :], ALU.subtract
                                      ).then_inc(rest_done, 1)
                    dve.wait_ge(rest_done, n * 6 + v + 7)
                    dve.tensor_copy(part[:, 1, v, :], rest[:, v % 2, :]).then_inc(mid_done, 1)
                    dve.wait_ge(mid_done, n * 6 + v + 1)
                    dve.tensor_tensor(part[:, 2, v, :], rest[:, v % 2, :], part[:, 1, v, :], ALU.subtract
                                      ).then_inc(low_done, 1)

def attend(nc, q_stack, k_parts, v_wide, rel_T, ident, part_sum, attn):
    NEXT_GEN = CHUNKS + 1
    TOTAL = HEADS * CHUNKS
    MAX_GROUPS = TPC * (TILES // TPC)
    with ExitStack() as ctx:
        sb = lambda name, shape, dt=F32: ctx.enter_context(nc.sbuf_tensor(name, shape, dt))
        ps = lambda name, shape, dt=F32: ctx.enter_context(nc.psum_tensor(name, shape, dt))
        sem = lambda name: ctx.enter_context(nc.semaphore(name))
        keys = [sb(f"keys{i}", [ROWS + MROWS, WIN_TILES * P], BF16) for i in range(2)]
        queries = [sb(f"queries{i}", [ROWS + MROWS, CH], BF16) for i in range(2)]
        values = [sb(f"values{i}", [P, TILES, VW]) for i in range(2)]
        head_q = sb("head_q", [ROWS, PAD + N + PAD], BF16)
        near_bias = sb("near_bias", [P, 2, TILES + 2, SLAB])
        near_window = [sb(f"near_window{i}", [P, TPC + 2, SLAB + 2 * PAD], BF16) for i in range(2)]
        probs = [sb(f"probs{i}", [P, 2, CH]) for i in range(4)]
        table = sb("table", [ROWS, CHUNKS, BLOCK_W], BF16)
        table_raw = sb("table_raw", [D, 2 * CLIP + 1])
        R_COLS = 3 * P - 1 - PAD
        L_COLS = 3 * P - 1 - 3 * PAD
        ext = sb("table_ext", [D, R_COLS + L_COLS])
        ext_rest = sb("table_rest", [D, R_COLS + L_COLS])
        ext_part = sb("table_part", [D, 3, R_COLS + L_COLS], BF16)
        ext_rows = sb("table_rows", [ROWS, R_COLS + L_COLS], BF16)
        ident_f = sb("ident_f", [P, P])
        ident_b = sb("ident_b", [P, P], BF16)
        sum_sel = sb("sum_sel", [P, VW])
        group_max = sb("group_max", [P, MAX_GROUPS])
        row_max = sb("row_max", [P, TPC])
        max_parts = sb("max_parts", [P, TPC, MROWS], BF16)
        out_copy = sb("out_copy", [P, CH])
        inv_sum = sb("inv_sum", [P, TPC, 1])

        scores = [ps(f"scores{i}", [P, 2, CH]) for i in range(2)]
        out_ps = ps("out_ps", [P, CH])
        max_ps = [ps(f"max_ps{i}", [P, CH]) for i in range(2)]
        small_ps = ps("small_ps", [P, CH])

        consts_in = sem("consts_in2")
        table_cut = sem("table_cut")
        table_rows_in = sem("table_rows_in")
        table_ready = sem("table_ready")
        cleared = sem("cleared")
        ident_ready = sem("ident_ready")
        PIECES = ((0, 8, 3), (8, 16, 7), (16, 24, 11), (24, WIN_TILES, 15))
        keys_in = [[sem(f"keys_in{i}_{j}") for j in range(4)] for i in range(2)]
        queries_in = [sem(f"queries_in{i}") for i in range(2)]
        values_in = [sem(f"values_in{i}") for i in range(2)]
        head_q_in = sem("head_q_in")
        bias_ready = sem("bias_ready")
        bias_read = sem("bias_read")
        window_ready = sem("window_ready")
        max_ready = sem("max_ready")
        max_read = sem("max_read")
        max_step = sem("max_step")
        max_cut = sem("max_cut")
        max_rows = sem("max_rows")
        max_placed = sem("max_placed")
        scores_ready = sem("scores_ready")
        near_added = sem("near_added")
        exp_done = sem("exp_done")
        pv_done = sem("pv_done")
        out_copied = sem("out_copied")
        out_summed = sem("out_summed")
        norm_step = sem("norm_step")
        normed = sem("normed")

        block = ctx.enter_context(nc.Block())

        def place(n):
            return n // CHUNKS, n % CHUNKS

        @block.sync
        def _(sp):
            sp.dma_start(table_raw[:], rel_T).then_inc(consts_in, 16)
            sp.dma_start(ident_f[:], ident).then_inc(consts_in, 16)
            sp.dma_start(sum_sel[:], part_sum).then_inc(consts_in, 16)

            def load_keys(n, par, j):
                h, c = place(n)
                a, b, _ = PIECES[j]
                row = 0
                for run in K_RUNS:
                    rows = run * D
                    sp.dma_start(keys[par][row:row + rows, a * P:b * P],
                                 k_parts[bass.ds(h, 1), 0:rows, bass.ds(c * CH + a * P, (b - a) * P)]
                                 ).then_inc(keys_in[par][j], 16)
                    row += rows

            def load_queries(n, par):
                h, c = place(n)
                sp.dma_start(queries[par][0:ROWS, :], q_stack[bass.ds(h, 1), :, bass.ds(c * CH, CH)]
                             ).then_inc(queries_in[par], 16)

            def load_values(n, par):
                h, c = place(n)
                sp.dma_start(values[par][:], v_wide[bass.ds(h, 1), :, bass.ds(c * (TPC * VW), TILES * VW)]
                             ).then_inc(values_in[par], 16)

            for par in range(2):
                load_queries(par, par)
                for j in range(4):
                    load_keys(par, par, j)
                load_values(par, par)
            for i in range(3):
                pass
            sp.wait_ge(table_cut, 3)
            row = 0
            for run in K_RUNS:
                for which in range(run):
                    sp.dma_start(ext_rows[row:row + D, :], ext_part[:, which, :]
                                 ).then_inc(table_rows_in, 16)
                    row += D
            with sp.Fori(0, TOTAL // 2 - 1) as m:
                for par in range(2):
                    n = m * 2 + par
                    for j in range(4):
                        sp.wait_ge(scores_ready, n * PAIRS + PIECES[j][2] + 1)
                        load_keys(n + 2, par, j)
                    load_queries(n + 2, par)
                    sp.wait_ge(pv_done, n * QUADS + QUADS + 2)
                    load_values(n + 2, par)

        @block.gpsimd
        def _(pool):
            for i in range(2):
                pool.memset(near_window[i][:], 0.0).then_inc(cleared, 1)
                pool.memset(near_bias[:, i, 0, :], 0.0).then_inc(cleared, 1)
                pool.memset(near_bias[:, i, TILES + 1, :], 0.0).then_inc(cleared, 1)
            pool.memset(head_q[:, 0:PAD], 0.0).then_inc(cleared, 1)
            pool.memset(head_q[:, PAD + N:], 0.0).then_inc(cleared, 1)
            pool.wait_ge(cleared, 8)

            def load_head_q(h):
                pool.dma_start(head_q[:, PAD:PAD + N], q_stack[bass.ds(h, 1), :, :]).then_inc(head_q_in, 16)

            def copy_window(h, c):
                n = h * CHUNKS + c
                pool.wait_ge(max_cut, n + 1)
                ins = pool.tensor_copy(near_window[c % 2][:, :, PAD:PAD + SLAB],
                                       near_bias[:, bass.ds(h % 2, 1), TPC * c:TPC * c + TPC + 2, :])
                ins.then_inc(window_ready, 1)

            load_head_q(0)
            pool.wait_ge(bias_ready, 2 * CHUNKS)
            load_head_q(1)
            with pool.Fori(0, HEADS - 2) as h:
                pool.wait_ge(bias_read, (h + 1) * (2 * CHUNKS))
                for c in range(CHUNKS):
                    copy_window(h, c)
                pool.wait_ge(bias_ready, (h + 2) * (2 * CHUNKS))
                load_head_q(h + 2)
            with pool.Fori(HEADS - 2, HEADS) as h:
                pool.wait_ge(bias_read, (h + 1) * (2 * CHUNKS))
                for c in range(CHUNKS):
                    copy_window(h, c)

        @block.tensor
        def _(pe):
            def max_group(n, par, k):
                t, g = k % TPC, k // TPC
                if k == 0:
                    pe.wait_ge(window_ready, n + 1)
                    pe.wait_ge(queries_in[par], (n // 2) * 16 + 16)
                if t == 0:
                    last_tile = TPC * g + 2 * TPC - 2
                    for j, (a, b, _) in enumerate(PIECES):
                        if a <= last_tile < b or (g == 0 and j == 0):
                            pe.wait_ge(keys_in[par][j], (n // 2) * 48 + 48)
                pe.wait_ge(max_read, n * MAX_GROUPS + k + 1)
                bank = max_ps[k % 2]
                near = {0: [(0, t + 1, P), (1, t + 2, 0)],
                        TILES // TPC - 1: [(TPC - 1, t, 2 * P)]}.get(g, [])
                mm = pe.matmul(bank[:], queries[par][0:ROWS, t * P:(t + 1) * P],
                               keys[par][0:ROWS, (t + TPC * g) * P:(t + TPC * (g + 1)) * P],
                               start=True, stop=not near)
                for i, (pos, slab, u) in enumerate(near):
                    mm = pe.matmul(bank[:, pos * P:(pos + 1) * P], near_window[par][:, slab, u:u + P],
                                   ident_b[:], start=False, stop=i == len(near) - 1)
                mm.then_inc(max_ready, 1)

            def max_to_rows(n, par):
                pe.wait_ge(max_cut, n + 3)
                for t in range(TPC):
                    mm = pe.matmul(small_ps[ROWS:ROWS + MROWS, t * P:(t + 1) * P], max_parts[:, t, :],
                                   ident_b[:], start=True, stop=True)
                mm.then_inc(max_rows, 1)

            def score_pair(n, par, s):
                if s == 0:
                    pe.wait_ge(max_placed, n + 1)
                pe.wait_ge(exp_done, n * PAIRS + s + 1)
                for i in range(2):
                    c = 2 * s + i
                    cut = min(c + 1, TPC) * P
                    out = scores[s % 2][:, i, :]
                    mm = pe.matmul(out[:, 0:cut], keys[par][:, c * P:(c + 1) * P],
                                   queries[par][:, 0:cut], start=True, stop=True)
                    if cut < CH:
                        mm = pe.matmul(out[:, cut:CH], keys[par][:, (c + TILES) * P:(c + TILES + 1) * P],
                                       queries[par][:, cut:CH], start=True, stop=True)
                mm.then_inc(scores_ready, 1)

            def pv_quad(n, par, q):
                if q == 0:
                    pe.wait_ge(values_in[par], (n // 2) * 16 + 16)
                    pe.wait_ge(out_copied, n)
                pe.wait_ge(exp_done, n * PAIRS + 2 * q + 4)
                for i in range(4):
                    mm = pe.matmul(out_ps[32 * i:32 * i + VW, :], values[par][:, 4 * q + i, :],
                                   probs[(2 * q + i // 2) % 4][:, i % 2, :],
                                   start=q == 0, stop=q == QUADS - 1, skip_group_check=True)
                mm.then_inc(pv_done, 1)

            def make_bias(block_no, half):
                h, b = place(block_no)
                for i in range(UG):
                    u = half * UG + i
                    mm = pe.matmul(small_ps[:, i * TILES:(i + 1) * TILES],
                                   table[:, bass.ds(b, 1), BLOCK_U - 1 - u:BLOCK_U - 1 - u + P],
                                   head_q[:, bass.ds(b * BLOCK_U + u, TILES, P)],
                                   start=True, stop=True)
                mm.then_inc(bias_ready, 1)

            def sum_quadrants(n, par):
                pe.wait_ge(out_copied, n + 1)
                for t in range(TPC):
                    mm = pe.matmul(small_ps[:, t * VW:(t + 1) * VW], out_copy[:, t * P:(t + 1) * P],
                                   sum_sel[:], start=True, stop=True)
                mm.then_inc(out_summed, 1)

            def chunk(n, par, bias, more):
                groups = iter(range(MAX_GROUPS))
                for s in range(2, PAIRS):
                    score_pair(n, par, s)
                    if more and s < 14:
                        for _ in range(3 if s < 10 else 2):
                            max_group(n + 1, 1 - par, next(groups))
                    if bias and s in (4, 8):
                        g = (n + NEXT_GEN) * 2 + s // 8
                        if s == 4:
                            pe.wait_ge(normed, n)
                            pe.wait_ge(head_q_in, ((n + NEXT_GEN) // CHUNKS) * 16 + 16)
                        pe.wait_ge(bias_read, g)
                        make_bias(n + NEXT_GEN, s // 8)
                    if s % 2 == 1:
                        pv_quad(n, par, (s - 3) // 2)
                if more:
                    if bias:
                        pe.wait_ge(bias_read, (n + NEXT_GEN) * 2 + 2)
                    else:
                        pe.wait_ge(normed, n)
                    max_to_rows(n + 1, 1 - par)
                    for s in range(2):
                        score_pair(n + 1, 1 - par, s)
                pv_quad(n, par, QUADS - 1)
                if more:
                    pe.wait_ge(max_placed, n + 2)
                sum_quadrants(n, par)

            pe.wait_ge(consts_in, 48)
            pe.wait_ge(table_ready, 1)
            pe.wait_ge(cleared, 8)
            pe.wait_ge(ident_ready, 4)
            for e in range(NEXT_GEN):
                if e % CHUNKS == 0:
                    pe.wait_ge(head_q_in, (e // CHUNKS) * 16 + 16)
                for half in range(2):
                    pe.wait_ge(bias_read, 2 * e + half)
                    make_bias(e, half)
            for k in range(MAX_GROUPS):
                max_group(0, 0, k)
            pe.wait_ge(bias_read, 2 * NEXT_GEN)
            max_to_rows(0, 0)
            for s in range(2):
                score_pair(0, 0, s)
            last_bias = (TOTAL - NEXT_GEN) // 2
            with pe.Fori(0, last_bias) as m:
                for par in range(2):
                    chunk(m * 2 + par, par, True, True)
            chunk(2 * last_bias, 0, True, True)
            chunk(2 * last_bias + 1, 1, False, True)
            with pe.Fori(last_bias + 1, TOTAL // 2 - 1) as m:
                for par in range(2):
                    chunk(m * 2 + par, par, False, True)
            chunk(TOTAL - 2, 0, False, True)
            chunk(TOTAL - 1, 1, False, False)

        @block.scalar
        def _(act):
            act.preload_act_table(ACT.Exp)
            act.sem_inc(exp_done, 2)

            def keep_bias(block_no, half):
                h, b = place(block_no)
                act.wait_ge(bias_ready, block_no * 2 + half + 1)
                act.activation(near_bias[:, bass.ds(h % 2, 1), 1:TILES + 1, bass.ds(b * BLOCK_U + half * UG, UG)],
                               small_ps[:].rearrange("p (a u j) -> p a j u", a=1, u=UG), ACT.Copy
                               ).then_inc(bias_read, 1)

            def chunk(n, bias):
                for s in range(PAIRS):
                    if s in (0, 1, 2, 15):
                        act.wait_ge(near_added, n * 4 + {0: 1, 1: 2, 2: 3, 15: 4}[s])
                    act.wait_ge(scores_ready, n * PAIRS + s + 1)
                    act.wait_ge(pv_done, n * QUADS + s // 2 + 1)
                    act.activation(probs[s % 4][:], scores[s % 2][:], ACT.Exp).then_inc(exp_done, 1)
                    if bias and s in (4, 8):
                        if s == 4:
                            act.wait_ge(window_ready, n + 1)
                        keep_bias(n + NEXT_GEN, s // 8)

            act.wait_ge(cleared, 8)
            for e in range(NEXT_GEN):
                for half in range(2):
                    keep_bias(e, half)
            last_bias = TOTAL - NEXT_GEN
            with act.Fori(0, last_bias) as n:
                chunk(n, True)
            with act.Fori(last_bias, TOTAL) as n:
                chunk(n, False)

        @block.vector
        def _(dve):
            dve.sem_inc(max_read, 2)
            dve.sem_inc(max_cut, 2)
            dve.sem_inc(pv_done, 2)
            dve.memset(out_ps[:], 0.0).then_inc(ident_ready, 1)
            for i in range(2):
                dve.memset(keys[i][ROWS:ROWS + MROWS, :], 1.0).then_inc(ident_ready, 1)
            dve.wait_ge(consts_in, 48)
            dve.tensor_copy(ident_b[:], ident_f[:]).then_inc(ident_ready, 1)
            spans = ((0, PAD, 0, None), (PAD, 2 * CLIP - 1, 1, None), (PAD + 2 * CLIP - 1, P, 2 * CLIP, None),
                     (R_COLS, P, 0, None), (R_COLS + P, CLIP - 1, 1, None))
            for start, width, first, _ in spans:
                if first in (0, 2 * CLIP):
                    src = table_raw[:, first:first + 1].to_broadcast([D, width])
                else:
                    src = table_raw[:, first:first + width]
                ins = dve.tensor_copy(ext[:, start:start + width], src)
            ins.then_inc(max_step, 1)
            dve.wait_ge(max_step, 1)
            dve.tensor_scalar(ext[:, 0:R_COLS], ext[:, 0:R_COLS], table_raw[:, 2 * CLIP:2 * CLIP + 1], None,
                              ALU.subtract)
            dve.tensor_scalar(ext[:, R_COLS:], ext[:, R_COLS:], table_raw[:, 0:1], None,
                              ALU.subtract).then_inc(max_step, 1)
            dve.wait_ge(max_step, 2)
            dve.tensor_copy(ext_part[:, 0, :], ext[:]).then_inc(table_cut, 1)
            dve.wait_ge(table_cut, 1)
            dve.tensor_tensor(ext_rest[:], ext[:], ext_part[:, 0, :], ALU.subtract).then_inc(max_step, 1)
            dve.wait_ge(max_step, 3)
            dve.tensor_copy(ext_part[:, 1, :], ext_rest[:]).then_inc(table_cut, 1)
            dve.wait_ge(table_cut, 2)
            dve.tensor_tensor(ext_part[:, 2, :], ext_rest[:], ext_part[:, 1, :], ALU.subtract
                              ).then_inc(table_cut, 1)
            dve.wait_ge(table_rows_in, 16 * TERMS)
            for b in range(CHUNKS):
                if (b + 1) * BLOCK_U <= PAD + P:
                    first = P - 1 + PAD - b * BLOCK_U - (BLOCK_U - 1)
                else:
                    first = R_COLS + SLAB - 1 - b * BLOCK_U - (BLOCK_U - 1)
                ins = dve.tensor_copy(table[:, b, :], ext_rows[:, first:first + BLOCK_W])
            ins.then_inc(table_ready, 1)
            SETUP = 3

            def near_add(n, s):
                h, c = place(n)
                spans = {0: [(0, 0, 192, 1, 64), (1, 0, 320, 2, 0)],
                         1: [(0, 192, 448, 3, 0), (1, 320, 512, 4, 0)],
                         2: [(0, 448, 512, 5, 0)],
                         15: [(1, 0, 64, 0, 192)]}[s]
                if s == 0:
                    spans = [(0, 0, 192, 1, 64), (1, 64, 320, 2, 0)]
                dve.wait_ge(scores_ready, n * PAIRS + s + 1)
                for tile, a, b, slab, u in spans:
                    part = scores[s % 2][:, tile, a:b]
                    ins = dve.tensor_tensor(part, part,
                                            near_bias[:, bass.ds(h % 2, 1), bass.ds(c * TPC + slab, 1), u:u + b - a],
                                            ALU.add)
                ins.then_inc(near_added, 1)

            def cut_max(n):
                step = SETUP + n
                dve.wait_ge(max_read, n * MAX_GROUPS + MAX_GROUPS + 2)
                dve.tensor_reduce(row_max[:], group_max[:].rearrange("p (g t) -> p t g", t=TPC), AX.X,
                                  ALU.max).then_inc(max_step, 1)
                dve.wait_ge(max_step, n * 2 + SETUP + 1)
                dve.tensor_scalar(max_parts[:, :, 0], row_max[:], -1.0, None, ALU.mult).then_inc(max_step, 1)
                dve.wait_ge(max_step, n * 2 + SETUP + 2)
                dve.scalar_tensor_tensor(out=max_parts[:, :, 1], in0=row_max[:], scalar=-1.0,
                                         in1=max_parts[:, :, 0], op0=ALU.mult, op1=ALU.subtract
                                         ).then_inc(max_cut, 1)

            def max_pass(n):
                for k in range(MAX_GROUPS):
                    dve.wait_ge(max_ready, n * MAX_GROUPS + k + 1)
                    dve.tensor_reduce(group_max[:, k:k + 1], max_ps[k % 2][:], AX.X, ALU.max
                                      ).then_inc(max_read, 1)
                cut_max(n)

            def place_max(n, par):
                dve.wait_ge(max_rows, n + 1)
                dve.tensor_copy(queries[par][ROWS:ROWS + MROWS, :], small_ps[ROWS:ROWS + MROWS, :]
                                ).then_inc(max_placed, 1)

            def finish(n):
                h, c = place(n)
                dve.wait_ge(pv_done, n * QUADS + QUADS + 2)
                dve.tensor_copy(out_copy[:], out_ps[:]).then_inc(out_copied, 1)
                dve.wait_ge(out_summed, n + 1)
                summed = small_ps[:, 0:TPC * VW].rearrange("p (t e) -> p t e", e=VW)
                dve.reciprocal(inv_sum[:], summed[:, :, D:VW]).then_inc(norm_step, 1)
                dve.wait_ge(norm_step, n + 1)
                dve.tensor_tensor(attn[:, bass.ds(c * TPC, TPC), bass.ds(h * D, D)], summed[:, :, 0:D],
                                  inv_sum[:].to_broadcast([P, TPC, D]), ALU.mult).then_inc(normed, 1)

            def chunk(n, par, more):
                near_add(n, 2)
                if more:
                    max_pass(n + 1)
                near_add(n, 15)
                if more:
                    place_max(n + 1, 1 - par)
                    near_add(n + 1, 0)
                    near_add(n + 1, 1)
                finish(n)

            max_pass(0)
            place_max(0, 0)
            near_add(0, 0)
            near_add(0, 1)
            with dve.Fori(0, TOTAL // 2 - 1) as m:
                for par in range(2):
                    chunk(m * 2 + par, par, True)
            chunk(TOTAL - 2, 0, True)
            chunk(TOTAL - 1, 1, False)


def layernorm_params(dve, pool, stats, mean, rstd, scratch, expo, step, first):
    tiles = stats.shape[1]
    if dve is not None:
        a, b = stats[:, :, 1], stats[:, :, 4]
        dve.tensor_tensor(mean, a, b, ALU.add).then_inc(step, 1)
        dve.tensor_tensor(scratch, a, b, ALU.subtract).then_inc(step, 1)
        dve.wait_ge(step, first + 2)
        dve.tensor_scalar(mean, mean, 0.5, None, ALU.mult).then_inc(step, 1)
        dve.tensor_tensor(scratch, scratch, scratch, ALU.mult).then_inc(step, 1)
        dve.tensor_tensor(rstd, stats[:, :, 2], stats[:, :, 5], ALU.add).then_inc(step, 1)
        dve.wait_ge(step, first + 5)
        dve.tensor_scalar(scratch, scratch, 0.25, LN_EPS, ALU.mult, ALU.add).then_inc(step, 1)
        dve.wait_ge(step, first + 6)
        dve.scalar_tensor_tensor(out=rstd, in0=rstd, scalar=1.0 / E, in1=scratch, op0=ALU.mult,
                                 op1=ALU.add).then_inc(step, 1)
    if pool is not None:
        pool.wait_ge(step, first + 7)
        pool.tensor_tensor(rstd, rstd, expo[:, 0:tiles], ALU.pow).then_inc(step, 1)
    return first + 8


def join_heads(nc, x, w_out_T, b_out, ident, attn, tokens, first_norm):
    with ExitStack() as ctx:
        sb = lambda name, shape, dt=F32: ctx.enter_context(nc.sbuf_tensor(name, shape, dt))
        sem = lambda name: ctx.enter_context(nc.semaphore(name))
        weights = sb("out_weights", [P, KE, E])
        bias = sb("out_bias", [1, E])
        ones_row = sb("join_ones", [1, P])
        ident_f = sb("join_ident", [P, P])
        tile_in = sb("join_tile", [P, 2, E])
        tile_T = sb("join_tile_T", [P, 2, E])
        stats = sb("join_stats", [P, TILES, 6])
        mean, rstd, scratch, expo = (sb(f"join_{n}", [P, TILES]) for n in ("mean", "rstd", "scratch", "expo"))
        turned = [ctx.enter_context(nc.psum_tensor(f"join_turned{i}", [P, CH], F32)) for i in range(2)]
        joined = [ctx.enter_context(nc.psum_tensor(f"join_joined{i}", [P, CH], F32)) for i in range(2)]
        consts_in = sem("join_consts")
        ones_set = sem("join_ones_set")
        x_in = sem("join_x_in")
        picked = sem("picked")
        tile_turned = sem("tile_turned")
        tile_kept = sem("tile_kept")
        tile_joined = sem("tile_joined")
        summed = sem("summed")
        counted = sem("counted")
        step = sem("join_step")
        normed = sem("join_normed")
        copied = sem("join_copied")
        block = ctx.enter_context(nc.Block())

        @block.sync
        def _(sp):
            sp.dma_start(weights[:], w_out_T.rearrange("(k p) n -> p k n", p=P)).then_inc(consts_in, 16)
            sp.dma_start(bias[:], b_out.rearrange("(a n) -> a n", a=1)).then_inc(consts_in, 16)
            sp.dma_start(ident_f[:], ident).then_inc(consts_in, 16)
            sp.dma_start(tokens[:], x.rearrange("(t p) e -> p t e", p=P)).then_inc(x_in, 16)
            sp.wait_ge(normed, TILES)
            sp.dma_start(first_norm, tokens[:]).then_inc(copied, 16)
            sp.wait_ge(copied, 16)

        @block.gpsimd
        def _(pool):
            pool.memset(expo[:], -0.5).then_inc(ones_set, 1)
            pool.sem_inc(tile_turned, 2)
            with pool.Fori(0, TILES // 2) as m:
                for par in range(2):
                    t = m * 2 + par
                    pool.wait_ge(tile_turned, t + 1)
                    pool.tensor_copy(tile_in[:, par, :], attn[:, bass.ds(t, 1), :]).then_inc(picked, 1)
            pool.wait_ge(ones_set, 2)
            layernorm_params(None, pool, stats, mean[:], rstd[:], scratch[:], expo, step, 0)

        @block.tensor
        def _(pe):
            pe.wait_ge(consts_in, 48)
            pe.wait_ge(ones_set, 2)
            with pe.Fori(0, TILES // 2) as m:
                for par in range(2):
                    t = m * 2 + par
                    pe.wait_ge(picked, t + 1)
                    pe.wait_ge(tile_kept, t + 1)
                    for k in range(KE):
                        mm = pe.transpose(turned[par][:, k * P:(k + 1) * P],
                                          tile_in[:, par, k * P:(k + 1) * P], ident_f[:])
                    mm.then_inc(tile_turned, 1)
                    pe.wait_ge(tile_kept, t + 3)
                    pe.wait_ge(summed, t + 1)
                    for k in range(KE):
                        pe.matmul(joined[par][:, 0:E], tile_T[:, par, k * P:(k + 1) * P],
                                  weights[:, k, :], start=k == 0, stop=False)
                    pe.matmul(joined[par][:, 0:E], ones_row[:], bias[:], start=False, stop=True
                              ).then_inc(tile_joined, 1)

        @block.scalar
        def _(act):
            act.preload_act_table(ACT.Exp)
            act.sem_inc(tile_kept, 2)
            with act.Fori(0, TILES // 2) as m:
                for par in range(2):
                    t = m * 2 + par
                    act.wait_ge(tile_turned, t + 3)
                    act.wait_ge(summed, t + 1)
                    act.activation(tile_T[:, par, :], turned[par][:, 0:E], ACT.Copy).then_inc(tile_kept, 1)

        @block.vector
        def _(dve):
            dve.memset(ones_row[:], 1.0).then_inc(ones_set, 1)
            dve.sem_inc(summed, 2)
            dve.wait_ge(x_in, 16)
            with dve.Fori(0, TILES // 2) as m:
                for par in range(2):
                    t = m * 2 + par
                    dve.wait_ge(tile_joined, t + 1)
                    tile = tokens[:, bass.ds(t, 1), :]
                    dve.tensor_tensor(tile, joined[par][:, 0:E], tile, ALU.add).then_inc(summed, 1)
                    dve.wait_ge(summed, t + 3)
                    dve.bn_stats(stats[:, bass.ds(t, 1), :], tile).then_inc(counted, 1)
            dve.wait_ge(counted, TILES)
            end = layernorm_params(dve, None, stats, mean[:], rstd[:], scratch[:], expo, step, 0)
            dve.wait_ge(step, end)
            normalise(dve, tokens, mean, rstd, normed)


def normalise(dve, tokens, mean, rstd, normed):
    with dve.Fori(0, TILES) as t:
        tile = tokens[:, bass.ds(t, 1), :]
        dve.tensor_scalar(tile, tile, mean[:, bass.ds(t, 1)], rstd[:, bass.ds(t, 1)],
                          ALU.subtract, ALU.mult).then_inc(normed, 1)


DEPTH = 2
LHEADS = 8
LD = 64
INNER = LHEADS * LD
KI = INNER // P
HID = 682
HT = -(-HID // P)
HTAIL = HID - (HT - 1) * P
BATCH = 4
BATCHES = TILES // BATCH
QK_SCALE = 8.0


def same(pool, out, in_, ones):
    return pool.tensor_tensor(out, in_, ones[:].to_broadcast(list(in_.shape)), ALU.mult)


def local_layers(nc, w_qkv, qk_rows, w_o, ln_gb, w_1, b_1, w_2, b_2, rotary, masks, ident, tokens, first_norm, out):
    with ExitStack() as ctx:
        sb = lambda name, shape, dt=F32: ctx.enter_context(nc.sbuf_tensor(name, shape, dt))
        sem = lambda name: ctx.enter_context(nc.semaphore(name))
        bank = [ctx.enter_context(nc.psum_tensor(f"bank{i}", [P, CH], F32)) for i in range(4, 8)]
        quad = ctx.enter_context(nc.psum_tensor("quad", [P, 4, CH], F32))
        wqkv = sb("wqkv", [P, KE, 3 * INNER])
        wo = sb("wo", [P, KI, E])
        w1 = sb("w1", [P, KE, 2 * HID])
        w2 = sb("w2", [P, HT, E])
        b2 = sb("b2", [1, E])
        ones_row = sb("layer_ones", [1, P])
        b1 = sb("b1", [P, 2, HT])
        gb = sb("ln_gb", [P, 2, KE])
        qk_row = sb("qk_row", [P, 4 * LD])
        rot = sb("rot", [P, TILES, 4 * LD])
        mask = sb("mask", [P, 2, SLAB])
        ident_f = sb("layer_ident", [P, P])
        tile_in = [sb(f"win_tile{i}", [P, E]) for i in range(2)]
        hT_a = [sb(f"hT_a{i}", [P, P]) for i in range(2)]
        hT_b = [sb(f"hT_b{i}", [P, P + 1]) for i in range(2)]
        v_kept = [sb(f"v_kept{i}", [P, INNER]) for i in range(2)]
        k_T = [sb(f"k_T{i}", [P, KI, P]) for i in range(2)]
        q_T = sb("q_T", [P, KI, P])
        squares = sb("squares", [P, 2 * LHEADS, LD])
        norm = sb("norm", [P, 2 * LHEADS, 1])
        turn = sb("turn", [P, 4 * LD])
        rot_a = sb("rot_a", [P, 2 * LHEADS, LD])
        rot_b = sb("rot_b", [P, 2 * LHEADS, LD])
        sim = sb("sim", [P, LHEADS, SLAB])
        prob = sb("prob", [P, LHEADS, SLAB])
        top = sb("top", [P, LHEADS])
        shift = sb("shift", [P, LHEADS])
        total = sb("total", [P, LHEADS, 1])
        inv_total = sb("inv_total", [P, LHEADS, 1])
        prob_T = sb("prob_T", [P, 2 * LHEADS, P])
        o_tok = sb("o_tok", [P, LHEADS, LD])
        o_T = sb("o_T", [P, KI, P])
        half_in = sb("half_in", [P, BATCH, P])
        half_T = sb("half_T", [P, BATCH * P + 1])
        h_tok = sb("h_tok", [P, BATCH, E])
        h_T = sb("h_T", [P, KE, CH])
        gate = sb("gate", [P, 2, CH])
        hidden = sb("hidden", [P, HT, CH])
        stats = sb("layer_stats", [P, BATCH, 6])
        mean, rstd, scratch = (sb(f"layer_{n}", [P, BATCH]) for n in ("mean", "rstd", "scratch"))
        expo = sb("layer_expo", [P, TILES])
        one = sb("one", [P, 1, 1])
        end_stats = sb("end_stats", [P, TILES, 6])
        end_mean, end_rstd, end_scratch = (sb(f"end_{n}", [P, TILES]) for n in ("mean", "rstd", "scratch"))

        fixed_in = sem("fixed_in")
        set_up = sem("set_up")
        attn_w_in = sem("attn_w_in")
        ffn_w_in = sem("ffn_w_in")
        names = ("tile_ready hT_ready hT_kept qkv_ready squared v_taken turn_ready turned_a turned_b norm_guard "
                 "norm_ready rot_sum rotated qk_T_ready qk_T_kept sim_ready sim_kept top_ready shift_ready "
                 "exp_done prob_T_ready prob_T_act prob_T_dve pv_ready total_inv o_ready o_T_ready o_T_kept "
                 "wo_ready win_done "
                 "half_ready half_T_ready carried half_T_kept half_back h_left h_right h_stats step h_normed "
                 "h_T_ready h_T_kept up_ready gate_ready hidden_ready down_ready batch_done "
                 "past_cleared first_in end_added end_counted end_step end_normed stored").split()
        s = {n: sem("l_" + n) for n in names}
        S = type("Semaphores", (), s)
        block = ctx.enter_context(nc.Block())
        qk_ps = (bank[1], bank[2])
        v_ps = bank[3]
        o_ps = bank[0]
        LAYER = TILES
        last_pair = TILES // 2 - 1

        def slot(h):
            return (h % 2) * (LHEADS // 2) + h // 2

        def windows(eng, l, step):
            with eng.Fori(0, last_pair) as m:
                for par in range(2):
                    step(m * 2 + par, l * LAYER + m * 2 + par, par, True)
            step(TILES - 2, l * LAYER + TILES - 2, 0, True)
            step(TILES - 1, l * LAYER + TILES - 1, 1, False)

        def batches(eng, l, step):
            with eng.Fori(0, BATCHES - 1) as b:
                step(b, l * BATCHES + b, True)
            step(BATCHES - 1, l * BATCHES + BATCHES - 1, False)

        @block.sync
        def _(sp):
            sp.dma_start(ident_f[:], ident).then_inc(fixed_in, 16)
            sp.dma_start(mask[:], masks.rearrange("m p n -> p m n")).then_inc(fixed_in, 16)
            sp.dma_start(rot[:], rotary.rearrange("(t p) n -> p t n", p=P)).then_inc(fixed_in, 16)
            with sp.Fori(0, DEPTH) as l:
                sp.wait_ge(S.win_done, l * LAYER)
                one = bass.ds(l, 1)
                sp.dma_start(wqkv[:], w_qkv[one].rearrange("a (k p) n -> p (a k) n", p=P)).then_inc(attn_w_in, 16)
                sp.dma_start(wo[:], w_o[one].rearrange("a (k p) n -> p (a k) n", p=P)).then_inc(attn_w_in, 16)
                sp.dma_start(qk_row[:], qk_rows[one].partition_broadcast(P)).then_inc(attn_w_in, 16)
                sp.wait_ge(S.batch_done, l * BATCHES)
                sp.dma_start(w1[:], w_1[one].rearrange("a (k p) n -> p (a k) n", p=P)).then_inc(ffn_w_in, 16)
                full = (HT - 1) * P
                sp.dma_start(w2[:, 0:HT - 1, :], w_2[one, 0:full].rearrange("a (k p) n -> p (a k) n", p=P)
                             ).then_inc(ffn_w_in, 16)
                sp.dma_start(w2[0:HTAIL, HT - 1, :], w_2[one, full:HID].rearrange("a p n -> p (a n)")
                             ).then_inc(ffn_w_in, 16)
                for side in range(2):
                    at = side * HID
                    sp.dma_start(b1[:, side, 0:HT - 1], b_1[one, at:at + full].rearrange("a (k p) -> p (a k)", p=P),
                                 allow_slow_non_contiguous=True).then_inc(ffn_w_in, 16)
                    sp.dma_start(b1[0:HTAIL, side, HT - 1:HT],
                                 b_1[one, at + full:at + HID].rearrange("a p -> p a"),
                                 allow_slow_non_contiguous=True).then_inc(ffn_w_in, 16)
                sp.dma_start(b2[:], b_2[one]).then_inc(ffn_w_in, 16)
                sp.dma_start(gb[:], ln_gb[one].rearrange("a g (k p) -> p (a g) k", p=P),
                             allow_slow_non_contiguous=True).then_inc(ffn_w_in, 16)
            sp.wait_ge(S.win_done, DEPTH * LAYER)
            sp.dma_start(rot[:], first_norm).then_inc(S.first_in, 16)
            QUARTER = TILES // 4
            for i in range(4):
                sp.wait_ge(S.end_normed, (i + 1) * QUARTER)
                sp.dma_start(out.rearrange("(t p) e -> p t e", p=P)[:, i * QUARTER:(i + 1) * QUARTER, :],
                             tokens[:, i * QUARTER:(i + 1) * QUARTER, :]).then_inc(S.stored, 16)
            sp.wait_ge(S.stored, 64)
        FFN_DMAS = 9 * 16

        @block.gpsimd
        def _(pool):
            pool.memset(expo[:], -0.5).then_inc(set_up, 1)
            pool.memset(one[:], 1.0).then_inc(set_up, 1)
            for i in range(2):
                pool.memset(k_T[i][:], 0.0).then_inc(set_up, 1)
                pool.memset(v_kept[i][:], 0.0).then_inc(set_up, 1)
            pool.wait_ge(set_up, 8)

            def pick(w, g, par):
                pool.wait_ge(S.hT_ready, g + 1)
                same(pool, tile_in[par][:].rearrange("p (a n) -> p a n", a=1), tokens[:, bass.ds(w, 1), :], one).then_inc(S.tile_ready, 1)

            def rotate(g):
                pool.wait_ge(S.norm_guard, g + 1)
                pool.tensor_tensor(norm[:], norm[:], expo[:, 0:2 * LHEADS].rearrange("p (h a) -> p h a", a=1),
                                   ALU.pow).then_inc(S.norm_ready, 1)
                pool.wait_ge(S.turned_b, g * 2 + 2)
                pool.tensor_tensor(rot_a[:], rot_a[:], rot_b[:], ALU.add).then_inc(S.rot_sum, 1)

            def window(w, g, par, more):
                if more:
                    pick(w + 1, g + 1, 1 - par)
                    rotate(g + 1)

            def take_half(b, g):
                pool.wait_ge(S.half_T_ready, g + 0)
                same(pool, half_in[:], tokens[:, bass.ds(b * BATCH, BATCH), P:E], one).then_inc(S.half_ready, 1)
                pool.wait_ge(S.h_T_ready, g * 2)
                same(pool, h_tok[:, :, 0:P], tokens[:, bass.ds(b * BATCH, BATCH), 0:P], one).then_inc(S.h_left, 1)
                layernorm_params(None, pool, stats, mean[:], rstd[:], scratch[:], expo, S.step, g * 8)

            with pool.Fori(0, DEPTH) as l:
                pool.wait_ge(S.batch_done, l * BATCHES)
                pick(0, l * LAYER, 0)
                rotate(l * LAYER)
                windows(pool, l, window)
                pool.wait_ge(S.win_done, l * LAYER + LAYER)
                take_half(0, l * BATCHES)
                batches(pool, l, lambda b, g, more: take_half(b + 1, g + 1) if more else None)
            layernorm_params(None, pool, end_stats, end_mean[:], end_rstd[:], end_scratch[:], expo, S.end_step, 0)

        @block.tensor
        def _(pe):
            def turn_tile(g, par):
                pe.wait_ge(S.tile_ready, g + 1)
                pe.wait_ge(S.v_taken, g)
                for k in range(KE):
                    mm = pe.transpose(v_ps[:, k * P:(k + 1) * P], tile_in[par][:, k * P:(k + 1) * P], ident_f[:])
                mm.then_inc(S.hT_ready, 1)

            def project(g, par):
                pe.wait_ge(S.hT_kept, g + 1)
                pe.wait_ge(S.qk_T_kept, g)
                for j, ps in enumerate((*qk_ps, v_ps)):
                    for k, h in enumerate((hT_a[par][:], hT_b[par][:, 0:P])):
                        mm = pe.matmul(ps[:], h, wqkv[:, k, j * INNER:(j + 1) * INNER],
                                       start=k == 0, stop=k == KE - 1)
                mm.then_inc(S.qkv_ready, 1)

            def turn_qk(g):
                pe.wait_ge(S.rotated, g + 1)
                for j in range(2):
                    for i in range(KI):
                        mm = pe.transpose(qk_ps[j][:, i * P:(i + 1) * P],
                                          rot_a[:].rearrange("p h d -> p (h d)")[:, (j * KI + i) * P:(j * KI + i + 1) * P],
                                          ident_f[:])
                mm.then_inc(S.qk_T_ready, 1)

            def similarities(g, par):
                pe.wait_ge(S.qk_T_kept, g + 1)
                pe.wait_ge(S.prob_T_act, g)
                pe.wait_ge(S.prob_T_dve, g)
                for h in range(LHEADS):
                    rows = slice(LD * (h % 2), LD * (h % 2 + 1))
                    for c, keys in enumerate((k_T[1 - par], k_T[par])):
                        at = (slot(h) % 2) * SLAB + c * P
                        mm = pe.matmul(quad[:, slot(h) // 2, at:at + P], q_T[rows, h // 2, :], keys[rows, h // 2, :],
                                       start=True, stop=True)
                mm.then_inc(S.sim_ready, 1)

            def turn_prob(g):
                pe.wait_ge(S.exp_done, g + 1)
                for h in range(LHEADS):
                    for c in range(2):
                        j = 2 * h + c
                        mm = pe.transpose(quad[:, j // 4, (j % 4) * P:(j % 4 + 1) * P],
                                          prob[:, h, c * P:(c + 1) * P], ident_f[:])
                mm.then_inc(S.prob_T_ready, 1)

            def weigh(g, par):
                pe.wait_ge(S.prob_T_act, g + 1)
                pe.wait_ge(S.prob_T_dve, g + 1)
                pe.wait_ge(S.win_done, g)
                for h in range(LHEADS):
                    for c, v in enumerate((v_kept[1 - par], v_kept[par])):
                        j = slot(h)
                        mm = pe.matmul(o_ps[:, j * LD:(j + 1) * LD], prob_T[:, 2 * j + c, :],
                                       v[:, h * LD:(h + 1) * LD], start=c == 0, stop=c == 1)
                mm.then_inc(S.pv_ready, 1)

            def turn_o(g):
                pe.wait_ge(S.o_ready, g + 1)
                for i in range(KI):
                    mm = pe.transpose(o_ps[:, i * P:(i + 1) * P],
                                      o_tok[:].rearrange("p h d -> p (h d)")[:, i * P:(i + 1) * P], ident_f[:])
                mm.then_inc(S.o_T_ready, 1)

            def project_o(g):
                pe.wait_ge(S.o_T_kept, g + 1)
                for i in range(KI):
                    mm = pe.matmul(o_ps[:, 0:E], o_T[:, i, :], wo[:, i, :], start=i == 0, stop=i == KI - 1)
                mm.then_inc(S.wo_ready, 1)

            def window(w, g, par, more):
                if more:
                    turn_tile(g + 1, 1 - par)
                similarities(g, par)
                if more:
                    project(g + 1, 1 - par)
                turn_prob(g)
                weigh(g, par)
                if more:
                    turn_qk(g + 1)
                turn_o(g)
                project_o(g)

            turned, back, h_ps = bank[0], bank[0], bank[1]
            down = (bank[2], bank[3])

            def turn_half(g):
                pe.wait_ge(S.half_ready, g + 1)
                pe.wait_ge(S.h_right, g)
                for i in range(BATCH):
                    mm = pe.transpose(turned[:, i * P:(i + 1) * P], half_in[:, i, :], ident_f[:])
                mm.then_inc(S.half_T_ready, 1)

            def turn_back(g):
                pe.wait_ge(S.half_T_kept, g + 1)
                for i in range(BATCH):
                    mm = pe.transpose(back[:, i * P:(i + 1) * P], half_T[:, i * P:(i + 1) * P], ident_f[:])
                mm.then_inc(S.half_back, 1)

            def turn_h(g):
                pe.wait_ge(S.h_normed, g + 1)
                for k in range(KE):
                    pe.wait_ge(S.h_T_kept, g * 2 + k)
                    for i in range(BATCH):
                        mm = pe.transpose(h_ps[:, i * P:(i + 1) * P], h_tok[:, i, k * P:(k + 1) * P], ident_f[:])
                    mm.then_inc(S.h_T_ready, 1)

            def up(g, i):
                rows = P if i < HT - 1 else HTAIL
                if i == 0:
                    pe.wait_ge(S.h_T_kept, g * 2 + 2)
                pe.wait_ge(S.hidden_ready, g * HT + i + 1)
                for side in range(2):
                    at = side * HID + i * P
                    for k in range(KE):
                        mm = pe.matmul(quad[0:rows, 2 * (i % 2) + side, :], w1[:, k, at:at + rows], h_T[:, k, :],
                                       start=k == 0, stop=k == KE - 1)
                mm.then_inc(S.up_ready, 1)

            def go_down(g):
                pe.wait_ge(S.hidden_ready, g * HT + HT + 2)
                pe.wait_ge(S.batch_done, g)
                for w in range(BATCH):
                    res = down[w // 2][:, (w % 2) * E:(w % 2 + 1) * E]
                    for i in range(HT):
                        rows = P if i < HT - 1 else HTAIL
                        pe.matmul(res, hidden[0:rows, i, w * P:(w + 1) * P], w2[0:rows, i, :],
                                  start=i == 0, stop=False)
                    mm = pe.matmul(res, ones_row[:], b2[:], start=False, stop=True)
                mm.then_inc(S.down_ready, 1)

            def batch(b, g, more):
                for i in range(HT):
                    up(g, i)
                    if more and i == 0:
                        turn_half(g + 1)
                    if more and i == 1:
                        turn_back(g + 1)
                go_down(g)
                if more:
                    turn_h(g + 1)

            pe.wait_ge(fixed_in, 48)
            pe.wait_ge(set_up, 8)
            with pe.Fori(0, DEPTH) as l:
                pe.wait_ge(attn_w_in, l * 48 + 48)
                turn_tile(l * LAYER, 0)
                project(l * LAYER, 0)
                turn_qk(l * LAYER)
                windows(pe, l, window)
                pe.wait_ge(S.win_done, l * LAYER + LAYER)
                pe.wait_ge(ffn_w_in, l * FFN_DMAS + FFN_DMAS)
                turn_half(l * BATCHES)
                turn_back(l * BATCHES)
                turn_h(l * BATCHES)
                batches(pe, l, batch)
                pe.wait_ge(S.batch_done, l * BATCHES + BATCHES)

        @block.scalar
        def _(act):
            def keep_hT(g, par):
                act.wait_ge(S.hT_ready, g + 3)
                act.activation(hT_a[par][:], v_ps[:, 0:P], ACT.Copy)
                act.activation(hT_b[1 - par][:, 0:1], v_ps[:, 2 * P - 1:2 * P], ACT.Copy)
                act.activation(hT_b[par][:, 1:P + 1], v_ps[:, P:2 * P], ACT.Copy).then_inc(S.hT_kept, 1)

            def square(g):
                act.wait_ge(S.qkv_ready, g + 1)
                act.wait_ge(S.norm_guard, g)
                for j in range(2):
                    act.activation(squares[:, j * LHEADS:(j + 1) * LHEADS, :],
                                   qk_ps[j][:].rearrange("p (h d) -> p h d", d=LD), ACT.Square
                                   ).then_inc(S.squared, 1)

            def take_v(g, par):
                act.wait_ge(S.pv_ready, g)
                act.activation(v_kept[par][:], v_ps[:], ACT.Copy).then_inc(S.v_taken, 1)

            def keep_qk(g, par):
                act.wait_ge(S.qk_T_ready, g + 1)
                act.activation(q_T[:].rearrange("p i n -> p (i n)"), qk_ps[0][:], ACT.Copy)
                act.activation(k_T[par][:].rearrange("p i n -> p (i n)"), qk_ps[1][:], ACT.Copy
                               ).then_inc(S.qk_T_kept, 1)

            def exps(g):
                act.wait_ge(S.shift_ready, g + 1)
                act.wait_ge(S.prob_T_ready, g)
                for h in range(LHEADS):
                    ins = act.activation(prob[:, h, :], sim[:, h, :], ACT.Exp, bias=shift[:, h:h + 1],
                                         scale=QK_SCALE, accum_out=total[:, h, :])
                ins.then_inc(S.exp_done, 1)

            def window(w, g, par, more):
                if more:
                    keep_hT(g + 1, 1 - par)
                act.wait_ge(S.o_ready, g)
                if more:
                    square(g + 1)
                exps(g)
                act.wait_ge(S.prob_T_ready, g + 1)
                act.activation(prob_T[:, 0:LHEADS, :].rearrange("p (a b) n -> p a (b n)", a=2), quad[:, 0:2, :],
                               ACT.Copy).then_inc(S.prob_T_act, 1)
                if more:
                    act.wait_ge(S.pv_ready, g + 1)
                    take_v(g + 1, 1 - par)
                    keep_qk(g + 1, 1 - par)
                act.wait_ge(S.o_T_ready, g + 1)
                act.activation(o_T[:].rearrange("p i n -> p (i n)"), o_ps[:], ACT.Copy).then_inc(S.o_T_kept, 1)

            def keep_half(g):
                act.wait_ge(S.half_T_ready, g + 1)
                act.wait_ge(S.half_back, g)
                act.activation(half_T[:, 0:1], half_T[:, BATCH * P:BATCH * P + 1], ACT.Copy).then_inc(S.carried, 1)
                act.wait_ge(S.carried, g + 1)
                act.activation(half_T[:, 1:BATCH * P + 1], bank[0][:], ACT.Copy).then_inc(S.half_T_kept, 1)

            def keep_h(g):
                for k in range(KE):
                    act.wait_ge(S.h_T_ready, g * 2 + k + 1)
                    act.activation(h_T[:, k, :], bank[1][:], ACT.Identity, scale=gb[:, 0, k:k + 1],
                                   bias=gb[:, 1, k:k + 1]).then_inc(S.h_T_kept, 1)

            def batch(b, g, more):
                for i in range(HT):
                    rows = P if i < HT - 1 else HTAIL
                    act.wait_ge(S.up_ready, g * HT + i + 1)
                    act.wait_ge(S.hidden_ready, g * HT + i + 1)
                    act.activation(gate[0:rows, i % 2, :], quad[0:rows, 2 * (i % 2) + 1, :], ACT.Gelu,
                                   bias=b1[0:rows, 1, i:i + 1]).then_inc(S.gate_ready, 1)
                    if more and i == 0:
                        keep_half(g + 1)
                if more:
                    keep_h(g + 1)

            act.wait_ge(set_up, 8)
            with act.Fori(0, DEPTH) as l:
                act.preload_act_table(ACT.Exp)
                act.wait_ge(S.past_cleared, l + 1)
                keep_hT(l * LAYER, 0)
                square(l * LAYER)
                take_v(l * LAYER, 0)
                keep_qk(l * LAYER, 0)
                windows(act, l, window)
                act.preload_act_table(ACT.Gelu)
                keep_half(l * BATCHES)
                act.wait_ge(ffn_w_in, l * FFN_DMAS + FFN_DMAS)
                keep_h(l * BATCHES)
                batches(act, l, batch)

        @block.vector
        def _(dve):
            dve.memset(ones_row[:], 1.0).then_inc(set_up, 1)
            dve.memset(squares[:], 0.0).then_inc(set_up, 1)
            dve.sem_inc(S.hT_ready, 2)
            dve.sem_inc(S.hidden_ready, 2)

            def scale_rotate(w, g):
                dve.wait_ge(S.turned_b, g * 2)
                dve.tensor_tensor(turn[:], rot[:, bass.ds(w, 1), :], qk_row[:], ALU.mult).then_inc(S.turn_ready, 1)
                dve.wait_ge(S.turn_ready, g + 1)
                dve.wait_ge(S.qk_T_ready, g)
                LH = LD // 2
                for j in range(2):
                    dve.wait_ge(S.squared, g * 2 + j + 1)
                    qk = qk_ps[j][:].rearrange("p (h d) -> p h d", d=LD)
                    heads = slice(j * LHEADS, (j + 1) * LHEADS)
                    cos = turn[:, j * LD:(j + 1) * LD].rearrange("p (a d) -> p a d", a=1)
                    sin = turn[:, (2 + j) * LD:(3 + j) * LD].rearrange("p (a d) -> p a d", a=1)
                    dve.tensor_tensor(rot_a[:, heads, :], qk, cos.to_broadcast([P, LHEADS, LD]), ALU.mult)
                    dve.tensor_tensor(rot_b[:, heads, 0:LH], qk[:, :, LH:LD],
                                      sin[:, :, 0:LH].to_broadcast([P, LHEADS, LH]), ALU.mult)
                    dve.tensor_tensor(rot_b[:, heads, LH:LD], qk[:, :, 0:LH],
                                      sin[:, :, LH:LD].to_broadcast([P, LHEADS, LH]), ALU.mult
                                      ).then_inc(S.turned_b, 1)

            def sum_squares(g):
                dve.wait_ge(S.squared, g * 2 + 2)
                dve.wait_ge(S.rotated, g)
                dve.tensor_reduce(norm[:, :, 0], squares[:], AX.X, ALU.add).then_inc(S.turned_a, 1)
                dve.wait_ge(S.turned_a, g + 1)
                dve.tensor_scalar(norm[:], norm[:], 1e-24, None, ALU.max).then_inc(S.norm_guard, 1)

            def divide_norm(g):
                dve.wait_ge(S.rot_sum, g + 1)
                dve.wait_ge(S.norm_ready, g + 1)
                dve.tensor_tensor(rot_a[:], rot_a[:], norm[:].to_broadcast([P, 2 * LHEADS, LD]), ALU.mult
                                  ).then_inc(S.rotated, 1)

            def window(w, g, par, more):
                dve.wait_ge(S.sim_ready, g + 1)
                dve.wait_ge(S.exp_done, g)
                which = (w + TILES - 1) // TILES
                sims = quad[:].rearrange("p a (b n) -> p a b n", b=2)
                dve.tensor_tensor(sim[:].rearrange("p (a b) n -> p a b n", b=2), sims,
                                  mask[:, bass.ds(which, 1), :].rearrange("p (a b) n -> p a b n", b=1)
                                  .to_broadcast([P, 4, 2, SLAB]), ALU.add).then_inc(S.sim_kept, 1)
                dve.wait_ge(S.sim_kept, g + 1)
                dve.tensor_reduce(top[:], sim[:], AX.X, ALU.max).then_inc(S.top_ready, 1)
                dve.wait_ge(S.top_ready, g + 1)
                dve.tensor_scalar(shift[:], top[:], -QK_SCALE, None, ALU.mult).then_inc(S.shift_ready, 1)
                if more:
                    scale_rotate(w + 1, g + 1)
                dve.wait_ge(S.prob_T_ready, g + 1)
                dve.tensor_copy(prob_T[:, LHEADS:, :].rearrange("p (a b) n -> p a (b n)", a=2), quad[:, 2:4, :]
                                ).then_inc(S.prob_T_dve, 1)
                if more:
                    sum_squares(g + 1)
                dve.reciprocal(inv_total[:], total[:]).then_inc(S.total_inv, 1)
                dve.wait_ge(S.total_inv, g + 1)
                dve.wait_ge(S.pv_ready, g + 1)
                dve.tensor_tensor(o_tok[:].rearrange("p (a b) d -> p b a d", b=2),
                                  o_ps[:].rearrange("p (b a d) -> p b a d", b=2, d=LD),
                                  inv_total[:].rearrange("p (b a) d -> p b a d", b=2)
                                  .to_broadcast([P, 2, LHEADS // 2, LD]), ALU.mult).then_inc(S.o_ready, 1)
                if more:
                    divide_norm(g + 1)
                dve.wait_ge(S.wo_ready, g + 1)
                tile = tokens[:, bass.ds(w, 1), :]
                dve.tensor_tensor(tile, o_ps[:, 0:E], tile, ALU.add).then_inc(S.win_done, 1)

            def norm_batch(g):
                dve.wait_ge(S.half_back, g + 1)
                dve.wait_ge(S.h_left, g + 1)
                dve.tensor_copy(h_tok[:, :, P:E], bank[0][:].rearrange("p (b n) -> p b n", n=P)).then_inc(S.h_right, 1)
                dve.wait_ge(S.h_right, g + 1)
                for i in range(BATCH):
                    ins = dve.bn_stats(stats[:, i, :], h_tok[:, i, :])
                ins.then_inc(S.h_stats, 1)
                dve.wait_ge(S.h_stats, g + 1)
                layernorm_params(dve, None, stats, mean[:], rstd[:], scratch[:], expo, S.step, g * 8)
                dve.wait_ge(S.step, g * 8 + 8)
                for i in range(BATCH):
                    ins = dve.tensor_scalar(h_tok[:, i, :], h_tok[:, i, :], mean[:, i:i + 1], rstd[:, i:i + 1],
                                            ALU.subtract, ALU.mult)
                ins.then_inc(S.h_normed, 1)

            def batch(b, g, more):
                for i in range(HT):
                    rows = P if i < HT - 1 else HTAIL
                    dve.wait_ge(S.gate_ready, g * HT + i + 1)
                    if i == 0:
                        dve.wait_ge(S.down_ready, g)
                    dve.scalar_tensor_tensor(out=hidden[0:rows, i, :], in0=quad[0:rows, 2 * (i % 2), :],
                                             scalar=b1[0:rows, 0, i:i + 1], in1=gate[0:rows, i % 2, :],
                                             op0=ALU.add, op1=ALU.mult).then_inc(S.hidden_ready, 1)
                    if more and i == 2:
                        norm_batch(g + 1)
                dve.wait_ge(S.down_ready, g + 1)
                for j in range(2):
                    tiles = tokens[:, bass.ds(b * BATCH + 2 * j, 2), :]
                    ins = dve.tensor_tensor(tiles, bank[2 + j][:].rearrange("p (b n) -> p b n", n=E), tiles, ALU.add)
                ins.then_inc(S.batch_done, 1)

            dve.wait_ge(fixed_in, 48)
            with dve.Fori(0, DEPTH) as l:
                dve.memset(hT_b[0][:, 0:1], 0.0)
                dve.memset(half_T[:, BATCH * P:BATCH * P + 1], 0.0).then_inc(S.past_cleared, 1)
                dve.wait_ge(attn_w_in, l * 48 + 48)
                scale_rotate(0, l * LAYER)
                sum_squares(l * LAYER)
                divide_norm(l * LAYER)
                windows(dve, l, window)
                dve.wait_ge(ffn_w_in, l * FFN_DMAS + FFN_DMAS)
                norm_batch(l * BATCHES)
                batches(dve, l, batch)
            dve.wait_ge(S.batch_done, DEPTH * BATCHES)
            dve.wait_ge(S.first_in, 16)
            with dve.Fori(0, TILES) as t:
                tile = tokens[:, bass.ds(t, 1), :]
                dve.tensor_tensor(tile, tile, rot[:, bass.ds(t, 1), :], ALU.add).then_inc(S.end_added, 1)
                dve.wait_ge(S.end_added, t + 1)
                dve.bn_stats(end_stats[:, bass.ds(t, 1), :], tokens[:, bass.ds(t, 1), :]).then_inc(S.end_counted, 1)
            dve.wait_ge(S.end_counted, TILES)
            end = layernorm_params(dve, None, end_stats, end_mean[:], end_rstd[:], end_scratch[:], expo,
                                   S.end_step, 0)
            dve.wait_ge(S.end_step, end)
            normalise(dve, tokens, end_mean, end_rstd, S.end_normed)


def build(nc, ins, out):
    q_stack = nc.dram_tensor("q_stack", [HEADS, ROWS, N], BF16, kind="Internal").ap()
    k_parts = nc.dram_tensor("k_parts", [HEADS, 3 * D, 2 * N], BF16, kind="Internal").ap()
    v_wide = nc.dram_tensor("v_wide", [HEADS, P, 2 * TILES * VW], F32, kind="Internal").ap()
    first_norm = nc.dram_tensor("first_norm", [P, TILES, E], F32, kind="Internal").ap()
    with ExitStack() as ctx:
        tokens = ctx.enter_context(nc.sbuf_tensor("tokens", [P, TILES, E], F32))
        project_heads(nc, ins["x_T"], ins["w_in_T"], ins["b_in"], ins["pe_edges"], q_stack, k_parts, v_wide)
        with nc.sbuf_tensor("attn", [P, TILES, E], F32) as attn:
            attend(nc, q_stack, k_parts, v_wide, ins["rel_T"], ins["ident"], ins["part_sum"], attn)
            join_heads(nc, ins["x"], ins["w_out_T"], ins["b_out"], ins["ident"], attn, tokens, first_norm)
        local_layers(nc, ins["w_qkv"], ins["qk_rows"], ins["w_o"], ins["ln_gb"], ins["w_1"], ins["b_1"],
                     ins["w_2"], ins["b_2"], ins["rotary"], ins["masks"], ins["ident"], tokens, first_norm, out)


def shape_constants():
    import numpy as np
    f = np.float32
    half = np.arange(0, LD, 2, dtype=f)
    inv_freq = f(1.0) / np.power(f(10000.0), half / f(LD), dtype=f)
    t = np.arange(N, dtype=f)
    freqs = t[:, None] * inv_freq[None, :]
    base = (half + f(0.4 * LD)) / f(1.4 * LD)
    power = (t - f(N // 2)) / f(P // 2)
    scale = np.power(base[None, :], power[:, None], dtype=f)
    cos, sin = np.cos(freqs), np.sin(freqs)
    both = lambda a, b: np.concatenate([a, b], axis=1)
    rotary = np.concatenate([both(cos * scale, cos * scale), both(cos / scale, cos / scale),
                             both(-sin * scale, sin * scale), both(-sin / scale, sin / scale)], axis=1)
    i, j = np.arange(P)[:, None], np.arange(SLAB)[None, :] - P
    hidden = (i < j) | (i > j + P)
    masks = np.stack([hidden | (j < 0), hidden]) * f(-3e37)
    part_sum = np.zeros((P, VW), f)
    for quadrant in range(0, P, 32):
        part_sum[quadrant:quadrant + VW] = np.eye(VW, dtype=f)
    return {"rotary": rotary.astype(f), "masks": masks.astype(f), "part_sum": part_sum,
            "ident": np.eye(P, dtype=f)}


def kernel(**inputs):
    import numpy as np
    import concourse.bacc as bacc
    from concourse.bass_utils import run_bass_kernel_spmd

    g = {k: np.asarray(v) for k, v in inputs.items()}
    x = g["L0_attn_q"].reshape(N, E)
    pe = g["L0_attn_rel_pe"]
    qs, ks = g["L0_ffn_q_scale"], g["L0_ffn_k_scale"]
    swap = lambda a: np.concatenate([a[:, LD // 2:], a[:, :LD // 2]], axis=1)
    arrays = {
        "x": x, "x_T": x.T, "w_in_T": g["L0_attn_in_proj_weight"].T, "b_in": g["L0_attn_in_proj_bias"],
        "pe_edges": np.tile(pe[::2 * CLIP], (1, GROUP)), "rel_T": pe.T,
        "w_out_T": g["L0_attn_out_w"].T, "b_out": g["L0_attn_out_b"],
        "w_qkv": g["L0_ffn_wqkv"], "qk_rows": np.concatenate([qs, ks, swap(qs), swap(ks)], axis=1),
        "w_o": g["L0_ffn_wo"], "ln_gb": np.stack([g["L0_ffn_ln_g"], g["L0_ffn_ln_b"]], axis=1),
        "w_1": g["L0_ffn_w1"], "b_1": g["L0_ffn_b1"], "w_2": g["L0_ffn_w2"], "b_2": g["L0_ffn_b2"],
        **shape_constants(),
    }
    nc = bacc.Bacc("TRN2", target_bir_lowering=False, num_devices=1)
    ins, feed = {}, {}
    for name, a in arrays.items():
        a = np.ascontiguousarray(a)
        feed[f"in_{name}"] = a
        ins[name] = nc.dram_tensor(f"in_{name}", a.shape, mybir.dt.from_np(a.dtype), kind="ExternalInput").ap()
    out = nc.dram_tensor("out_tokens", (N, E), F32, kind="ExternalOutput").ap()
    build(nc, ins, out)
    r = run_bass_kernel_spmd(nc, [feed], core_ids=[0])
    return r.results[0]["out_tokens"].reshape(1, N, E)
```

```python
from contextlib import ExitStack

import concourse.bass as bass
from concourse import mybir

F32 = mybir.dt.float32
BF16 = mybir.dt.bfloat16
ACT = mybir.ActivationFunctionType
ALU = mybir.AluOpType
AX = mybir.AxisListType

P = 128
N = 4096
E = 256
KE = E // P
TILES = N // P
LN_EPS = 1e-5

HEADS = 16
D = E // HEADS
CLIP = 64
GROUP = P // D
CH = 512
CHUNKS = N // CH
TPC = CH // P
Q_PARTS = (0, 0, 0, 1, 1, 2)
K_RUNS = (3, 2, 1)
TERMS = len(Q_PARTS)
ROWS = TERMS * D
MROWS = 2
VW = D + 1
WIN_TILES = TILES + TPC - 1
SLAB = 2 * P
PAD = CLIP
PAIRS = TILES // 2
QUADS = TILES // 4
BLOCK_U = SLAB // CHUNKS
BLOCK_W = BLOCK_U - 1 + P
UG = BLOCK_U // 2


def project_heads(nc, x_T, w_in_T, b_in, pe_edges, q_stack, k_parts, v_wide):
    with ExitStack() as ctx:
        sb = lambda name, shape, dt=F32: ctx.enter_context(nc.sbuf_tensor(name, shape, dt))
        sem = lambda name: ctx.enter_context(nc.semaphore(name))
        weights = sb("in_weights", [P, KE, 3 * E])
        v_bias = sb("v_bias", [1, E])
        ones_row = sb("ones_row", [1, P])
        qk_bias = sb("qk_bias", [P, 4])
        edges = sb("edges", [P, 2])
        bias = sb("unit_bias", [P, 6])
        x_in = sb("x_in", [P, 2, KE, CH])
        exact = sb("exact", [P, 6, CH])
        rest = sb("rest", [P, 2, CH])
        part = sb("part", [P, 3, 6, CH], BF16)
        v_stage = sb("v_stage", [P, HEADS, TPC, VW])
        unit_ps = [ctx.enter_context(nc.psum_tensor(f"unit_ps{u}", [P, CH], F32)) for u in range(4)]
        value_ps = [ctx.enter_context(nc.psum_tensor(f"value_ps{u}", [P, 2, E], F32)) for u in range(2)]

        consts_in = sem("consts_in")
        x_loaded = [sem(f"x_loaded{i}") for i in range(2)]
        ones_set = sem("ones_set")
        bias_made = sem("bias_made")
        units_done = sem("units_done")
        values_done = sem("values_done")
        exact_done = sem("exact_done")
        hi_done = sem("hi_done")
        rest_done = sem("rest_done")
        mid_done = sem("mid_done")
        low_done = sem("low_done")
        v_staged = sem("v_staged")
        v_stored = sem("v_stored")
        parts_stored = [sem(f"parts_stored{v}") for v in range(6)]
        VARIANTS = ((0, 0), (1, 1), (2, 2), (2, 3), (3, 4), (3, 5))
        UNIT_READ = (1, 2, 4, 6)
        Q_STORES, K_STORES = TERMS, 3

        block = ctx.enter_context(nc.Block())

        @block.gpsimd
        def _(pool):
            with pool.Fori(0, CHUNKS // 2) as m:
                for par in range(2):
                    n = m * 2 + par
                    pool.wait_ge(values_done, m * 2 if par == 0 else m * 2)
                    pool.dma_start(x_in[:, par, :, :],
                                   x_T.rearrange("(k p) n -> p k n", p=P)[:, :, bass.ds(n * CH, CH)]
                                   ).then_inc(x_loaded[par], 16)

        @block.sync
        def _(sp):
            sp.dma_start(weights[:], w_in_T.rearrange("(k p) n -> p k n", p=P)).then_inc(consts_in, 16)
            sp.dma_start(qk_bias[:], b_in[0:2 * E].rearrange("(u p) -> p u", p=P),
                         allow_slow_non_contiguous=True).then_inc(consts_in, 16)
            sp.dma_start(edges[:], pe_edges.rearrange("e p -> p e"),
                         allow_slow_non_contiguous=True).then_inc(consts_in, 16)
            sp.dma_start(v_bias[:], b_in[2 * E:3 * E].rearrange("(a n) -> a n", a=1)).then_inc(consts_in, 16)
            with sp.Fori(0, CHUNKS) as n:
                col = n * CH
                for v, (unit, _) in enumerate(VARIANTS):
                    sp.wait_ge(low_done, n * 6 + v + 1)
                    heads = slice(GROUP * (unit % 2), GROUP * (unit % 2 + 1))
                    if unit < 2:
                        for t, which in enumerate(Q_PARTS):
                            sp.dma_start(q_stack[heads, t * D:(t + 1) * D, bass.ds(col, CH)],
                                         part[:, which, v, :]).then_inc(parts_stored[v], 16)
                    else:
                        side = col if v in (2, 4) else col + N
                        for which in range(3):
                            sp.dma_start(k_parts[heads, which * D:(which + 1) * D, bass.ds(side, CH)],
                                         part[:, which, v, :]).then_inc(parts_stored[v], 16)
                sp.wait_ge(v_staged, n + 2)
                for again in range(2):
                    sp.dma_start(v_wide.rearrange("h p (t e) -> p h t e", e=VW)
                                 [:, :, bass.ds(n * TPC + again * TILES, TPC), :],
                                 v_stage[:]).then_inc(v_stored, 16)
            for v in range(6):
                sp.wait_ge(parts_stored[v], 16 * CHUNKS * (Q_STORES if v < 2 else K_STORES))
            sp.wait_ge(v_stored, 32 * CHUNKS)

        @block.tensor
        def _(pe):
            pe.wait_ge(consts_in, 64)
            pe.wait_ge(ones_set, 2)
            with pe.Fori(0, CHUNKS // 2) as m:
                for par in range(2):
                    n = m * 2 + par
                    pe.wait_ge(x_loaded[par], m * 16 + 16)
                    for u in range(4):
                        pe.wait_ge(exact_done, n * 6 + UNIT_READ[u])
                        for k in range(KE):
                            mm = pe.matmul(unit_ps[u][:], weights[:, k, u * P:(u + 1) * P],
                                           x_in[:, par, k, :], start=k == 0, stop=k == KE - 1)
                        mm.then_inc(units_done, 1)
                    pe.wait_ge(v_staged, n + 1)
                    for t in range(TPC):
                        out = value_ps[t // 2][:, t % 2, :]
                        for k in range(KE):
                            pe.matmul(out, x_in[:, par, k, t * P:(t + 1) * P],
                                      weights[:, k, 2 * E:3 * E], start=k == 0, stop=False)
                        mm = pe.matmul(out, ones_row[:], v_bias[:], start=False, stop=True)
                    mm.then_inc(values_done, 1)

        @block.scalar
        def _(act):
            act.preload_act_table(ACT.Identity)
            act.sem_inc(exact_done, 6)
            act.sem_inc(v_staged, 1)
            act.wait_ge(bias_made, 1)
            act.wait_ge(ones_set, 2)
            with act.Fori(0, CHUNKS) as n:
                for v, (unit, b) in enumerate(VARIANTS):
                    act.wait_ge(units_done, n * 4 + unit + 1)
                    act.wait_ge(rest_done, n * 6 + v + 1)
                    act.activation(exact[:, v, :], unit_ps[unit][:], ACT.Identity,
                                   bias=bias[:, b:b + 1], scale=D ** -0.5 if unit < 2 else 1.0
                                   ).then_inc(exact_done, 1)
                    act.wait_ge(exact_done, n * 6 + v + 7)
                    act.wait_ge(parts_stored[v], n * (16 * (Q_STORES if v < 2 else K_STORES)))
                    act.activation(part[:, 0, v, :], exact[:, v, :], ACT.Identity).then_inc(hi_done, 1)
                act.wait_ge(values_done, n + 1)
                act.wait_ge(v_stored, n * 32)
                for half in range(2):
                    ins = act.activation(v_stage[:, :, 2 * half:2 * half + 2, 0:D],
                                         value_ps[half][:].rearrange("p t (h d) -> p h t d", d=D),
                                         ACT.Identity)
                ins.then_inc(v_staged, 1)

        @block.vector
        def _(dve):
            dve.memset(ones_row[:], 1.0).then_inc(ones_set, 1)
            dve.memset(v_stage[:], 1.0).then_inc(ones_set, 1)
            dve.sem_inc(rest_done, 6)
            dve.wait_ge(consts_in, 64)
            dve.tensor_scalar(bias[:, 0:2], qk_bias[:, 0:2], D ** -0.5, None, ALU.mult)
            for unit in range(2):
                for side in range(2):
                    ins = dve.tensor_tensor(bias[:, 2 + 2 * unit + side:3 + 2 * unit + side],
                                            qk_bias[:, 2 + unit:3 + unit], edges[:, 1 - side:2 - side],
                                            ALU.add)
            ins.then_inc(bias_made, 1)
            with dve.Fori(0, CHUNKS) as n:
                for v in range(6):
                    dve.wait_ge(hi_done, n * 6 + v + 1)
                    dve.tensor_tensor(rest[:, v % 2, :], exact[:, v, :], part[:, 0, v, :], ALU.subtract
                                      ).then_inc(rest_done, 1)
                    dve.wait_ge(rest_done, n * 6 + v + 7)
                    dve.tensor_copy(part[:, 1, v, :], rest[:, v % 2, :]).then_inc(mid_done, 1)
                    dve.wait_ge(mid_done, n * 6 + v + 1)
                    dve.tensor_tensor(part[:, 2, v, :], rest[:, v % 2, :], part[:, 1, v, :], ALU.subtract
                                      ).then_inc(low_done, 1)
def same(pool, out, in_, ones):
    return pool.tensor_tensor(out, in_, ones[:].to_broadcast(list(in_.shape)), ALU.mult)



def attend(nc, q_stack, k_parts, v_wide, rel_T, ident, part_sum, attn):
    NEXT_GEN = CHUNKS + 1
    LEAD = 12
    TOTAL = HEADS * CHUNKS
    MAX_GROUPS = TPC * (TILES // TPC)
    with ExitStack() as ctx:
        sb = lambda name, shape, dt=F32: ctx.enter_context(nc.sbuf_tensor(name, shape, dt))
        ps = lambda name, shape, dt=F32: ctx.enter_context(nc.psum_tensor(name, shape, dt))
        sem = lambda name: ctx.enter_context(nc.semaphore(name))
        keys = [sb(f"keys{i}", [ROWS + MROWS, WIN_TILES * P], BF16) for i in range(2)]
        queries = [sb(f"queries{i}", [ROWS + MROWS, CH], BF16) for i in range(2)]
        max_queries = [sb(f"max_queries{i}", [ROWS, CH], BF16) for i in range(2)]
        values = [sb(f"values{i}", [P, TILES, VW]) for i in range(2)]
        head_q = sb("head_q", [ROWS, 2, N + SLAB], BF16)
        near_bias = sb("near_bias", [P, 2, TILES + 2, SLAB])
        near_window = [sb(f"near_window{i}", [P, TPC + 2, SLAB + 2 * PAD], BF16) for i in range(2)]
        block_q = [sb(f"block_q{i}", [ROWS, TILES, BLOCK_U], BF16) for i in range(2)]
        block_table = [sb(f"block_table{i}", [ROWS, BLOCK_W], BF16) for i in range(2)]
        probs = [sb(f"probs{i}", [P, 2, CH]) for i in range(4)]
        table = sb("table", [ROWS, CHUNKS, BLOCK_W], BF16)
        table_raw = sb("table_raw", [D, 2 * CLIP + 1])
        R_COLS = 3 * P - 1 - PAD
        L_COLS = 3 * P - 1 - 3 * PAD
        ext = sb("table_ext", [D, R_COLS + L_COLS])
        ext_rest = sb("table_rest", [D, R_COLS + L_COLS])
        ext_part = sb("table_part", [D, 3, R_COLS + L_COLS], BF16)
        ext_rows = sb("table_rows", [ROWS, R_COLS + L_COLS], BF16)
        ident_f = sb("ident_f", [P, P])
        ident_b = sb("ident_b", [P, P], BF16)
        one_f = sb("one_f", [P, 1, 1])
        one_b = sb("one_b", [ROWS, 1], BF16)
        sum_sel = sb("sum_sel", [P, VW])
        group_max = [sb(f"group_max{i}", [P, MAX_GROUPS]) for i in range(2)]
        row_max = sb("row_max", [P, TPC])
        max_parts = sb("max_parts", [P, TPC, MROWS], BF16)
        out_copy = sb("out_copy", [P, CH])
        inv_sum = sb("inv_sum", [P, TPC, 1])

        scores = [ps(f"scores{i}", [P, 2, CH]) for i in range(2)]
        out_ps = ps("out_ps", [P, CH])
        max_ps = [ps(f"max_ps{i}", [P, CH]) for i in range(2)]
        small_ps = ps("small_ps", [P, CH])

        consts_in = sem("consts_in2")
        table_cut = sem("table_cut")
        table_rows_in = sem("table_rows_in")
        table_ready = sem("table_ready")
        cleared = sem("cleared")
        ident_ready = sem("ident_ready")
        PIECES = ((0, 8, 3), (8, 16, 7), (16, 24, 11), (24, WIN_TILES, 15))
        keys_in = [[sem(f"keys_in{i}_{j}") for j in range(4)] for i in range(2)]
        queries_in = [sem(f"queries_in{i}") for i in range(2)]
        max_queries_in = [sem(f"max_queries_in{i}") for i in range(2)]
        values_in = [sem(f"values_in{i}") for i in range(2)]
        head_q_in = [sem(f"head_q_in{i}") for i in range(2)]
        block_ready = sem("block_ready")
        bias_ready = sem("bias_ready")
        bias_read = sem("bias_read")
        window_ready = sem("window_ready")
        max_ready = sem("max_ready")
        max_read = sem("max_read")
        max_step = sem("max_step")
        max_cut = sem("max_cut")
        max_rows = sem("max_rows")
        max_placed = sem("max_placed")
        scores_ready = sem("scores_ready")
        near_added = sem("near_added")
        exp_done = sem("exp_done")
        pv_done = sem("pv_done")
        out_copied = sem("out_copied")
        out_summed = sem("out_summed")
        norm_step = sem("norm_step")
        normed = sem("normed")

        block = ctx.enter_context(nc.Block())

        def place(n):
            return n // CHUNKS, n % CHUNKS

        @block.sync
        def _(sp):
            sp.dma_start(table_raw[:], rel_T).then_inc(consts_in, 16)
            sp.dma_start(ident_f[:], ident).then_inc(consts_in, 16)
            sp.dma_start(sum_sel[:], part_sum).then_inc(consts_in, 16)

            def load_keys(n, par, j):
                h, c = place(n)
                a, b, _ = PIECES[j]
                row = 0
                for run in K_RUNS:
                    rows = run * D
                    sp.dma_start(keys[par][row:row + rows, a * P:b * P],
                                 k_parts[bass.ds(h, 1), 0:rows, bass.ds(c * CH + a * P, (b - a) * P)]
                                 ).then_inc(keys_in[par][j], 16)
                    row += rows

            def load_queries(n, par):
                h, c = place(n)
                sp.dma_start(queries[par][0:ROWS, :], q_stack[bass.ds(h, 1), :, bass.ds(c * CH, CH)]
                             ).then_inc(queries_in[par], 16)

            def load_max_queries(n, par):
                h, c = place(n)
                sp.dma_start(max_queries[par][:], q_stack[bass.ds(h, 1), :, bass.ds(c * CH, CH)]
                             ).then_inc(max_queries_in[par], 16)

            def load_values(n, par):
                h, c = place(n)
                sp.dma_start(values[par][:], v_wide[bass.ds(h, 1), :, bass.ds(c * (TPC * VW), TILES * VW)]
                             ).then_inc(values_in[par], 16)

            for par in range(2):
                load_queries(par, par)
                load_max_queries(par, par)
                for j in range(4):
                    load_keys(par, par, j)
                load_values(par, par)
            sp.wait_ge(table_cut, 3)
            row = 0
            for run in K_RUNS:
                for which in range(run):
                    sp.dma_start(ext_rows[row:row + D, :], ext_part[:, which, :]
                                 ).then_inc(table_rows_in, 16)
                    row += D
            with sp.Fori(0, TOTAL // 2 - 1) as m:
                for par in range(2):
                    n = m * 2 + par
                    sp.wait_ge(max_ready, (n + 1) * MAX_GROUPS)
                    load_max_queries(n + 2, par)
                    for j in range(4):
                        sp.wait_ge(scores_ready, n * PAIRS + PIECES[j][2] + 1)
                        load_keys(n + 2, par, j)
                    load_queries(n + 2, par)
                    sp.wait_ge(pv_done, n * QUADS + QUADS + 2)
                    load_values(n + 2, par)

        @block.gpsimd
        def _(pool):
            for i in range(2):
                pool.memset(near_window[i][:], 0.0).then_inc(cleared, 1)
                pool.memset(near_bias[:, i, 0, :], 0.0).then_inc(cleared, 1)
                pool.memset(near_bias[:, i, TILES + 1, :], 0.0).then_inc(cleared, 1)
            pool.memset(head_q[:, :, 0:PAD], 0.0).then_inc(cleared, 1)
            pool.memset(head_q[:, :, PAD + N:], 0.0).then_inc(cleared, 1)
            pool.memset(one_f[:], 1.0).then_inc(cleared, 1)
            pool.memset(one_b[:], 1.0).then_inc(cleared, 1)
            pool.wait_ge(cleared, 10)

            def load_head_q(h, par):
                pool.dma_start(head_q[:, par, PAD:PAD + N], q_stack[bass.ds(h, 1), :, :]
                               ).then_inc(head_q_in[par], 16)

            def copy_window(h, c, par):
                n = h * CHUNKS + c
                if c == 0:
                    pool.wait_ge(bias_read, (h + 1) * (2 * CHUNKS))
                pool.wait_ge(max_cut, n + 1)
                same(pool, near_window[c % 2][:, :, PAD:PAD + SLAB],
                     near_bias[:, par, TPC * c:TPC * c + TPC + 2, :], one_f).then_inc(window_ready, 1)

            def copy_block(h, b, par):
                e = h * CHUNKS + b
                if b == 0:
                    pool.wait_ge(head_q_in[par], h // 2 * 16 + 16)
                if not isinstance(e, int) or e >= 2:
                    pool.wait_ge(bias_ready, e * 2 - 2)
                first = b * BLOCK_U
                same(pool, block_table[b % 2][:], table[:, b, :], one_b)
                src = head_q[:, par, first:first + N].rearrange("r (j u) -> r j u", u=P)
                pool.tensor_copy(block_q[b % 2][:], src[:, :, 0:BLOCK_U]).then_inc(block_ready, 1)

            pool.wait_ge(table_ready, 1)
            for h in range(2):
                load_head_q(h, h)
            for b in range(CHUNKS):
                copy_block(0, b, 0)
            copy_block(1, 0, 1)
            copy_window(0, 0, 0)
            copy_window(0, 1, 0)
            copy_block(1, 1, 1)

            def during(h, c, par, block, window):
                later = (c + 2) // CHUNKS
                if window:
                    copy_window(h + later, (c + 2) % CHUNKS, (par + later) % 2)
                if block:
                    copy_block(h + later + 1, (c + 2) % CHUNKS, (par + later + 1) % 2)

            with pool.Fori(0, HEADS // 2 - 1) as m:
                for par in range(2):
                    h = m * 2 + par
                    pool.wait_ge(block_ready, h * CHUNKS + CHUNKS)
                    load_head_q(h + 2, par)
                    for c in range(CHUNKS):
                        during(h, c, par, True, True)
            for c in range(CHUNKS):
                during(HEADS - 2, c, 0, c < CHUNKS - 2, True)
            for c in range(CHUNKS - 2):
                during(HEADS - 1, c, 1, False, True)

        @block.tensor
        def _(pe):
            def max_group(n, par, k):
                t, g = k % TPC, k // TPC
                if k == 0:
                    pe.wait_ge(window_ready, n + 1)
                    pe.wait_ge(max_queries_in[par], (n // 2) * 16 + 16)
                if t == 0:
                    last_tile = TPC * g + 2 * TPC - 2
                    for j, (a, b, _) in enumerate(PIECES):
                        if a <= last_tile < b or (g == 0 and j == 0):
                            pe.wait_ge(keys_in[par][j], (n // 2) * 48 + 48)
                pe.wait_ge(max_read, n * MAX_GROUPS + k + 1)
                bank = max_ps[k % 2]
                near = {0: [(0, t + 1, P), (1, t + 2, 0)],
                        TILES // TPC - 1: [(TPC - 1, t, 2 * P)]}.get(g, [])
                mm = pe.matmul(bank[:], max_queries[par][:, t * P:(t + 1) * P],
                               keys[par][0:ROWS, (t + TPC * g) * P:(t + TPC * (g + 1)) * P],
                               start=True, stop=not near)
                for i, (pos, slab, u) in enumerate(near):
                    mm = pe.matmul(bank[:, pos * P:(pos + 1) * P], near_window[par][:, slab, u:u + P],
                                   ident_b[:], start=False, stop=i == len(near) - 1)
                mm.then_inc(max_ready, 1)

            def max_to_rows(n, par):
                pe.wait_ge(max_cut, n + 3)
                for t in range(TPC):
                    mm = pe.matmul(small_ps[ROWS:ROWS + MROWS, t * P:(t + 1) * P], max_parts[:, t, :],
                                   ident_b[:], start=True, stop=True)
                mm.then_inc(max_rows, 1)

            def score(n, par, c):
                s = c // 2
                if c == 0:
                    pe.wait_ge(queries_in[par], (n // 2) * 16 + 16)
                    pe.wait_ge(max_placed, n + 1)
                if c % 2 == 0:
                    pe.wait_ge(exp_done, n * PAIRS + s + 1)
                cut = min(c + 1, TPC) * P
                out = scores[s % 2][:, c % 2, :]
                mm = pe.matmul(out[:, 0:cut], keys[par][:, c * P:(c + 1) * P],
                               queries[par][:, 0:cut], start=True, stop=True)
                if cut < CH:
                    mm = pe.matmul(out[:, cut:CH], keys[par][:, (c + TILES) * P:(c + TILES + 1) * P],
                                   queries[par][:, cut:CH], start=True, stop=True)
                if c % 2 == 1:
                    mm.then_inc(scores_ready, 1)

            def pv_quad(n, par, q):
                if q == 0:
                    pe.wait_ge(values_in[par], (n // 2) * 16 + 16)
                    pe.wait_ge(out_copied, n)
                pe.wait_ge(exp_done, n * PAIRS + 2 * q + 4)
                for i in range(4):
                    mm = pe.matmul(out_ps[32 * i:32 * i + VW, :], values[par][:, 4 * q + i, :],
                                   probs[(2 * q + i // 2) % 4][:, i % 2, :],
                                   start=q == 0, stop=q == QUADS - 1, skip_group_check=True)
                mm.then_inc(pv_done, 1)

            def make_bias(e, par, half):
                if half == 0:
                    pe.wait_ge(block_ready, e + 1)
                pe.wait_ge(bias_read, e * 2 + half)
                for i in range(UG):
                    u = half * UG + i
                    mm = pe.matmul(small_ps[:, i * TILES:(i + 1) * TILES],
                                   block_table[par][:, BLOCK_U - 1 - u:BLOCK_U - 1 - u + P],
                                   block_q[par][:, :, u], start=True, stop=True)
                mm.then_inc(bias_ready, 1)

            def sum_quadrants(n, par):
                pe.wait_ge(out_copied, n + 1)
                for t in range(TPC):
                    mm = pe.matmul(small_ps[:, t * VW:(t + 1) * VW], out_copy[:, t * P:(t + 1) * P],
                                   sum_sel[:], start=True, stop=True)
                mm.then_inc(out_summed, 1)

            def max_slot(n, par, slot, ahead):
                k = LEAD + slot
                if k < MAX_GROUPS and ahead >= 1:
                    max_group(n + 1, 1 - par, k)
                if k >= MAX_GROUPS and ahead >= 2:
                    max_group(n + 2, par, k - MAX_GROUPS)

            def chunk(n, par, bias, ahead):
                for turn in range(QUADS):
                    nxt = turn >= QUADS - 2
                    if turn == QUADS - 2 and ahead:
                        if bias:
                            pe.wait_ge(bias_read, (n + NEXT_GEN) * 2 + 2)
                        else:
                            pe.wait_ge(normed, n)
                        max_to_rows(n + 1, 1 - par)
                    pv_quad(n, par, turn)
                    for i in range(4):
                        max_slot(n, par, 4 * turn + i, ahead)
                        for c in ((0, 1), (2,), (3,), ())[i]:
                            if nxt and ahead:
                                score(n + 1, 1 - par, 4 * (turn - QUADS + 2) + c)
                            elif not nxt:
                                score(n, par, 4 * (turn + 2) + c)
                    if bias and turn < 2:
                        if turn == 0:
                            pe.wait_ge(normed, n)
                        make_bias(n + NEXT_GEN, (par + NEXT_GEN) % 2, turn)
                if ahead:
                    pe.wait_ge(max_placed, n + 2)
                sum_quadrants(n, par)

            pe.wait_ge(consts_in, 48)
            pe.wait_ge(cleared, 10)
            pe.wait_ge(ident_ready, 4)
            for e in range(NEXT_GEN):
                for half in range(2):
                    make_bias(e, e % 2, half)
            for k in range(MAX_GROUPS + LEAD):
                max_group(k // MAX_GROUPS, k // MAX_GROUPS, k % MAX_GROUPS)
            pe.wait_ge(bias_read, 2 * NEXT_GEN)
            max_to_rows(0, 0)
            for c in range(8):
                score(0, 0, c)
            last_bias = (TOTAL - NEXT_GEN) // 2
            with pe.Fori(0, last_bias) as m:
                for par in range(2):
                    chunk(m * 2 + par, par, True, 2)
            chunk(2 * last_bias, 0, True, 2)
            chunk(2 * last_bias + 1, 1, False, 2)
            with pe.Fori(last_bias + 1, TOTAL // 2 - 1) as m:
                for par in range(2):
                    chunk(m * 2 + par, par, False, 2)
            chunk(TOTAL - 2, 0, False, 1)
            chunk(TOTAL - 1, 1, False, 0)

        @block.scalar
        def _(act):
            act.preload_act_table(ACT.Exp)
            act.sem_inc(exp_done, 2)

            def keep_bias(block_no, half):
                h, b = place(block_no)
                act.wait_ge(bias_ready, block_no * 2 + half + 1)
                act.activation(near_bias[:, bass.ds(h % 2, 1), 1:TILES + 1, bass.ds(b * BLOCK_U + half * UG, UG)],
                               small_ps[:].rearrange("p (a u j) -> p a j u", a=1, u=UG), ACT.Copy
                               ).then_inc(bias_read, 1)

            def exp_pair(n, s):
                if s in (0, 1, 2, PAIRS - 1):
                    act.wait_ge(near_added, n * 4 + {0: 1, 1: 2, 2: 3, PAIRS - 1: 4}[s])
                act.wait_ge(scores_ready, n * PAIRS + s + 1)
                act.wait_ge(pv_done, n * QUADS + s // 2 + 1)
                act.activation(probs[s % 4][:], scores[s % 2][:], ACT.Exp).then_inc(exp_done, 1)

            def place_max(n, par):
                act.wait_ge(max_rows, n + 1)
                act.activation(queries[par][ROWS:ROWS + MROWS, :], small_ps[ROWS:ROWS + MROWS, :], ACT.Copy
                               ).then_inc(max_placed, 1)

            def chunk(n, par, bias, more):
                for s in range(4, PAIRS):
                    if s == PAIRS - 1 and more:
                        place_max(n + 1, 1 - par)
                    exp_pair(n, s)
                    if bias and s in (5, 7):
                        if s == 5:
                            act.wait_ge(window_ready, n + 1)
                        keep_bias(n + NEXT_GEN, s // 7)
                for s in range(4):
                    if more:
                        exp_pair(n + 1, s)
                    if s == 1:
                        act.wait_ge(pv_done, n * QUADS + QUADS + 2)
                        act.wait_ge(out_summed, n)
                        act.activation(out_copy[:], out_ps[:], ACT.Copy).then_inc(out_copied, 1)

            act.wait_ge(cleared, 10)
            for e in range(NEXT_GEN):
                for half in range(2):
                    keep_bias(e, half)
            place_max(0, 0)
            for s in range(4):
                exp_pair(0, s)
            last_bias = (TOTAL - NEXT_GEN) // 2
            with act.Fori(0, last_bias) as m:
                for par in range(2):
                    chunk(m * 2 + par, par, True, True)
            chunk(2 * last_bias, 0, True, True)
            chunk(2 * last_bias + 1, 1, False, True)
            with act.Fori(last_bias + 1, TOTAL // 2 - 1) as m:
                for par in range(2):
                    chunk(m * 2 + par, par, False, True)
            chunk(TOTAL - 2, 0, False, True)
            chunk(TOTAL - 1, 1, False, False)

        @block.vector
        def _(dve):
            dve.sem_inc(max_read, 2)
            dve.sem_inc(max_cut, 2)
            dve.sem_inc(pv_done, 2)
            dve.memset(out_ps[:], 0.0).then_inc(ident_ready, 1)
            for i in range(2):
                dve.memset(keys[i][ROWS:ROWS + MROWS, :], 1.0).then_inc(ident_ready, 1)
            dve.wait_ge(consts_in, 48)
            dve.tensor_copy(ident_b[:], ident_f[:]).then_inc(ident_ready, 1)
            spans = ((0, PAD, 0, None), (PAD, 2 * CLIP - 1, 1, None), (PAD + 2 * CLIP - 1, P, 2 * CLIP, None),
                     (R_COLS, P, 0, None), (R_COLS + P, CLIP - 1, 1, None))
            for start, width, first, _ in spans:
                if first in (0, 2 * CLIP):
                    src = table_raw[:, first:first + 1].to_broadcast([D, width])
                else:
                    src = table_raw[:, first:first + width]
                ins = dve.tensor_copy(ext[:, start:start + width], src)
            ins.then_inc(max_step, 1)
            dve.wait_ge(max_step, 1)
            dve.tensor_scalar(ext[:, 0:R_COLS], ext[:, 0:R_COLS], table_raw[:, 2 * CLIP:2 * CLIP + 1], None,
                              ALU.subtract)
            dve.tensor_scalar(ext[:, R_COLS:], ext[:, R_COLS:], table_raw[:, 0:1], None,
                              ALU.subtract).then_inc(max_step, 1)
            dve.wait_ge(max_step, 2)
            dve.tensor_copy(ext_part[:, 0, :], ext[:]).then_inc(table_cut, 1)
            dve.wait_ge(table_cut, 1)
            dve.tensor_tensor(ext_rest[:], ext[:], ext_part[:, 0, :], ALU.subtract).then_inc(max_step, 1)
            dve.wait_ge(max_step, 3)
            dve.tensor_copy(ext_part[:, 1, :], ext_rest[:]).then_inc(table_cut, 1)
            dve.wait_ge(table_cut, 2)
            dve.tensor_tensor(ext_part[:, 2, :], ext_rest[:], ext_part[:, 1, :], ALU.subtract
                              ).then_inc(table_cut, 1)
            dve.wait_ge(table_rows_in, 16 * TERMS)
            for b in range(CHUNKS):
                if (b + 1) * BLOCK_U <= PAD + P:
                    first = P - 1 + PAD - b * BLOCK_U - (BLOCK_U - 1)
                else:
                    first = R_COLS + SLAB - 1 - b * BLOCK_U - (BLOCK_U - 1)
                ins = dve.tensor_copy(table[:, b, :], ext_rows[:, first:first + BLOCK_W])
            ins.then_inc(table_ready, 1)
            SETUP = 3

            def near_add(n, s):
                h, c = place(n)
                spans = {0: [(0, 0, 192, 1, 64), (1, 0, 320, 2, 0)],
                         1: [(0, 192, 448, 3, 0), (1, 320, 512, 4, 0)],
                         2: [(0, 448, 512, 5, 0)],
                         15: [(1, 0, 64, 0, 192)]}[s]
                if s == 0:
                    spans = [(0, 0, 192, 1, 64), (1, 64, 320, 2, 0)]
                dve.wait_ge(scores_ready, n * PAIRS + s + 1)
                for tile, a, b, slab, u in spans:
                    part = scores[s % 2][:, tile, a:b]
                    ins = dve.tensor_tensor(part, part,
                                            near_bias[:, bass.ds(h % 2, 1), bass.ds(c * TPC + slab, 1), u:u + b - a],
                                            ALU.add)
                ins.then_inc(near_added, 1)

            def find_max(n, par):
                dve.wait_ge(max_read, n * MAX_GROUPS + MAX_GROUPS + 2)
                dve.tensor_reduce(row_max[:], group_max[par][:].rearrange("p (g t) -> p t g", t=TPC), AX.X,
                                  ALU.max).then_inc(max_step, 1)

            def cut_high(n, par):
                dve.wait_ge(max_step, n * 2 + SETUP + 1)
                dve.wait_ge(max_rows, n)
                dve.tensor_scalar(max_parts[:, :, 0], row_max[:], -1.0, None, ALU.mult).then_inc(max_step, 1)

            def cut_low(n, par):
                dve.wait_ge(max_step, n * 2 + SETUP + 2)
                dve.scalar_tensor_tensor(out=max_parts[:, :, 1], in0=row_max[:], scalar=-1.0,
                                         in1=max_parts[:, :, 0], op0=ALU.mult, op1=ALU.subtract
                                         ).then_inc(max_cut, 1)

            def bank_max(n, par, k):
                dve.wait_ge(max_ready, n * MAX_GROUPS + k + 1)
                dve.tensor_reduce(group_max[par][:, k:k + 1], max_ps[k % 2][:], AX.X, ALU.max
                                  ).then_inc(max_read, 1)

            def finish(n):
                h, c = place(n)
                dve.wait_ge(out_summed, n + 1)
                summed = small_ps[:, 0:TPC * VW].rearrange("p (t e) -> p t e", e=VW)
                dve.reciprocal(inv_sum[:], summed[:, :, D:VW]).then_inc(norm_step, 1)
                dve.wait_ge(norm_step, n + 1)
                dve.tensor_tensor(attn[:, bass.ds(c * TPC, TPC), bass.ds(h * D, D)], summed[:, :, 0:D],
                                  inv_sum[:].to_broadcast([P, TPC, D]), ALU.mult).then_inc(normed, 1)

            def chunk(n, par, ahead):
                for slot in range(MAX_GROUPS):
                    k = LEAD + slot
                    if slot == 4 * (QUADS - 2) - 1:
                        near_add(n, PAIRS - 1)
                    if ahead:
                        at = slot - 4 * (QUADS - 2)
                        if at in (1, 3, 5):
                            near_add(n + 1, at // 2)
                    if k < MAX_GROUPS and ahead >= 1:
                        bank_max(n + 1, 1 - par, k)
                    if k >= MAX_GROUPS and ahead >= 2:
                        bank_max(n + 2, par, k - MAX_GROUPS)
                    if ahead >= 1 and MAX_GROUPS - 1 <= k <= MAX_GROUPS + 1:
                        (find_max, cut_high, cut_low)[k - MAX_GROUPS + 1](n + 1, 1 - par)
                finish(n)

            for k in range(MAX_GROUPS):
                bank_max(0, 0, k)
            find_max(0, 0)
            cut_high(0, 0)
            cut_low(0, 0)
            for k in range(LEAD):
                bank_max(1, 1, k)
            for s in range(3):
                near_add(0, s)
            with dve.Fori(0, TOTAL // 2 - 1) as m:
                for par in range(2):
                    chunk(m * 2 + par, par, 2)
            chunk(TOTAL - 2, 0, 1)
            chunk(TOTAL - 1, 1, 0)


def layernorm_params(dve, pool, stats, mean, rstd, scratch, expo, step, first):
    tiles = stats.shape[1]
    if dve is not None:
        a, b = stats[:, :, 1], stats[:, :, 4]
        dve.tensor_tensor(mean, a, b, ALU.add).then_inc(step, 1)
        dve.tensor_tensor(scratch, a, b, ALU.subtract).then_inc(step, 1)
        dve.wait_ge(step, first + 2)
        dve.tensor_scalar(mean, mean, 0.5, None, ALU.mult).then_inc(step, 1)
        dve.tensor_tensor(scratch, scratch, scratch, ALU.mult).then_inc(step, 1)
        dve.tensor_tensor(rstd, stats[:, :, 2], stats[:, :, 5], ALU.add).then_inc(step, 1)
        dve.wait_ge(step, first + 5)
        dve.tensor_scalar(scratch, scratch, 0.25, LN_EPS, ALU.mult, ALU.add).then_inc(step, 1)
        dve.wait_ge(step, first + 6)
        dve.scalar_tensor_tensor(out=rstd, in0=rstd, scalar=1.0 / E, in1=scratch, op0=ALU.mult,
                                 op1=ALU.add).then_inc(step, 1)
    if pool is not None:
        pool.wait_ge(step, first + 7)
        pool.tensor_tensor(rstd, rstd, expo[:, 0:tiles], ALU.pow).then_inc(step, 1)
    return first + 8




def layernorm_params(dve, pool, stats, mean, rstd, scratch, expo, step, first):
    tiles = stats.shape[1]
    if dve is not None:
        a, b = stats[:, :, 1], stats[:, :, 4]
        dve.tensor_tensor(mean, a, b, ALU.add).then_inc(step, 1)
        dve.tensor_tensor(scratch, a, b, ALU.subtract).then_inc(step, 1)
        dve.wait_ge(step, first + 2)
        dve.tensor_scalar(mean, mean, 0.5, None, ALU.mult).then_inc(step, 1)
        dve.tensor_tensor(scratch, scratch, scratch, ALU.mult).then_inc(step, 1)
        dve.tensor_tensor(rstd, stats[:, :, 2], stats[:, :, 5], ALU.add).then_inc(step, 1)
        dve.wait_ge(step, first + 5)
        dve.tensor_scalar(scratch, scratch, 0.25, LN_EPS, ALU.mult, ALU.add).then_inc(step, 1)
        dve.wait_ge(step, first + 6)
        dve.scalar_tensor_tensor(out=rstd, in0=rstd, scalar=1.0 / E, in1=scratch, op0=ALU.mult,
                                 op1=ALU.add).then_inc(step, 1)
    if pool is not None:
        pool.wait_ge(step, first + 7)
        pool.tensor_tensor(rstd, rstd, expo[:, 0:tiles], ALU.pow).then_inc(step, 1)
    return first + 8


def join_heads(nc, x, w_out_T, b_out, ident, tokens, first_norm):
    with ExitStack() as ctx:
        sb = lambda name, shape, dt=F32: ctx.enter_context(nc.sbuf_tensor(name, shape, dt))
        sem = lambda name: ctx.enter_context(nc.semaphore(name))
        weights = sb("out_weights", [P, KE, E])
        bias = sb("out_bias", [1, E])
        ones_row = sb("join_ones", [1, P])
        ident_f = sb("join_ident", [P, P])
        tile_in = sb("join_tile", [P, 2, E])
        tile_T = sb("join_tile_T", [P, 2, E])
        x_rows = sb("x_rows", [P, TILES, E])
        stats = sb("join_stats", [P, TILES, 6])
        mean, rstd, scratch, expo = (sb(f"join_{n}", [P, TILES]) for n in ("mean", "rstd", "scratch", "expo"))
        turned = [ctx.enter_context(nc.psum_tensor(f"join_turned{i}", [P, CH], F32)) for i in range(2)]
        joined = [ctx.enter_context(nc.psum_tensor(f"join_joined{i}", [P, CH], F32)) for i in range(2)]
        consts_in = sem("join_consts")
        ones_set = sem("join_ones_set")
        x_in = sem("join_x_in")
        picked = sem("picked")
        tile_turned = sem("tile_turned")
        tile_kept = sem("tile_kept")
        tile_joined = sem("tile_joined")
        summed = sem("summed")
        counted = sem("counted")
        step = sem("join_step")
        normed = sem("join_normed")
        copied = sem("join_copied")
        block = ctx.enter_context(nc.Block())

        @block.sync
        def _(sp):
            sp.dma_start(weights[:], w_out_T.rearrange("(k p) n -> p k n", p=P)).then_inc(consts_in, 16)
            sp.dma_start(bias[:], b_out.rearrange("(a n) -> a n", a=1)).then_inc(consts_in, 16)
            sp.dma_start(ident_f[:], ident).then_inc(consts_in, 16)
            sp.dma_start(x_rows[:], x.rearrange("(t p) e -> p t e", p=P)).then_inc(x_in, 16)
            sp.wait_ge(normed, TILES)
            sp.dma_start(first_norm, tokens[:]).then_inc(copied, 16)
            sp.wait_ge(copied, 16)

        @block.gpsimd
        def _(pool):
            pool.memset(expo[:], -0.5).then_inc(ones_set, 1)
            pool.sem_inc(tile_turned, 2)
            with pool.Fori(0, TILES // 2) as m:
                for par in range(2):
                    t = m * 2 + par
                    pool.wait_ge(tile_turned, t + 1)
                    pool.tensor_copy(tile_in[:, par, :], tokens[:, bass.ds(t, 1), :]).then_inc(picked, 1)
            pool.wait_ge(ones_set, 2)
            layernorm_params(None, pool, stats, mean[:], rstd[:], scratch[:], expo, step, 0)

        @block.tensor
        def _(pe):
            pe.wait_ge(consts_in, 48)
            pe.wait_ge(ones_set, 2)
            with pe.Fori(0, TILES // 2) as m:
                for par in range(2):
                    t = m * 2 + par
                    pe.wait_ge(picked, t + 1)
                    pe.wait_ge(tile_kept, t + 1)
                    for k in range(KE):
                        mm = pe.transpose(turned[par][:, k * P:(k + 1) * P],
                                          tile_in[:, par, k * P:(k + 1) * P], ident_f[:])
                    mm.then_inc(tile_turned, 1)
                    pe.wait_ge(tile_kept, t + 3)
                    pe.wait_ge(summed, t + 1)
                    for k in range(KE):
                        pe.matmul(joined[par][:, 0:E], tile_T[:, par, k * P:(k + 1) * P],
                                  weights[:, k, :], start=k == 0, stop=False)
                    pe.matmul(joined[par][:, 0:E], ones_row[:], bias[:], start=False, stop=True
                              ).then_inc(tile_joined, 1)

        @block.scalar
        def _(act):
            act.preload_act_table(ACT.Exp)
            act.sem_inc(tile_kept, 2)
            with act.Fori(0, TILES // 2) as m:
                for par in range(2):
                    t = m * 2 + par
                    act.wait_ge(tile_turned, t + 3)
                    act.wait_ge(summed, t + 1)
                    act.activation(tile_T[:, par, :], turned[par][:, 0:E], ACT.Copy).then_inc(tile_kept, 1)

        @block.vector
        def _(dve):
            dve.memset(ones_row[:], 1.0).then_inc(ones_set, 1)
            dve.sem_inc(summed, 2)
            dve.wait_ge(x_in, 16)
            with dve.Fori(0, TILES // 2) as m:
                for par in range(2):
                    t = m * 2 + par
                    dve.wait_ge(tile_joined, t + 1)
                    tile = tokens[:, bass.ds(t, 1), :]
                    dve.tensor_tensor(tile, joined[par][:, 0:E], x_rows[:, bass.ds(t, 1), :], ALU.add
                                      ).then_inc(summed, 1)
                    dve.wait_ge(summed, t + 3)
                    dve.bn_stats(stats[:, bass.ds(t, 1), :], tile).then_inc(counted, 1)
            dve.wait_ge(counted, TILES)
            end = layernorm_params(dve, None, stats, mean[:], rstd[:], scratch[:], expo, step, 0)
            dve.wait_ge(step, end)
            normalise(dve, tokens, mean, rstd, normed)


def normalise(dve, tokens, mean, rstd, normed):
    with dve.Fori(0, TILES) as t:
        tile = tokens[:, bass.ds(t, 1), :]
        dve.tensor_scalar(tile, tile, mean[:, bass.ds(t, 1)], rstd[:, bass.ds(t, 1)],
                          ALU.subtract, ALU.mult).then_inc(normed, 1)


DEPTH = 2
LHEADS = 8
LD = 64
INNER = LHEADS * LD
KI = INNER // P
HID = 682
HT = -(-HID // P)
HTAIL = HID - (HT - 1) * P
RING = 4
BATCH = 4
BATCHES = TILES // BATCH
QK_SCALE = 8.0


def local_layers(nc, w_qkv, qk_rows, w_o, ln_gb, w_1, b_1, w_2, b_2, rotary, masks, ident, tokens, first_norm, out):
    with ExitStack() as ctx:
        sb = lambda name, shape, dt=F32: ctx.enter_context(nc.sbuf_tensor(name, shape, dt))
        sem = lambda name: ctx.enter_context(nc.semaphore(name))
        bank = [ctx.enter_context(nc.psum_tensor(f"bank{i}", [P, CH], F32)) for i in range(4, 8)]
        quad = ctx.enter_context(nc.psum_tensor("quad", [P, 4, CH], F32))
        wqkv = sb("wqkv", [P, KE, 3 * INNER])
        wo = sb("wo", [P, KI, E])
        w1 = sb("w1", [P, KE, 2 * HID])
        w2 = sb("w2", [P, HT, E])
        b2 = sb("b2", [1, E])
        ones_row = sb("layer_ones", [1, P])
        b1 = sb("b1", [P, 2, HT])
        gb = sb("ln_gb", [P, 2, KE])
        qk_row = sb("qk_row", [P, 4 * LD])
        rot = sb("rot", [P, TILES, 4 * LD])
        mask = sb("mask", [P, 2, SLAB])
        ident_f = sb("layer_ident", [P, P])
        tile_in = [sb(f"win_tile{i}", [P, E]) for i in range(2)]
        hT_a = [sb(f"hT_a{i}", [P, P]) for i in range(2)]
        hT_b = [sb(f"hT_b{i}", [P, P + 1]) for i in range(2)]
        v_kept = [sb(f"v_kept{i}", [P, INNER]) for i in range(RING)]
        k_T = [sb(f"k_T{i}", [P, KI, P]) for i in range(2)]
        q_T = sb("q_T", [P, KI, P])
        squares = sb("squares", [P, 2 * LHEADS, LD])
        norm = sb("norm", [P, 2 * LHEADS, 1])
        turn = sb("turn", [P, 4 * LD])
        rot_a = sb("rot_a", [P, 2 * LHEADS, LD])
        rot_b = sb("rot_b", [P, 2 * LHEADS, LD])
        sim = sb("sim", [P, LHEADS, SLAB])
        prob = sb("prob", [P, LHEADS, SLAB])
        top = sb("top", [P, LHEADS])
        shift = sb("shift", [P, LHEADS])
        total = sb("total", [P, LHEADS, 1])
        inv_total = sb("inv_total", [P, LHEADS, 1])
        prob_T = sb("prob_T", [P, 2 * LHEADS, P])
        o_tok = sb("o_tok", [P, LHEADS, LD])
        o_T = sb("o_T", [P, KI, P])
        half_in = sb("half_in", [P, BATCH, P])
        half_T = sb("half_T", [P, BATCH * P + 1])
        h_tok = sb("h_tok", [P, BATCH, E])
        h_T = sb("h_T", [P, KE, CH])
        gate = sb("gate", [P, 2, CH])
        hidden = sb("hidden", [P, HT, CH])
        stats = sb("layer_stats", [P, BATCH, 6])
        mean, rstd, scratch = (sb(f"layer_{n}", [P, BATCH]) for n in ("mean", "rstd", "scratch"))
        expo = sb("layer_expo", [P, TILES])
        one = sb("one", [P, 1, 1])
        end_stats = sb("end_stats", [P, TILES, 6])
        end_mean, end_rstd, end_scratch = (sb(f"end_{n}", [P, TILES]) for n in ("mean", "rstd", "scratch"))

        fixed_in = sem("fixed_in")
        set_up = sem("set_up")
        attn_w_in = sem("attn_w_in")
        ffn_w_in = sem("ffn_w_in")
        names = ("tile_ready hT_ready hT_kept qkv_ready squared v_taken turn_ready turned_a turned_b norm_guard "
                 "norm_ready rot_sum rotated qk_T_ready qk_T_kept sim_ready sim_kept top_ready shift_ready "
                 "exp_done prob_T_ready prob_T_act prob_T_dve pv_ready total_inv o_ready o_T_ready o_T_kept "
                 "wo_ready win_done "
                 "half_ready half_T_ready carried half_T_kept half_back h_left h_right h_stats step h_normed "
                 "h_T_ready h_T_kept up_ready gate_ready hidden_ready down_ready batch_done "
                 "past_cleared first_in end_added end_counted end_step end_normed stored").split()
        s = {n: sem("l_" + n) for n in names}
        S = type("Semaphores", (), s)
        block = ctx.enter_context(nc.Block())
        qk_ps = (bank[1], bank[2])
        v_ps = bank[3]
        o_ps = bank[0]
        LAYER = TILES

        def slot(h):
            return (h % 2) * (LHEADS // 2) + h // 2

        def windows(eng, l, step):
            for w in range(RING):
                step(w, l * LAYER + w, w, w > 0, True)
            with eng.Fori(1, LAYER // RING - 1) as m:
                for i in range(RING):
                    step(m * RING + i, l * LAYER + m * RING + i, i, True, True)
            for w in range(LAYER - RING, LAYER):
                step(w, l * LAYER + w, w % RING, True, w < LAYER - 1)

        def batches(eng, l, step):
            with eng.Fori(0, BATCHES - 1) as b:
                step(b, l * BATCHES + b, True)
            step(BATCHES - 1, l * BATCHES + BATCHES - 1, False)

        @block.sync
        def _(sp):
            sp.dma_start(ident_f[:], ident).then_inc(fixed_in, 16)
            sp.dma_start(mask[:], masks.rearrange("m p n -> p m n")).then_inc(fixed_in, 16)
            sp.dma_start(rot[:], rotary.rearrange("(t p) n -> p t n", p=P)).then_inc(fixed_in, 16)
            with sp.Fori(0, DEPTH) as l:
                sp.wait_ge(S.win_done, l * LAYER)
                one = bass.ds(l, 1)
                sp.dma_start(wqkv[:], w_qkv[one].rearrange("a (k p) n -> p (a k) n", p=P)).then_inc(attn_w_in, 16)
                sp.dma_start(wo[:], w_o[one].rearrange("a (k p) n -> p (a k) n", p=P)).then_inc(attn_w_in, 16)
                sp.dma_start(qk_row[:], qk_rows[one].partition_broadcast(P)).then_inc(attn_w_in, 16)
                sp.wait_ge(S.batch_done, l * BATCHES)
                sp.dma_start(w1[:], w_1[one].rearrange("a (k p) n -> p (a k) n", p=P)).then_inc(ffn_w_in, 16)
                full = (HT - 1) * P
                sp.dma_start(w2[:, 0:HT - 1, :], w_2[one, 0:full].rearrange("a (k p) n -> p (a k) n", p=P)
                             ).then_inc(ffn_w_in, 16)
                sp.dma_start(w2[0:HTAIL, HT - 1, :], w_2[one, full:HID].rearrange("a p n -> p (a n)")
                             ).then_inc(ffn_w_in, 16)
                for side in range(2):
                    at = side * HID
                    sp.dma_start(b1[:, side, 0:HT - 1], b_1[one, at:at + full].rearrange("a (k p) -> p (a k)", p=P),
                                 allow_slow_non_contiguous=True).then_inc(ffn_w_in, 16)
                    sp.dma_start(b1[0:HTAIL, side, HT - 1:HT],
                                 b_1[one, at + full:at + HID].rearrange("a p -> p a"),
                                 allow_slow_non_contiguous=True).then_inc(ffn_w_in, 16)
                sp.dma_start(b2[:], b_2[one]).then_inc(ffn_w_in, 16)
                sp.dma_start(gb[:], ln_gb[one].rearrange("a g (k p) -> p (a g) k", p=P),
                             allow_slow_non_contiguous=True).then_inc(ffn_w_in, 16)
            sp.wait_ge(S.win_done, DEPTH * LAYER)
            sp.dma_start(rot[:], first_norm).then_inc(S.first_in, 16)
            QUARTER = TILES // 4
            for i in range(4):
                sp.wait_ge(S.end_normed, (i + 1) * QUARTER)
                sp.dma_start(out.rearrange("(t p) e -> p t e", p=P)[:, i * QUARTER:(i + 1) * QUARTER, :],
                             tokens[:, i * QUARTER:(i + 1) * QUARTER, :]).then_inc(S.stored, 16)
            sp.wait_ge(S.stored, 64)
        FFN_DMAS = 9 * 16

        @block.gpsimd
        def _(pool):
            pool.memset(expo[:], -0.5).then_inc(set_up, 1)
            pool.memset(one[:], 1.0).then_inc(set_up, 1)
            pool.memset(k_T[1][:], 0.0).then_inc(set_up, 1)
            pool.memset(v_kept[RING - 1][:], 0.0).then_inc(set_up, 1)
            pool.wait_ge(set_up, 6)

            def pick(w, g, par):
                pool.wait_ge(S.hT_ready, g + 1)
                same(pool, tile_in[par][:].rearrange("p (a n) -> p a n", a=1), tokens[:, bass.ds(w, 1), :], one).then_inc(S.tile_ready, 1)

            def rotate(g):
                pool.wait_ge(S.norm_guard, g + 1)
                pool.tensor_tensor(norm[:], norm[:], expo[:, 0:2 * LHEADS].rearrange("p (h a) -> p h a", a=1),
                                   ALU.pow).then_inc(S.norm_ready, 1)
                pool.wait_ge(S.turned_b, g * 2 + 2)
                pool.tensor_tensor(rot_a[:], rot_a[:], rot_b[:], ALU.add).then_inc(S.rot_sum, 1)

            def window(w, g, at, before, more):
                if more:
                    pick(w + 1, g + 1, (at + 1) % 2)
                    rotate(g + 1)

            def take_half(b, g):
                pool.wait_ge(S.half_T_ready, g + 0)
                same(pool, half_in[:], tokens[:, bass.ds(b * BATCH, BATCH), P:E], one).then_inc(S.half_ready, 1)
                pool.wait_ge(S.h_T_ready, g * 2)
                same(pool, h_tok[:, :, 0:P], tokens[:, bass.ds(b * BATCH, BATCH), 0:P], one).then_inc(S.h_left, 1)
                layernorm_params(None, pool, stats, mean[:], rstd[:], scratch[:], expo, S.step, g * 8)

            with pool.Fori(0, DEPTH) as l:
                pool.wait_ge(S.batch_done, l * BATCHES)
                pick(0, l * LAYER, 0)
                rotate(l * LAYER)
                windows(pool, l, window)
                pool.wait_ge(S.win_done, l * LAYER + LAYER)
                take_half(0, l * BATCHES)
                batches(pool, l, lambda b, g, more: take_half(b + 1, g + 1) if more else None)
            layernorm_params(None, pool, end_stats, end_mean[:], end_rstd[:], end_scratch[:], expo, S.end_step, 0)

        @block.tensor
        def _(pe):
            def turn_tile(g, par):
                pe.wait_ge(S.tile_ready, g + 1)
                pe.wait_ge(S.v_taken, g)
                for k in range(KE):
                    mm = pe.transpose(v_ps[:, k * P:(k + 1) * P], tile_in[par][:, k * P:(k + 1) * P], ident_f[:])
                mm.then_inc(S.hT_ready, 1)

            def project(g, par):
                pe.wait_ge(S.hT_kept, g + 1)
                pe.wait_ge(S.qk_T_kept, g)
                for j, ps in enumerate((*qk_ps, v_ps)):
                    for k, h in enumerate((hT_a[par][:], hT_b[par][:, 0:P])):
                        mm = pe.matmul(ps[:], h, wqkv[:, k, j * INNER:(j + 1) * INNER],
                                       start=k == 0, stop=k == KE - 1)
                mm.then_inc(S.qkv_ready, 1)

            def turn_qk(g):
                pe.wait_ge(S.rotated, g + 1)
                for j in range(2):
                    for i in range(KI):
                        mm = pe.transpose(qk_ps[j][:, i * P:(i + 1) * P],
                                          rot_a[:].rearrange("p h d -> p (h d)")[:, (j * KI + i) * P:(j * KI + i + 1) * P],
                                          ident_f[:])
                mm.then_inc(S.qk_T_ready, 1)

            def similarities(g, par):
                pe.wait_ge(S.qk_T_kept, g + 1)
                pe.wait_ge(S.prob_T_act, g)
                pe.wait_ge(S.prob_T_dve, g)
                for h in range(LHEADS):
                    rows = slice(LD * (h % 2), LD * (h % 2 + 1))
                    for c, keys in enumerate((k_T[1 - par], k_T[par])):
                        at = (slot(h) % 2) * SLAB + c * P
                        mm = pe.matmul(quad[:, slot(h) // 2, at:at + P], q_T[rows, h // 2, :], keys[rows, h // 2, :],
                                       start=True, stop=True)
                mm.then_inc(S.sim_ready, 1)

            def turn_prob(g):
                pe.wait_ge(S.exp_done, g + 1)
                for h in range(LHEADS):
                    for c in range(2):
                        j = 2 * h + c
                        mm = pe.transpose(quad[:, j // 4, (j % 4) * P:(j % 4 + 1) * P],
                                          prob[:, h, c * P:(c + 1) * P], ident_f[:])
                mm.then_inc(S.prob_T_ready, 1)

            def weigh(g, at):
                pe.wait_ge(S.prob_T_act, g + 1)
                pe.wait_ge(S.prob_T_dve, g + 1)
                pe.wait_ge(S.win_done, g)
                for h in range(LHEADS):
                    for c, v in enumerate((v_kept[at - 1], v_kept[at])):
                        j = slot(h)
                        mm = pe.matmul(o_ps[:, j * LD:(j + 1) * LD], prob_T[:, 2 * j + c, :],
                                       v[:, h * LD:(h + 1) * LD], start=c == 0, stop=c == 1)
                mm.then_inc(S.pv_ready, 1)

            def turn_o(g):
                pe.wait_ge(S.o_ready, g + 1)
                for i in range(KI):
                    mm = pe.transpose(o_ps[:, i * P:(i + 1) * P],
                                      o_tok[:].rearrange("p h d -> p (h d)")[:, i * P:(i + 1) * P], ident_f[:])
                mm.then_inc(S.o_T_ready, 1)

            def project_o(g):
                pe.wait_ge(S.o_T_kept, g + 1)
                for i in range(KI):
                    mm = pe.matmul(o_ps[:, 0:E], o_T[:, i, :], wo[:, i, :], start=i == 0, stop=i == KI - 1)
                mm.then_inc(S.wo_ready, 1)

            def window(w, g, at, before, more):
                par = at % 2
                if more:
                    turn_tile(g + 1, 1 - par)
                similarities(g, par)
                if more:
                    project(g + 1, 1 - par)
                if before:
                    weigh(g - 1, (at - 1) % RING)
                turn_prob(g)
                if before:
                    turn_o(g - 1)
                if more:
                    turn_qk(g + 1)
                if before:
                    project_o(g - 1)
                if not more:
                    weigh(g, at)
                    turn_o(g)
                    project_o(g)

            turned, back, h_ps = bank[0], bank[0], bank[1]
            down = (bank[2], bank[3])

            def turn_half(g):
                pe.wait_ge(S.half_ready, g + 1)
                pe.wait_ge(S.h_right, g)
                for i in range(BATCH):
                    mm = pe.transpose(turned[:, i * P:(i + 1) * P], half_in[:, i, :], ident_f[:])
                mm.then_inc(S.half_T_ready, 1)

            def turn_back(g):
                pe.wait_ge(S.half_T_kept, g + 1)
                for i in range(BATCH):
                    mm = pe.transpose(back[:, i * P:(i + 1) * P], half_T[:, i * P:(i + 1) * P], ident_f[:])
                mm.then_inc(S.half_back, 1)

            def turn_h(g):
                pe.wait_ge(S.h_normed, g + 1)
                for k in range(KE):
                    pe.wait_ge(S.h_T_kept, g * 2 + k)
                    for i in range(BATCH):
                        mm = pe.transpose(h_ps[:, i * P:(i + 1) * P], h_tok[:, i, k * P:(k + 1) * P], ident_f[:])
                    mm.then_inc(S.h_T_ready, 1)

            def up(g, i):
                rows = P if i < HT - 1 else HTAIL
                if i == 0:
                    pe.wait_ge(S.h_T_kept, g * 2 + 2)
                pe.wait_ge(S.hidden_ready, g * HT + i + 1)
                for side in range(2):
                    at = side * HID + i * P
                    for k in range(KE):
                        mm = pe.matmul(quad[0:rows, 2 * (i % 2) + side, :], w1[:, k, at:at + rows], h_T[:, k, :],
                                       start=k == 0, stop=k == KE - 1)
                mm.then_inc(S.up_ready, 1)

            def go_down(g):
                pe.wait_ge(S.hidden_ready, g * HT + HT + 2)
                pe.wait_ge(S.batch_done, g)
                for w in range(BATCH):
                    res = down[w // 2][:, (w % 2) * E:(w % 2 + 1) * E]
                    for i in range(HT):
                        rows = P if i < HT - 1 else HTAIL
                        pe.matmul(res, hidden[0:rows, i, w * P:(w + 1) * P], w2[0:rows, i, :],
                                  start=i == 0, stop=False)
                    mm = pe.matmul(res, ones_row[:], b2[:], start=False, stop=True)
                mm.then_inc(S.down_ready, 1)

            def batch(b, g, more):
                for i in range(HT):
                    up(g, i)
                    if more and i == 0:
                        turn_half(g + 1)
                    if more and i == 1:
                        turn_back(g + 1)
                go_down(g)
                if more:
                    turn_h(g + 1)

            pe.wait_ge(fixed_in, 48)
            pe.wait_ge(set_up, 6)
            with pe.Fori(0, DEPTH) as l:
                pe.wait_ge(attn_w_in, l * 48 + 48)
                turn_tile(l * LAYER, 0)
                project(l * LAYER, 0)
                turn_qk(l * LAYER)
                windows(pe, l, window)
                pe.wait_ge(S.win_done, l * LAYER + LAYER)
                pe.wait_ge(ffn_w_in, l * FFN_DMAS + FFN_DMAS)
                turn_half(l * BATCHES)
                turn_back(l * BATCHES)
                turn_h(l * BATCHES)
                batches(pe, l, batch)
                pe.wait_ge(S.batch_done, l * BATCHES + BATCHES)

        @block.scalar
        def _(act):
            def keep_hT(g, par):
                act.wait_ge(S.hT_ready, g + 3)
                act.activation(hT_a[par][:], v_ps[:, 0:P], ACT.Copy)
                act.activation(hT_b[1 - par][:, 0:1], v_ps[:, 2 * P - 1:2 * P], ACT.Copy)
                act.activation(hT_b[par][:, 1:P + 1], v_ps[:, P:2 * P], ACT.Copy).then_inc(S.hT_kept, 1)

            def square(g):
                act.wait_ge(S.qkv_ready, g + 1)
                act.wait_ge(S.norm_guard, g)
                for j in range(2):
                    act.activation(squares[:, j * LHEADS:(j + 1) * LHEADS, :],
                                   qk_ps[j][:].rearrange("p (h d) -> p h d", d=LD), ACT.Square
                                   ).then_inc(S.squared, 1)

            def take_v(g, at):
                act.activation(v_kept[at][:], v_ps[:], ACT.Copy).then_inc(S.v_taken, 1)

            def keep_qk(g, par):
                act.wait_ge(S.qk_T_ready, g + 1)
                act.activation(q_T[:].rearrange("p i n -> p (i n)"), qk_ps[0][:], ACT.Copy)
                act.activation(k_T[par][:].rearrange("p i n -> p (i n)"), qk_ps[1][:], ACT.Copy
                               ).then_inc(S.qk_T_kept, 1)

            def exps(g):
                act.wait_ge(S.shift_ready, g + 1)
                act.wait_ge(S.prob_T_ready, g)
                act.wait_ge(S.total_inv, g)
                for h in range(LHEADS):
                    ins = act.activation(prob[:, h, :], sim[:, h, :], ACT.Exp, bias=shift[:, h:h + 1],
                                         scale=QK_SCALE, accum_out=total[:, h, :])
                ins.then_inc(S.exp_done, 1)

            def keep_o(g):
                act.wait_ge(S.o_T_ready, g + 1)
                act.activation(o_T[:].rearrange("p i n -> p (i n)"), o_ps[:], ACT.Copy).then_inc(S.o_T_kept, 1)

            def window(w, g, at, before, more):
                par = at % 2
                if more:
                    keep_hT(g + 1, 1 - par)
                    square(g + 1)
                exps(g)
                if more:
                    take_v(g + 1, (at + 1) % RING)
                act.wait_ge(S.prob_T_ready, g + 1)
                act.activation(prob_T[:, 0:LHEADS, :].rearrange("p (a b) n -> p a (b n)", a=2), quad[:, 0:2, :],
                               ACT.Copy).then_inc(S.prob_T_act, 1)
                if before:
                    keep_o(g - 1)
                if more:
                    keep_qk(g + 1, 1 - par)
                else:
                    keep_o(g)

            def keep_half(g):
                act.wait_ge(S.half_T_ready, g + 1)
                act.wait_ge(S.half_back, g)
                act.activation(half_T[:, 0:1], half_T[:, BATCH * P:BATCH * P + 1], ACT.Copy).then_inc(S.carried, 1)
                act.wait_ge(S.carried, g + 1)
                act.activation(half_T[:, 1:BATCH * P + 1], bank[0][:], ACT.Copy).then_inc(S.half_T_kept, 1)

            def keep_h(g):
                for k in range(KE):
                    act.wait_ge(S.h_T_ready, g * 2 + k + 1)
                    act.activation(h_T[:, k, :], bank[1][:], ACT.Identity, scale=gb[:, 0, k:k + 1],
                                   bias=gb[:, 1, k:k + 1]).then_inc(S.h_T_kept, 1)

            def batch(b, g, more):
                for i in range(HT):
                    rows = P if i < HT - 1 else HTAIL
                    act.wait_ge(S.up_ready, g * HT + i + 1)
                    act.wait_ge(S.hidden_ready, g * HT + i + 1)
                    act.activation(gate[0:rows, i % 2, :], quad[0:rows, 2 * (i % 2) + 1, :], ACT.Gelu,
                                   bias=b1[0:rows, 1, i:i + 1]).then_inc(S.gate_ready, 1)
                    if more and i == 0:
                        keep_half(g + 1)
                if more:
                    keep_h(g + 1)

            act.wait_ge(set_up, 6)
            with act.Fori(0, DEPTH) as l:
                act.preload_act_table(ACT.Exp)
                act.wait_ge(S.past_cleared, l + 1)
                keep_hT(l * LAYER, 0)
                square(l * LAYER)
                take_v(l * LAYER, 0)
                keep_qk(l * LAYER, 0)
                windows(act, l, window)
                act.preload_act_table(ACT.Gelu)
                keep_half(l * BATCHES)
                act.wait_ge(ffn_w_in, l * FFN_DMAS + FFN_DMAS)
                keep_h(l * BATCHES)
                batches(act, l, batch)

        @block.vector
        def _(dve):
            dve.memset(ones_row[:], 1.0).then_inc(set_up, 1)
            dve.memset(squares[:], 0.0).then_inc(set_up, 1)
            dve.sem_inc(S.hT_ready, 2)
            dve.sem_inc(S.hidden_ready, 2)

            def scale_rotate(w, g):
                dve.wait_ge(S.turned_b, g * 2)
                dve.tensor_tensor(turn[:], rot[:, bass.ds(w, 1), :], qk_row[:], ALU.mult).then_inc(S.turn_ready, 1)
                dve.wait_ge(S.turn_ready, g + 1)
                dve.wait_ge(S.qk_T_ready, g)
                LH = LD // 2
                for j in range(2):
                    dve.wait_ge(S.squared, g * 2 + j + 1)
                    qk = qk_ps[j][:].rearrange("p (h d) -> p h d", d=LD)
                    heads = slice(j * LHEADS, (j + 1) * LHEADS)
                    cos = turn[:, j * LD:(j + 1) * LD].rearrange("p (a d) -> p a d", a=1)
                    sin = turn[:, (2 + j) * LD:(3 + j) * LD].rearrange("p (a d) -> p a d", a=1)
                    dve.tensor_tensor(rot_a[:, heads, :], qk, cos.to_broadcast([P, LHEADS, LD]), ALU.mult)
                    dve.tensor_tensor(rot_b[:, heads, 0:LH], qk[:, :, LH:LD],
                                      sin[:, :, 0:LH].to_broadcast([P, LHEADS, LH]), ALU.mult)
                    dve.tensor_tensor(rot_b[:, heads, LH:LD], qk[:, :, 0:LH],
                                      sin[:, :, LH:LD].to_broadcast([P, LHEADS, LH]), ALU.mult
                                      ).then_inc(S.turned_b, 1)

            def sum_squares(g):
                dve.wait_ge(S.squared, g * 2 + 2)
                dve.wait_ge(S.rotated, g)
                dve.tensor_reduce(norm[:, :, 0], squares[:], AX.X, ALU.add).then_inc(S.turned_a, 1)
                dve.wait_ge(S.turned_a, g + 1)
                dve.tensor_scalar(norm[:], norm[:], 1e-24, None, ALU.max).then_inc(S.norm_guard, 1)

            def divide_norm(g):
                dve.wait_ge(S.rot_sum, g + 1)
                dve.wait_ge(S.norm_ready, g + 1)
                dve.tensor_tensor(rot_a[:], rot_a[:], norm[:].to_broadcast([P, 2 * LHEADS, LD]), ALU.mult
                                  ).then_inc(S.rotated, 1)

            def divide_o(g):
                dve.wait_ge(S.pv_ready, g + 1)
                dve.wait_ge(S.total_inv, g + 1)
                dve.tensor_tensor(o_tok[:].rearrange("p (a b) d -> p b a d", b=2),
                                  o_ps[:].rearrange("p (b a d) -> p b a d", b=2, d=LD),
                                  inv_total[:].rearrange("p (b a) d -> p b a d", b=2)
                                  .to_broadcast([P, 2, LHEADS // 2, LD]), ALU.mult).then_inc(S.o_ready, 1)

            def add_o(w, g):
                dve.wait_ge(S.wo_ready, g + 1)
                tile = tokens[:, bass.ds(w, 1), :]
                dve.tensor_tensor(tile, o_ps[:, 0:E], tile, ALU.add).then_inc(S.win_done, 1)

            def window(w, g, at, before, more):
                dve.wait_ge(S.sim_ready, g + 1)
                dve.wait_ge(S.exp_done, g)
                which = (w + TILES - 1) // TILES
                sims = quad[:].rearrange("p a (b n) -> p a b n", b=2)
                dve.tensor_tensor(sim[:].rearrange("p (a b) n -> p a b n", b=2), sims,
                                  mask[:, bass.ds(which, 1), :].rearrange("p (a b) n -> p a b n", b=1)
                                  .to_broadcast([P, 4, 2, SLAB]), ALU.add).then_inc(S.sim_kept, 1)
                dve.wait_ge(S.sim_kept, g + 1)
                dve.tensor_reduce(top[:], sim[:], AX.X, ALU.max).then_inc(S.top_ready, 1)
                dve.wait_ge(S.top_ready, g + 1)
                dve.tensor_scalar(shift[:], top[:], -QK_SCALE, None, ALU.mult).then_inc(S.shift_ready, 1)
                if more:
                    sum_squares(g + 1)
                    scale_rotate(w + 1, g + 1)
                if before:
                    divide_o(g - 1)
                dve.wait_ge(S.exp_done, g + 1)
                dve.wait_ge(S.o_ready, g)
                dve.reciprocal(inv_total[:], total[:]).then_inc(S.total_inv, 1)
                dve.wait_ge(S.prob_T_ready, g + 1)
                dve.tensor_copy(prob_T[:, LHEADS:, :].rearrange("p (a b) n -> p a (b n)", a=2), quad[:, 2:4, :]
                                ).then_inc(S.prob_T_dve, 1)
                if more:
                    divide_norm(g + 1)
                if before:
                    add_o(w - 1, g - 1)
                if not more:
                    divide_o(g)
                    add_o(w, g)

            def norm_batch(g):
                dve.wait_ge(S.half_back, g + 1)
                dve.wait_ge(S.h_left, g + 1)
                dve.tensor_copy(h_tok[:, :, P:E], bank[0][:].rearrange("p (b n) -> p b n", n=P)).then_inc(S.h_right, 1)
                dve.wait_ge(S.h_right, g + 1)
                for i in range(BATCH):
                    ins = dve.bn_stats(stats[:, i, :], h_tok[:, i, :])
                ins.then_inc(S.h_stats, 1)
                dve.wait_ge(S.h_stats, g + 1)
                layernorm_params(dve, None, stats, mean[:], rstd[:], scratch[:], expo, S.step, g * 8)
                dve.wait_ge(S.step, g * 8 + 8)
                for i in range(BATCH):
                    ins = dve.tensor_scalar(h_tok[:, i, :], h_tok[:, i, :], mean[:, i:i + 1], rstd[:, i:i + 1],
                                            ALU.subtract, ALU.mult)
                ins.then_inc(S.h_normed, 1)

            def batch(b, g, more):
                for i in range(HT):
                    rows = P if i < HT - 1 else HTAIL
                    dve.wait_ge(S.gate_ready, g * HT + i + 1)
                    if i == 0:
                        dve.wait_ge(S.down_ready, g)
                    dve.scalar_tensor_tensor(out=hidden[0:rows, i, :], in0=quad[0:rows, 2 * (i % 2), :],
                                             scalar=b1[0:rows, 0, i:i + 1], in1=gate[0:rows, i % 2, :],
                                             op0=ALU.add, op1=ALU.mult).then_inc(S.hidden_ready, 1)
                    if more and i == 2:
                        norm_batch(g + 1)
                dve.wait_ge(S.down_ready, g + 1)
                for j in range(2):
                    tiles = tokens[:, bass.ds(b * BATCH + 2 * j, 2), :]
                    ins = dve.tensor_tensor(tiles, bank[2 + j][:].rearrange("p (b n) -> p b n", n=E), tiles, ALU.add)
                ins.then_inc(S.batch_done, 1)

            dve.wait_ge(fixed_in, 48)
            with dve.Fori(0, DEPTH) as l:
                dve.memset(hT_b[0][:, 0:1], 0.0)
                dve.memset(half_T[:, BATCH * P:BATCH * P + 1], 0.0).then_inc(S.past_cleared, 1)
                dve.wait_ge(attn_w_in, l * 48 + 48)
                sum_squares(l * LAYER)
                scale_rotate(0, l * LAYER)
                divide_norm(l * LAYER)
                windows(dve, l, window)
                dve.wait_ge(ffn_w_in, l * FFN_DMAS + FFN_DMAS)
                norm_batch(l * BATCHES)
                batches(dve, l, batch)
            dve.wait_ge(S.batch_done, DEPTH * BATCHES)
            dve.wait_ge(S.first_in, 16)
            with dve.Fori(0, TILES) as t:
                tile = tokens[:, bass.ds(t, 1), :]
                dve.tensor_tensor(tile, tile, rot[:, bass.ds(t, 1), :], ALU.add).then_inc(S.end_added, 1)
                dve.wait_ge(S.end_added, t + 1)
                dve.bn_stats(end_stats[:, bass.ds(t, 1), :], tokens[:, bass.ds(t, 1), :]).then_inc(S.end_counted, 1)
            dve.wait_ge(S.end_counted, TILES)
            end = layernorm_params(dve, None, end_stats, end_mean[:], end_rstd[:], end_scratch[:], expo,
                                   S.end_step, 0)
            dve.wait_ge(S.end_step, end)
            normalise(dve, tokens, end_mean, end_rstd, S.end_normed)


def build(nc, ins, out):
    q_stack = nc.dram_tensor("q_stack", [HEADS, ROWS, N], BF16, kind="Internal").ap()
    k_parts = nc.dram_tensor("k_parts", [HEADS, 3 * D, 2 * N], BF16, kind="Internal").ap()
    v_wide = nc.dram_tensor("v_wide", [HEADS, P, 2 * TILES * VW], F32, kind="Internal").ap()
    first_norm = nc.dram_tensor("first_norm", [P, TILES, E], F32, kind="Internal").ap()
    with ExitStack() as ctx:
        project_heads(nc, ins["x_T"], ins["w_in_T"], ins["b_in"], ins["pe_edges"], q_stack, k_parts, v_wide)
        tokens = ctx.enter_context(nc.sbuf_tensor("tokens", [P, TILES, E], F32))
        attend(nc, q_stack, k_parts, v_wide, ins["rel_T"], ins["ident"], ins["part_sum"], tokens)
        join_heads(nc, ins["x"], ins["w_out_T"], ins["b_out"], ins["ident"], tokens, first_norm)
        local_layers(nc, ins["w_qkv"], ins["qk_rows"], ins["w_o"], ins["ln_gb"], ins["w_1"], ins["b_1"],
                     ins["w_2"], ins["b_2"], ins["rotary"], ins["masks"], ins["ident"], tokens, first_norm, out)


def shape_constants():
    import numpy as np
    f = np.float32
    half = np.arange(0, LD, 2, dtype=f)
    inv_freq = f(1.0) / np.power(f(10000.0), half / f(LD), dtype=f)
    t = np.arange(N, dtype=f)
    freqs = t[:, None] * inv_freq[None, :]
    base = (half + f(0.4 * LD)) / f(1.4 * LD)
    power = (t - f(N // 2)) / f(P // 2)
    scale = np.power(base[None, :], power[:, None], dtype=f)
    cos, sin = np.cos(freqs), np.sin(freqs)
    both = lambda a, b: np.concatenate([a, b], axis=1)
    rotary = np.concatenate([both(cos * scale, cos * scale), both(cos / scale, cos / scale),
                             both(-sin * scale, sin * scale), both(-sin / scale, sin / scale)], axis=1)
    i, j = np.arange(P)[:, None], np.arange(SLAB)[None, :] - P
    hidden = (i < j) | (i > j + P)
    masks = np.stack([hidden | (j < 0), hidden]) * f(-3e37)
    part_sum = np.zeros((P, VW), f)
    for quadrant in range(0, P, 32):
        part_sum[quadrant:quadrant + VW] = np.eye(VW, dtype=f)
    return {"rotary": rotary.astype(f), "masks": masks.astype(f), "part_sum": part_sum,
            "ident": np.eye(P, dtype=f)}


def kernel(**inputs):
    import numpy as np
    import concourse.bacc as bacc
    from concourse.bass_utils import run_bass_kernel_spmd

    g = {k: np.asarray(v) for k, v in inputs.items()}
    x = g["L0_attn_q"].reshape(N, E)
    pe = g["L0_attn_rel_pe"]
    qs, ks = g["L0_ffn_q_scale"], g["L0_ffn_k_scale"]
    swap = lambda a: np.concatenate([a[:, LD // 2:], a[:, :LD // 2]], axis=1)
    arrays = {
        "x": x, "x_T": x.T, "w_in_T": g["L0_attn_in_proj_weight"].T, "b_in": g["L0_attn_in_proj_bias"],
        "pe_edges": np.tile(pe[::2 * CLIP], (1, GROUP)), "rel_T": pe.T,
        "w_out_T": g["L0_attn_out_w"].T, "b_out": g["L0_attn_out_b"],
        "w_qkv": g["L0_ffn_wqkv"], "qk_rows": np.concatenate([qs, ks, swap(qs), swap(ks)], axis=1),
        "w_o": g["L0_ffn_wo"], "ln_gb": np.stack([g["L0_ffn_ln_g"], g["L0_ffn_ln_b"]], axis=1),
        "w_1": g["L0_ffn_w1"], "b_1": g["L0_ffn_b1"], "w_2": g["L0_ffn_w2"], "b_2": g["L0_ffn_b2"],
        **shape_constants(),
    }
    nc = bacc.Bacc("TRN2", target_bir_lowering=False, num_devices=1)
    ins, feed = {}, {}
    for name, a in arrays.items():
        a = np.ascontiguousarray(a)
        feed[f"in_{name}"] = a
        ins[name] = nc.dram_tensor(f"in_{name}", a.shape, mybir.dt.from_np(a.dtype), kind="ExternalInput").ap()
    out = nc.dram_tensor("out_tokens", (N, E), F32, kind="ExternalOutput").ap()
    build(nc, ins, out)
    r = run_bass_kernel_spmd(nc, [feed], core_ids=[0])
    return r.results[0]["out_tokens"].reshape(1, N, E)
```

```python
from contextlib import ExitStack

import concourse.bass as bass
from concourse import mybir

F32 = mybir.dt.float32
BF16 = mybir.dt.bfloat16
ACT = mybir.ActivationFunctionType
ALU = mybir.AluOpType
AX = mybir.AxisListType

P = 128
N = 4096
E = 256
KE = E // P
TILES = N // P
LN_EPS = 1e-5

HEADS = 16
D = E // HEADS
CLIP = 64
GROUP = P // D
CH = 512
CHUNKS = N // CH
TPC = CH // P
Q_PARTS = (0, 0, 0, 1, 1, 2)
K_RUNS = (3, 2, 1)
TERMS = len(Q_PARTS)
ROWS = TERMS * D
MROWS = 2
VW = D + 1
WIN_TILES = TILES + TPC - 1
SLAB = 2 * P
PAD = CLIP
PAIRS = TILES // 2
QUADS = TILES // 4
BLOCK_U = SLAB // CHUNKS
BLOCK_W = BLOCK_U - 1 + P
UG = BLOCK_U // 2

def project_heads(nc, x_T, w_in_T, b_in, pe_edges, q_stack, k_parts, v_wide):
    with ExitStack() as ctx:
        sb = lambda name, shape, dt=F32: ctx.enter_context(nc.sbuf_tensor(name, shape, dt))
        sem = lambda name: ctx.enter_context(nc.semaphore(name))
        weights = sb("in_weights", [P, KE, 3 * E])
        v_bias = sb("v_bias", [1, E])
        ones_row = sb("ones_row", [1, P])
        qk_bias = sb("qk_bias", [P, 4])
        edges = sb("edges", [P, 2])
        bias = sb("unit_bias", [P, 6])
        x_in = sb("x_in", [P, 2, KE, CH])
        exact = sb("exact", [P, 6, CH])
        rest = sb("rest", [P, 2, CH])
        part = sb("part", [P, 3, 6, CH], BF16)
        v_stage = sb("v_stage", [P, HEADS, TPC, VW])
        unit_ps = [ctx.enter_context(nc.psum_tensor(f"unit_ps{u}", [P, CH], F32)) for u in range(4)]
        value_ps = [ctx.enter_context(nc.psum_tensor(f"value_ps{u}", [P, 2, E], F32)) for u in range(2)]

        consts_in = sem("consts_in")
        x_loaded = [sem(f"x_loaded{i}") for i in range(2)]
        ones_set = sem("ones_set")
        bias_made = sem("bias_made")
        units_done = sem("units_done")
        values_done = sem("values_done")
        exact_done = sem("exact_done")
        hi_done = sem("hi_done")
        rest_done = sem("rest_done")
        mid_done = sem("mid_done")
        low_done = sem("low_done")
        v_staged = sem("v_staged")
        v_stored = sem("v_stored")
        parts_stored = [sem(f"parts_stored{v}") for v in range(6)]
        VARIANTS = ((0, 0), (1, 1), (2, 2), (2, 3), (3, 4), (3, 5))
        UNIT_READ = (1, 2, 4, 6)
        Q_STORES, K_STORES = TERMS, 3

        block = ctx.enter_context(nc.Block())

        @block.gpsimd
        def _(pool):
            with pool.Fori(0, CHUNKS // 2) as m:
                for par in range(2):
                    n = m * 2 + par
                    pool.wait_ge(values_done, m * 2 + 1)
                    pool.dma_start(x_in[:, par, :, :],
                                   x_T.rearrange("(k p) n -> p k n", p=P)[:, :, bass.ds(n * CH, CH)]
                                   ).then_inc(x_loaded[par], 16)

        @block.sync
        def _(sp):
            sp.dma_start(weights[:], w_in_T.rearrange("(k p) n -> p k n", p=P)).then_inc(consts_in, 16)
            sp.dma_start(qk_bias[:], b_in[0:2 * E].rearrange("(u p) -> p u", p=P),
                         allow_slow_non_contiguous=True).then_inc(consts_in, 16)
            sp.dma_start(edges[:], pe_edges.rearrange("e p -> p e"),
                         allow_slow_non_contiguous=True).then_inc(consts_in, 16)
            sp.dma_start(v_bias[:], b_in[2 * E:3 * E].rearrange("(a n) -> a n", a=1)).then_inc(consts_in, 16)
            with sp.Fori(0, CHUNKS) as n:
                col = n * CH
                for v, (unit, _) in enumerate(VARIANTS):
                    sp.wait_ge(low_done, n * 6 + v + 1)
                    heads = slice(GROUP * (unit % 2), GROUP * (unit % 2 + 1))
                    if unit < 2:
                        for t, which in enumerate(Q_PARTS):
                            sp.dma_start(q_stack[heads, t * D:(t + 1) * D, bass.ds(col, CH)],
                                         part[:, which, v, :]).then_inc(parts_stored[v], 16)
                    else:
                        side = col if v in (2, 4) else col + N
                        for which in range(3):
                            sp.dma_start(k_parts[heads, which * D:(which + 1) * D, bass.ds(side, CH)],
                                         part[:, which, v, :]).then_inc(parts_stored[v], 16)
                sp.wait_ge(v_staged, n + 2)
                for again in range(2):
                    sp.dma_start(v_wide.rearrange("h p (t e) -> p h t e", e=VW)
                                 [:, :, bass.ds(n * TPC + again * TILES, TPC), :],
                                 v_stage[:]).then_inc(v_stored, 16)
            for v in range(6):
                sp.wait_ge(parts_stored[v], 16 * CHUNKS * (Q_STORES if v < 2 else K_STORES) + 1)
            sp.wait_ge(v_stored, 32 * CHUNKS + 1)

        @block.tensor
        def _(pe):
            pe.wait_ge(consts_in, 64)
            pe.wait_ge(ones_set, 2)
            with pe.Fori(0, CHUNKS // 2) as m:
                for par in range(2):
                    n = m * 2 + par
                    pe.wait_ge(x_loaded[par], m * 16 + 16)
                    for u in range(4):
                        pe.wait_ge(exact_done, n * 6 + UNIT_READ[u])
                        for k in range(KE):
                            mm = pe.matmul(unit_ps[u][:], weights[:, k, u * P:(u + 1) * P],
                                           x_in[:, par, k, :], start=k == 0, stop=k == KE - 1)
                        mm.then_inc(units_done, 1)
                    pe.wait_ge(v_staged, n + 1)
                    for t in range(TPC):
                        out = value_ps[t // 2][:, t % 2, :]
                        for k in range(KE):
                            pe.matmul(out, x_in[:, par, k, t * P:(t + 1) * P],
                                      weights[:, k, 2 * E:3 * E], start=k == 0, stop=False)
                        mm = pe.matmul(out, ones_row[:], v_bias[:], start=False, stop=True)
                    mm.then_inc(values_done, 1)

        @block.scalar
        def _(act):
            act.preload_act_table(ACT.Identity)
            act.sem_inc(exact_done, 6)
            act.sem_inc(v_staged, 1)
            for semaphore in (values_done, v_stored, *parts_stored):
                act.sem_inc(semaphore, 1)
            act.wait_ge(bias_made, 1)
            act.wait_ge(ones_set, 2)
            with act.Fori(0, CHUNKS) as n:
                for v, (unit, b) in enumerate(VARIANTS):
                    act.wait_ge(units_done, n * 4 + unit + 1)
                    act.wait_ge(rest_done, n * 6 + v + 1)
                    act.activation(exact[:, v, :], unit_ps[unit][:], ACT.Identity,
                                   bias=bias[:, b:b + 1], scale=D ** -0.5 if unit < 2 else 1.0
                                   ).then_inc(exact_done, 1)
                    act.wait_ge(exact_done, n * 6 + v + 7)
                    act.wait_ge(parts_stored[v], n * (16 * (Q_STORES if v < 2 else K_STORES)) + 1)
                    act.activation(part[:, 0, v, :], exact[:, v, :], ACT.Identity).then_inc(hi_done, 1)
                act.wait_ge(values_done, n + 2)
                act.wait_ge(v_stored, n * 32 + 1)
                for half in range(2):
                    ins = act.activation(v_stage[:, :, 2 * half:2 * half + 2, 0:D],
                                         value_ps[half][:].rearrange("p t (h d) -> p h t d", d=D),
                                         ACT.Identity)
                ins.then_inc(v_staged, 1)

        @block.vector
        def _(dve):
            dve.memset(ones_row[:], 1.0).then_inc(ones_set, 1)
            dve.memset(v_stage[:], 1.0).then_inc(ones_set, 1)
            dve.sem_inc(rest_done, 6)
            dve.wait_ge(consts_in, 64)
            dve.tensor_scalar(bias[:, 0:2], qk_bias[:, 0:2], D ** -0.5, None, ALU.mult)
            for unit in range(2):
                for side in range(2):
                    ins = dve.tensor_tensor(bias[:, 2 + 2 * unit + side:3 + 2 * unit + side],
                                            qk_bias[:, 2 + unit:3 + unit], edges[:, 1 - side:2 - side],
                                            ALU.add)
            ins.then_inc(bias_made, 1)
            with dve.Fori(0, CHUNKS) as n:
                for v in range(6):
                    dve.wait_ge(hi_done, n * 6 + v + 1)
                    dve.tensor_tensor(rest[:, v % 2, :], exact[:, v, :], part[:, 0, v, :], ALU.subtract
                                      ).then_inc(rest_done, 1)
                    dve.wait_ge(rest_done, n * 6 + v + 7)
                    dve.tensor_copy(part[:, 1, v, :], rest[:, v % 2, :]).then_inc(mid_done, 1)
                    dve.wait_ge(mid_done, n * 6 + v + 1)
                    dve.tensor_tensor(part[:, 2, v, :], rest[:, v % 2, :], part[:, 1, v, :], ALU.subtract
                                      ).then_inc(low_done, 1)

def same(pool, out, in_, ones):
    return pool.tensor_tensor(out, in_, ones[:].to_broadcast(list(in_.shape)), ALU.mult)


def attend(nc, q_stack, k_parts, v_wide, rel_T, ident, part_sum, attn):
    NEXT_GEN = CHUNKS + 1
    LEAD = 16
    TOTAL = HEADS * CHUNKS
    SLOT_SCORES = ((0, 1), (2, 3), (), ())
    NEAR_SLOTS = (26, 27, 30, 23)
    ROWS_SLOT = 20
    MAX_GROUPS = TPC * (TILES // TPC)
    with ExitStack() as ctx:
        sb = lambda name, shape, dt=F32: ctx.enter_context(nc.sbuf_tensor(name, shape, dt))
        ps = lambda name, shape, dt=F32: ctx.enter_context(nc.psum_tensor(name, shape, dt))
        sem = lambda name: ctx.enter_context(nc.semaphore(name))
        keys = [sb(f"keys{i}", [ROWS + MROWS, WIN_TILES * P], BF16) for i in range(2)]
        queries = [sb(f"queries{i}", [ROWS + MROWS, CH], BF16) for i in range(2)]
        max_queries = [sb(f"max_queries{i}", [ROWS, CH], BF16) for i in range(2)]
        values = [sb(f"values{i}", [P, TILES, VW]) for i in range(2)]
        head_q = sb("head_q", [ROWS, 2, N + SLAB], BF16)
        near_bias = sb("near_bias", [P, 2, TILES + 2, SLAB])
        near_window = [sb(f"near_window{i}", [P, TPC + 2, SLAB + 2 * PAD], BF16) for i in range(2)]
        block_q = [sb(f"block_q{i}", [ROWS, TILES, BLOCK_U], BF16) for i in range(2)]
        block_table = [sb(f"block_table{i}", [ROWS, BLOCK_W], BF16) for i in range(2)]
        probs = [sb(f"probs{i}", [P, 2, CH]) for i in range(4)]
        table = sb("table", [ROWS, CHUNKS, BLOCK_W], BF16)
        table_raw = sb("table_raw", [D, 2 * CLIP + 1])
        R_COLS = 3 * P - 1 - PAD
        L_COLS = 3 * P - 1 - 3 * PAD
        ext = sb("table_ext", [D, R_COLS + L_COLS])
        ext_rest = sb("table_rest", [D, R_COLS + L_COLS])
        ext_part = sb("table_part", [D, 3, R_COLS + L_COLS], BF16)
        ext_rows = sb("table_rows", [ROWS, R_COLS + L_COLS], BF16)
        ident_f = sb("ident_f", [P, P])
        ident_b = sb("ident_b", [P, P], BF16)
        one_f = sb("one_f", [P, 1, 1])
        one_b = sb("one_b", [ROWS, 1], BF16)
        sum_sel = sb("sum_sel", [P, VW])
        group_max = [sb(f"group_max{i}", [P, MAX_GROUPS]) for i in range(2)]
        row_max = sb("row_max", [P, TPC])
        max_parts = sb("max_parts", [P, TPC, MROWS], BF16)
        out_copy = sb("out_copy", [P, CH])
        inv_sum = sb("inv_sum", [P, TPC, 1])

        scores = [ps(f"scores{i}", [P, 2, CH]) for i in range(2)]
        out_ps = ps("out_ps", [P, CH])
        shared_ps = [ps(f"shared_ps{i}", [P, CH]) for i in range(3)]
        max_uses = [("max", i) for i in range(MAX_GROUPS)]
        SHARED_USES = (max_uses[:4] + [("bias", 0)] + max_uses[4:8] + [("bias", 1)]
                       + max_uses[8:ROWS_SLOT] + [("rows", 0)] + max_uses[ROWS_SLOT:] + [("sum", 0)])
        shared = lambda *use: shared_ps[SHARED_USES.index(use) % 3][:]

        consts_in = sem("consts_in2")
        table_cut = sem("table_cut")
        table_rows_in = sem("table_rows_in")
        table_ready = sem("table_ready")
        cleared = sem("cleared")
        ident_ready = sem("ident_ready")
        PIECES = ((0, 8, 3), (8, 16, 7), (16, 24, 11), (24, WIN_TILES, 15))
        keys_in = [[sem(f"keys_in{i}_{j}") for j in range(4)] for i in range(2)]
        queries_in = [sem(f"queries_in{i}") for i in range(2)]
        max_queries_in = [sem(f"max_queries_in{i}") for i in range(2)]
        values_in = [sem(f"values_in{i}") for i in range(2)]
        head_q_in = [sem(f"head_q_in{i}") for i in range(2)]
        block_ready = sem("block_ready")
        bias_ready = sem("bias_ready")
        bias_read = sem("bias_read")
        window_ready = sem("window_ready")
        max_ready = sem("max_ready")
        max_read = sem("max_read")
        max_step = sem("max_step")
        max_cut = sem("max_cut")
        max_rows = sem("max_rows")
        max_placed = sem("max_placed")
        scores_ready = sem("scores_ready")
        near_added = sem("near_added")
        exp_done = sem("exp_done")
        pv_done = sem("pv_done")
        out_copied = sem("out_copied")
        out_summed = sem("out_summed")
        norm_step = sem("norm_step")
        normed = sem("normed")

        block = ctx.enter_context(nc.Block())

        def place(n):
            return n // CHUNKS, n % CHUNKS

        @block.sync
        def _(sp):
            sp.dma_start(table_raw[:], rel_T).then_inc(consts_in, 16)
            sp.dma_start(ident_f[:], ident).then_inc(consts_in, 16)
            sp.dma_start(sum_sel[:], part_sum).then_inc(consts_in, 16)

            def load_keys(n, par, j):
                h, c = place(n)
                a, b, _ = PIECES[j]
                row = 0
                for run in K_RUNS:
                    rows = run * D
                    sp.dma_start(keys[par][row:row + rows, a * P:b * P],
                                 k_parts[bass.ds(h, 1), 0:rows, bass.ds(c * CH + a * P, (b - a) * P)]
                                 ).then_inc(keys_in[par][j], 16)
                    row += rows

            def load_queries(n, par):
                h, c = place(n)
                sp.dma_start(queries[par][0:ROWS, :], q_stack[bass.ds(h, 1), :, bass.ds(c * CH, CH)]
                             ).then_inc(queries_in[par], 16)

            def load_max_queries(n, par):
                h, c = place(n)
                sp.dma_start(max_queries[par][:], q_stack[bass.ds(h, 1), :, bass.ds(c * CH, CH)]
                             ).then_inc(max_queries_in[par], 16)

            def load_values(n, par):
                h, c = place(n)
                sp.dma_start(values[par][:], v_wide[bass.ds(h, 1), :, bass.ds(c * (TPC * VW), TILES * VW)]
                             ).then_inc(values_in[par], 16)

            for par in range(2):
                load_queries(par, par)
                load_max_queries(par, par)
                for j in range(4):
                    load_keys(par, par, j)
                load_values(par, par)
            sp.wait_ge(table_cut, 3)
            row = 0
            for run in K_RUNS:
                for which in range(run):
                    sp.dma_start(ext_rows[row:row + D, :], ext_part[:, which, :]
                                 ).then_inc(table_rows_in, 16)
                    row += D
            with sp.Fori(0, TOTAL // 2 - 1) as m:
                for par in range(2):
                    n = m * 2 + par
                    sp.wait_ge(max_ready, (n + 1) * MAX_GROUPS)
                    load_max_queries(n + 2, par)
                    for j in range(4):
                        sp.wait_ge(scores_ready, n * PAIRS + PIECES[j][2] + 1)
                        load_keys(n + 2, par, j)
                    load_queries(n + 2, par)
                    sp.wait_ge(pv_done, n * QUADS + QUADS + 2)
                    load_values(n + 2, par)

        @block.gpsimd
        def _(pool):
            for i in range(2):
                pool.memset(near_window[i][:], 0.0).then_inc(cleared, 1)
                pool.memset(near_bias[:, i, 0, :], 0.0).then_inc(cleared, 1)
                pool.memset(near_bias[:, i, TILES + 1, :], 0.0).then_inc(cleared, 1)
            pool.memset(head_q[:, :, 0:PAD], 0.0).then_inc(cleared, 1)
            pool.memset(head_q[:, :, PAD + N:], 0.0).then_inc(cleared, 1)
            pool.memset(one_f[:], 1.0).then_inc(cleared, 1)
            pool.memset(one_b[:], 1.0).then_inc(cleared, 1)
            pool.wait_ge(cleared, 10)

            def load_head_q(h, par):
                pool.dma_start(head_q[:, par, PAD:PAD + N], q_stack[bass.ds(h, 1), :, :]
                               ).then_inc(head_q_in[par], 16)

            def copy_window(h, c, par):
                n = h * CHUNKS + c
                if c == 0:
                    pool.wait_ge(bias_read, (h + 1) * (2 * CHUNKS))
                pool.wait_ge(max_cut, n + 1)
                same(pool, near_window[c % 2][:, :, PAD:PAD + SLAB],
                     near_bias[:, par, TPC * c:TPC * c + TPC + 2, :], one_f).then_inc(window_ready, 1)

            def copy_block(h, b, par):
                e = h * CHUNKS + b
                if b == 0:
                    pool.wait_ge(head_q_in[par], h // 2 * 16 + 16)
                if not isinstance(e, int) or e >= 2:
                    pool.wait_ge(bias_ready, e * 2 - 2)
                first = b * BLOCK_U
                same(pool, block_table[b % 2][:], table[:, b, :], one_b)
                src = head_q[:, par, first:first + N].rearrange("r (j u) -> r j u", u=P)
                pool.tensor_copy(block_q[b % 2][:], src[:, :, 0:BLOCK_U]).then_inc(block_ready, 1)

            pool.wait_ge(table_ready, 1)
            for h in range(2):
                load_head_q(h, h)
            for b in range(CHUNKS):
                copy_block(0, b, 0)
            copy_block(1, 0, 1)
            copy_window(0, 0, 0)
            copy_window(0, 1, 0)
            copy_block(1, 1, 1)

            def during(h, c, par, block, window):
                later = (c + 2) // CHUNKS
                if window:
                    copy_window(h + later, (c + 2) % CHUNKS, (par + later) % 2)
                if block:
                    copy_block(h + later + 1, (c + 2) % CHUNKS, (par + later + 1) % 2)

            with pool.Fori(0, HEADS // 2 - 1) as m:
                for par in range(2):
                    h = m * 2 + par
                    pool.wait_ge(block_ready, h * CHUNKS + CHUNKS)
                    load_head_q(h + 2, par)
                    for c in range(CHUNKS):
                        during(h, c, par, True, True)
            for c in range(CHUNKS):
                during(HEADS - 2, c, 0, c < CHUNKS - 2, True)
            for c in range(CHUNKS - 2):
                during(HEADS - 1, c, 1, False, True)

        @block.tensor
        def _(pe):
            def bank_free(n, bias, *use):
                at = SHARED_USES.index(use) - 3
                if not bias and at >= 0 and SHARED_USES[at][0] == "bias":
                    at -= 3
                m = n if at >= 0 else n - 1
                kind, i = SHARED_USES[at]
                if kind == "max":
                    pe.wait_ge(max_read, m * MAX_GROUPS + (MAX_GROUPS + LEAD + i + 3))
                elif kind == "bias":
                    pe.wait_ge(bias_read, (m + NEXT_GEN) * 2 + (i + 1))
                elif kind == "rows":
                    pe.wait_ge(max_placed, m + 2)
                else:
                    pe.wait_ge(normed, m + 2)

            def max_group(n, par, k, bank):
                t, g = k % TPC, k // TPC
                if k == 0:
                    pe.wait_ge(window_ready, n + 1)
                    pe.wait_ge(max_queries_in[par], (n // 2) * 16 + 16)
                if t == 0:
                    last_tile = TPC * g + 2 * TPC - 2
                    for j, (a, b, _) in enumerate(PIECES):
                        if a <= last_tile < b or (g == 0 and j == 0):
                            pe.wait_ge(keys_in[par][j], (n // 2) * 48 + 48)
                near = {0: [(0, t + 1, P), (1, t + 2, 0)],
                        TILES // TPC - 1: [(TPC - 1, t, 2 * P)]}.get(g, [])
                mm = pe.matmul(bank, max_queries[par][:, t * P:(t + 1) * P],
                               keys[par][0:ROWS, (t + TPC * g) * P:(t + TPC * (g + 1)) * P],
                               start=True, stop=not near)
                for i, (pos, slab, u) in enumerate(near):
                    mm = pe.matmul(bank[:, pos * P:(pos + 1) * P], near_window[par][:, slab, u:u + P],
                                   ident_b[:], start=False, stop=i == len(near) - 1)
                mm.then_inc(max_ready, 1)

            def max_to_rows(n, par):
                pe.wait_ge(max_cut, n + 3)
                for t in range(TPC):
                    mm = pe.matmul(shared("rows", 0)[ROWS:ROWS + MROWS, t * P:(t + 1) * P], max_parts[:, t, :],
                                   ident_b[:], start=True, stop=True)
                mm.then_inc(max_rows, 1)

            def score(n, par, c):
                s = c // 2
                if c == 0:
                    pe.wait_ge(queries_in[par], (n // 2) * 16 + 16)
                    pe.wait_ge(max_placed, n + 1)
                if c % 2 == 0:
                    pe.wait_ge(exp_done, n * PAIRS + s + 1)
                cut = min(c + 1, TPC) * P
                out = scores[s % 2][:, c % 2, :]
                mm = pe.matmul(out[:, 0:cut], keys[par][:, c * P:(c + 1) * P],
                               queries[par][:, 0:cut], start=True, stop=True)
                if cut < CH:
                    mm = pe.matmul(out[:, cut:CH], keys[par][:, (c + TILES) * P:(c + TILES + 1) * P],
                                   queries[par][:, cut:CH], start=True, stop=True)
                if c % 2 == 1:
                    mm.then_inc(scores_ready, 1)

            def pv_quad(n, par, q):
                if q == 0:
                    pe.wait_ge(values_in[par], (n // 2) * 16 + 16)
                    pe.wait_ge(out_copied, n + 1)
                pe.wait_ge(exp_done, n * PAIRS + 2 * q + 4)
                for i in range(4):
                    mm = pe.matmul(out_ps[32 * i:32 * i + VW, :], values[par][:, 4 * q + i, :],
                                   probs[(2 * q + i // 2) % 4][:, i % 2, :],
                                   start=q == 0, stop=q == QUADS - 1, skip_group_check=True)
                mm.then_inc(pv_done, 1)

            def make_bias(e, par, half):
                if half == 0:
                    pe.wait_ge(block_ready, e + 1)
                for i in range(UG):
                    u = half * UG + i
                    mm = pe.matmul(shared("bias", half)[:, i * TILES:(i + 1) * TILES],
                                   block_table[par][:, BLOCK_U - 1 - u:BLOCK_U - 1 - u + P],
                                   block_q[par][:, :, u], start=True, stop=True)
                mm.then_inc(bias_ready, 1)

            def sum_quadrants(n, par):
                pe.wait_ge(out_copied, n + 2)
                for t in range(TPC):
                    mm = pe.matmul(shared("sum", 0)[:, t * VW:(t + 1) * VW], out_copy[:, t * P:(t + 1) * P],
                                   sum_sel[:], start=True, stop=True)
                mm.then_inc(out_summed, 1)

            def max_slot(n, par, bias, slot, ahead):
                k = LEAD + slot
                if ahead < (1 if k < MAX_GROUPS else 2):
                    return
                bank_free(n, bias, "max", slot)
                bank = shared("max", slot)
                if k < MAX_GROUPS:
                    max_group(n + 1, 1 - par, k, bank)
                else:
                    max_group(n + 2, par, k - MAX_GROUPS, bank)

            def chunk(n, par, bias, ahead):
                for turn in range(QUADS):
                    pv_quad(n, par, turn)
                    for i in range(4):
                        slot = 4 * turn + i
                        if slot == ROWS_SLOT and ahead:
                            if ahead == 2:
                                bank_free(n, bias, "rows", 0)
                            max_to_rows(n + 1, 1 - par)
                        max_slot(n, par, bias, slot, ahead)
                        for c in SLOT_SCORES[i]:
                            if turn < QUADS - 2:
                                score(n, par, 4 * (turn + 2) + c)
                            elif ahead:
                                score(n + 1, 1 - par, 4 * (turn - QUADS + 2) + c)
                    if bias and turn < 2:
                        bank_free(n, bias, "bias", turn)
                        make_bias(n + NEXT_GEN, (par + NEXT_GEN) % 2, turn)
                if ahead == 2:
                    bank_free(n, bias, "sum", 0)
                else:
                    pe.wait_ge(max_placed, TOTAL)
                    pe.wait_ge(normed, n + 1)
                sum_quadrants(n, par)

            pe.wait_ge(consts_in, 48)
            pe.wait_ge(cleared, 10)
            pe.wait_ge(ident_ready, 4)
            for e in range(NEXT_GEN):
                for half in range(2):
                    if e:
                        pe.wait_ge(bias_read, e * 2 + half - 1)
                    make_bias(e, e % 2, half)
            pe.wait_ge(bias_read, 2 * NEXT_GEN)
            for k in range(MAX_GROUPS + LEAD):
                if k >= 3:
                    pe.wait_ge(max_read, k)
                max_group(k // MAX_GROUPS, k // MAX_GROUPS, k % MAX_GROUPS, shared_ps[k % 3][:])
            pe.wait_ge(max_read, MAX_GROUPS + LEAD + 2)
            max_to_rows(0, 0)
            for c in range(8):
                score(0, 0, c)
            last_bias = (TOTAL - NEXT_GEN) // 2
            with pe.Fori(0, last_bias) as m:
                for par in range(2):
                    chunk(m * 2 + par, par, True, 2)
            chunk(2 * last_bias, 0, True, 2)
            chunk(2 * last_bias + 1, 1, False, 2)
            with pe.Fori(last_bias + 1, TOTAL // 2 - 1) as m:
                for par in range(2):
                    chunk(m * 2 + par, par, False, 2)
            chunk(TOTAL - 2, 0, False, 1)
            chunk(TOTAL - 1, 1, False, 0)

        @block.scalar
        def _(act):
            act.preload_act_table(ACT.Exp)
            act.sem_inc(exp_done, 2)
            for semaphore in (out_copied, normed, out_summed, max_rows):
                act.sem_inc(semaphore, 1)

            def keep_bias(block_no, half):
                h, b = place(block_no)
                act.wait_ge(bias_ready, block_no * 2 + half + 1)
                act.activation(near_bias[:, bass.ds(h % 2, 1), 1:TILES + 1, bass.ds(b * BLOCK_U + half * UG, UG)],
                               shared("bias", half).rearrange("p (a u j) -> p a j u", a=1, u=UG), ACT.Copy
                               ).then_inc(bias_read, 1)

            def exp_pair(n, s):
                if s in (0, 1, 2, PAIRS - 1):
                    act.wait_ge(near_added, n * 4 + {0: 1, 1: 2, 2: 3, PAIRS - 1: 4}[s])
                act.wait_ge(scores_ready, n * PAIRS + s + 1)
                act.wait_ge(pv_done, n * QUADS + s // 2 + 1)
                act.activation(probs[s % 4][:], scores[s % 2][:], ACT.Exp).then_inc(exp_done, 1)

            def place_max(n, par):
                act.wait_ge(max_rows, n + 2)
                act.activation(queries[par][ROWS:ROWS + MROWS, :], shared("rows", 0)[ROWS:ROWS + MROWS, :], ACT.Copy
                               ).then_inc(max_placed, 1)

            def chunk(n, par, bias, more):
                for s in range(4, PAIRS):
                    if s == PAIRS - 2 and more:
                        place_max(n + 1, 1 - par)
                    exp_pair(n, s)
                    if bias and s in (5, 7):
                        if s == 5:
                            act.wait_ge(window_ready, n + 1)
                        keep_bias(n + NEXT_GEN, s // 7)
                for s in range(4):
                    if more:
                        exp_pair(n + 1, s)
                    if s == 1:
                        act.wait_ge(pv_done, n * QUADS + QUADS + 2)
                        act.wait_ge(out_summed, n + 1)
                        act.activation(out_copy[:], out_ps[:], ACT.Copy).then_inc(out_copied, 1)

            act.wait_ge(cleared, 10)
            for e in range(NEXT_GEN):
                for half in range(2):
                    keep_bias(e, half)
            place_max(0, 0)
            for s in range(4):
                exp_pair(0, s)
            last_bias = (TOTAL - NEXT_GEN) // 2
            with act.Fori(0, last_bias) as m:
                for par in range(2):
                    chunk(m * 2 + par, par, True, True)
            chunk(2 * last_bias, 0, True, True)
            chunk(2 * last_bias + 1, 1, False, True)
            with act.Fori(last_bias + 1, TOTAL // 2 - 1) as m:
                for par in range(2):
                    chunk(m * 2 + par, par, False, True)
            chunk(TOTAL - 2, 0, False, True)
            chunk(TOTAL - 1, 1, False, False)

        @block.vector
        def _(dve):
            dve.sem_inc(max_read, 2)
            dve.sem_inc(max_cut, 2)
            dve.sem_inc(pv_done, 2)
            dve.memset(out_ps[:], 0.0).then_inc(ident_ready, 1)
            for i in range(2):
                dve.memset(keys[i][ROWS:ROWS + MROWS, :], 1.0).then_inc(ident_ready, 1)
            dve.wait_ge(consts_in, 48)
            dve.tensor_copy(ident_b[:], ident_f[:]).then_inc(ident_ready, 1)
            for start, width, first in ((0, PAD, 0), (PAD, 2 * CLIP - 1, 1), (PAD + 2 * CLIP - 1, P, 2 * CLIP),
                                        (R_COLS, P, 0), (R_COLS + P, CLIP - 1, 1)):
                if first in (0, 2 * CLIP):
                    src = table_raw[:, first:first + 1].to_broadcast([D, width])
                else:
                    src = table_raw[:, first:first + width]
                ins = dve.tensor_copy(ext[:, start:start + width], src)
            ins.then_inc(max_step, 1)
            dve.wait_ge(max_step, 1)
            dve.tensor_scalar(ext[:, 0:R_COLS], ext[:, 0:R_COLS], table_raw[:, 2 * CLIP:2 * CLIP + 1], None,
                              ALU.subtract)
            dve.tensor_scalar(ext[:, R_COLS:], ext[:, R_COLS:], table_raw[:, 0:1], None,
                              ALU.subtract).then_inc(max_step, 1)
            dve.wait_ge(max_step, 2)
            dve.tensor_copy(ext_part[:, 0, :], ext[:]).then_inc(table_cut, 1)
            dve.wait_ge(table_cut, 1)
            dve.tensor_tensor(ext_rest[:], ext[:], ext_part[:, 0, :], ALU.subtract).then_inc(max_step, 1)
            dve.wait_ge(max_step, 3)
            dve.tensor_copy(ext_part[:, 1, :], ext_rest[:]).then_inc(table_cut, 1)
            dve.wait_ge(table_cut, 2)
            dve.tensor_tensor(ext_part[:, 2, :], ext_rest[:], ext_part[:, 1, :], ALU.subtract
                              ).then_inc(table_cut, 1)
            dve.wait_ge(table_rows_in, 16 * TERMS)
            for b in range(CHUNKS):
                if (b + 1) * BLOCK_U <= PAD + P:
                    first = P - 1 + PAD - b * BLOCK_U - (BLOCK_U - 1)
                else:
                    first = R_COLS + SLAB - 1 - b * BLOCK_U - (BLOCK_U - 1)
                ins = dve.tensor_copy(table[:, b, :], ext_rows[:, first:first + BLOCK_W])
            ins.then_inc(table_ready, 1)
            SETUP = 3

            def near_add(n, s):
                h, c = place(n)
                spans = {0: [(0, 0, 192, 1, 64), (1, 64, 320, 2, 0)],
                         1: [(0, 192, 448, 3, 0), (1, 320, 512, 4, 0)],
                         2: [(0, 448, 512, 5, 0)],
                         PAIRS - 1: [(1, 0, 64, 0, 192)]}[s]
                dve.wait_ge(scores_ready, n * PAIRS + s + 1)
                for tile, a, b, slab, u in spans:
                    part = scores[s % 2][:, tile, a:b]
                    ins = dve.tensor_tensor(part, part,
                                            near_bias[:, bass.ds(h % 2, 1), bass.ds(c * TPC + slab, 1), u:u + b - a],
                                            ALU.add)
                ins.then_inc(near_added, 1)

            def find_max(n, par):
                dve.wait_ge(max_read, n * MAX_GROUPS + MAX_GROUPS + 2)
                dve.tensor_reduce(row_max[:], group_max[par][:].rearrange("p (g t) -> p t g", t=TPC), AX.X,
                                  ALU.max).then_inc(max_step, 1)

            def cut_high(n, par):
                dve.wait_ge(max_step, n * 2 + SETUP + 1)
                dve.wait_ge(max_rows, n + 1)
                dve.tensor_scalar(max_parts[:, :, 0], row_max[:], -1.0, None, ALU.mult).then_inc(max_step, 1)

            def cut_low(n, par):
                dve.wait_ge(max_step, n * 2 + SETUP + 2)
                dve.scalar_tensor_tensor(out=max_parts[:, :, 1], in0=row_max[:], scalar=-1.0,
                                         in1=max_parts[:, :, 0], op0=ALU.mult, op1=ALU.subtract
                                         ).then_inc(max_cut, 1)

            def bank_max(n, par, k, bank):
                dve.wait_ge(max_ready, n * MAX_GROUPS + k + 1)
                dve.tensor_reduce(group_max[par][:, k:k + 1], bank, AX.X, ALU.max
                                  ).then_inc(max_read, 1)

            def finish(n):
                h, c = place(n)
                dve.wait_ge(out_summed, n + 2)
                summed = shared("sum", 0)[:, 0:TPC * VW].rearrange("p (t e) -> p t e", e=VW)
                dve.reciprocal(inv_sum[:], summed[:, :, D:VW]).then_inc(norm_step, 1)
                dve.wait_ge(norm_step, n + 1)
                dve.tensor_tensor(attn[:, bass.ds(c * TPC, TPC), bass.ds(h * D, D)], summed[:, :, 0:D],
                                  inv_sum[:].to_broadcast([P, TPC, D]), ALU.mult).then_inc(normed, 1)

            def chunk(n, par, ahead):
                for slot in range(MAX_GROUPS):
                    k = LEAD + slot
                    if slot == NEAR_SLOTS[3]:
                        near_add(n, PAIRS - 1)
                    if ahead and slot in NEAR_SLOTS[:3]:
                        near_add(n + 1, NEAR_SLOTS.index(slot))
                    if k < MAX_GROUPS and ahead >= 1:
                        bank_max(n + 1, 1 - par, k, shared("max", slot))
                    if k >= MAX_GROUPS and ahead >= 2:
                        bank_max(n + 2, par, k - MAX_GROUPS, shared("max", slot))
                    if ahead >= 1 and MAX_GROUPS - 1 <= k <= MAX_GROUPS + 1:
                        (find_max, cut_high, cut_low)[k - MAX_GROUPS + 1](n + 1, 1 - par)
                finish(n)

            for k in range(MAX_GROUPS):
                bank_max(0, 0, k, shared_ps[k % 3][:])
            find_max(0, 0)
            cut_high(0, 0)
            cut_low(0, 0)
            for k in range(LEAD):
                bank_max(1, 1, k, shared_ps[(MAX_GROUPS + k) % 3][:])
            for s in range(3):
                near_add(0, s)
            with dve.Fori(0, TOTAL // 2 - 1) as m:
                for par in range(2):
                    chunk(m * 2 + par, par, 2)
            chunk(TOTAL - 2, 0, 1)
            chunk(TOTAL - 1, 1, 0)


def layernorm_params(dve, pool, stats, mean, rstd, scratch, expo, step, first):
    tiles = stats.shape[1]
    if dve is not None:
        a, b = stats[:, :, 1], stats[:, :, 4]
        dve.tensor_tensor(mean, a, b, ALU.add).then_inc(step, 1)
        dve.tensor_tensor(scratch, a, b, ALU.subtract).then_inc(step, 1)
        dve.wait_ge(step, first + 2)
        dve.tensor_scalar(mean, mean, 0.5, None, ALU.mult).then_inc(step, 1)
        dve.tensor_tensor(scratch, scratch, scratch, ALU.mult).then_inc(step, 1)
        dve.tensor_tensor(rstd, stats[:, :, 2], stats[:, :, 5], ALU.add).then_inc(step, 1)
        dve.wait_ge(step, first + 5)
        dve.tensor_scalar(scratch, scratch, 0.25, LN_EPS, ALU.mult, ALU.add).then_inc(step, 1)
        dve.wait_ge(step, first + 6)
        dve.scalar_tensor_tensor(out=rstd, in0=rstd, scalar=1.0 / E, in1=scratch, op0=ALU.mult,
                                 op1=ALU.add).then_inc(step, 1)
    if pool is not None:
        pool.wait_ge(step, first + 7)
        pool.tensor_tensor(rstd, rstd, expo[:, 0:tiles], ALU.pow).then_inc(step, 1)
    return first + 8


def layernorm_params(dve, pool, stats, mean, rstd, scratch, expo, step, first):
    tiles = stats.shape[1]
    if dve is not None:
        a, b = stats[:, :, 1], stats[:, :, 4]
        dve.tensor_tensor(mean, a, b, ALU.add).then_inc(step, 1)
        dve.tensor_tensor(scratch, a, b, ALU.subtract).then_inc(step, 1)
        dve.wait_ge(step, first + 2)
        dve.tensor_scalar(mean, mean, 0.5, None, ALU.mult).then_inc(step, 1)
        dve.tensor_tensor(scratch, scratch, scratch, ALU.mult).then_inc(step, 1)
        dve.tensor_tensor(rstd, stats[:, :, 2], stats[:, :, 5], ALU.add).then_inc(step, 1)
        dve.wait_ge(step, first + 5)
        dve.tensor_scalar(scratch, scratch, 0.25, LN_EPS, ALU.mult, ALU.add).then_inc(step, 1)
        dve.wait_ge(step, first + 6)
        dve.scalar_tensor_tensor(out=rstd, in0=rstd, scalar=1.0 / E, in1=scratch, op0=ALU.mult,
                                 op1=ALU.add).then_inc(step, 1)
    if pool is not None:
        pool.wait_ge(step, first + 7)
        pool.tensor_tensor(rstd, rstd, expo[:, 0:tiles], ALU.pow).then_inc(step, 1)
    return first + 8


def join_heads(nc, x, w_out_T, b_out, ident, tokens, first_norm, first_stored):
    with ExitStack() as ctx:
        sb = lambda name, shape, dt=F32: ctx.enter_context(nc.sbuf_tensor(name, shape, dt))
        sem = lambda name: ctx.enter_context(nc.semaphore(name))
        weights = sb("out_weights", [P, KE, E])
        bias = sb("out_bias", [1, E])
        ones_row = sb("join_ones", [1, P])
        ident_f = sb("join_ident", [P, P])
        tile_in = sb("join_tile", [P, 2, E])
        tile_T = sb("join_tile_T", [P, 2, E])
        x_rows = sb("x_rows", [P, TILES, E])
        stats = sb("join_stats", [P, TILES, 6])
        mean, rstd, scratch, expo = (sb(f"join_{n}", [P, TILES]) for n in ("mean", "rstd", "scratch", "expo"))
        turned = [ctx.enter_context(nc.psum_tensor(f"join_turned{i}", [P, CH], F32)) for i in range(2)]
        joined = [ctx.enter_context(nc.psum_tensor(f"join_joined{i}", [P, CH], F32)) for i in range(2)]
        consts_in = sem("join_consts")
        ones_set = sem("join_ones_set")
        x_in = sem("join_x_in")
        picked = sem("picked")
        tile_turned = sem("tile_turned")
        tile_kept = sem("tile_kept")
        tile_joined = sem("tile_joined")
        summed = sem("summed")
        counted = sem("counted")
        step = sem("join_step")
        normed = sem("join_normed")
        block = ctx.enter_context(nc.Block())

        @block.sync
        def _(sp):
            sp.dma_start(weights[:], w_out_T.rearrange("(k p) n -> p k n", p=P)).then_inc(consts_in, 16)
            sp.dma_start(bias[:], b_out.rearrange("(a n) -> a n", a=1)).then_inc(consts_in, 16)
            sp.dma_start(ident_f[:], ident).then_inc(consts_in, 16)
            sp.dma_start(x_rows[:], x.rearrange("(t p) e -> p t e", p=P)).then_inc(x_in, 16)
            sp.wait_ge(normed, TILES)
            sp.dma_start(first_norm, tokens[:]).then_inc(first_stored, 16)

        @block.gpsimd
        def _(pool):
            pool.memset(expo[:], -0.5).then_inc(ones_set, 1)
            pool.sem_inc(tile_turned, 2)
            with pool.Fori(0, TILES // 2) as m:
                for par in range(2):
                    t = m * 2 + par
                    pool.wait_ge(tile_turned, t + 1)
                    pool.tensor_copy(tile_in[:, par, :], tokens[:, bass.ds(t, 1), :]).then_inc(picked, 1)
            pool.wait_ge(ones_set, 2)
            layernorm_params(None, pool, stats, mean[:], rstd[:], scratch[:], expo, step, 0)

        @block.tensor
        def _(pe):
            pe.wait_ge(consts_in, 48)
            pe.wait_ge(ones_set, 2)
            with pe.Fori(0, TILES // 2) as m:
                for par in range(2):
                    t = m * 2 + par
                    pe.wait_ge(picked, t + 1)
                    pe.wait_ge(tile_kept, t + 1)
                    for k in range(KE):
                        mm = pe.transpose(turned[par][:, k * P:(k + 1) * P],
                                          tile_in[:, par, k * P:(k + 1) * P], ident_f[:])
                    mm.then_inc(tile_turned, 1)
                    pe.wait_ge(tile_kept, t + 3)
                    pe.wait_ge(summed, t + 1)
                    for k in range(KE):
                        pe.matmul(joined[par][:, 0:E], tile_T[:, par, k * P:(k + 1) * P],
                                  weights[:, k, :], start=k == 0, stop=False)
                    pe.matmul(joined[par][:, 0:E], ones_row[:], bias[:], start=False, stop=True
                              ).then_inc(tile_joined, 1)

        @block.scalar
        def _(act):
            act.preload_act_table(ACT.Exp)
            act.sem_inc(tile_kept, 2)
            with act.Fori(0, TILES // 2) as m:
                for par in range(2):
                    t = m * 2 + par
                    act.wait_ge(tile_turned, t + 3)
                    act.wait_ge(summed, t + 1)
                    act.activation(tile_T[:, par, :], turned[par][:, 0:E], ACT.Copy).then_inc(tile_kept, 1)

        @block.vector
        def _(dve):
            dve.memset(ones_row[:], 1.0).then_inc(ones_set, 1)
            dve.sem_inc(summed, 2)
            dve.wait_ge(x_in, 16)
            with dve.Fori(0, TILES // 2) as m:
                for par in range(2):
                    t = m * 2 + par
                    dve.wait_ge(tile_joined, t + 1)
                    tile = tokens[:, bass.ds(t, 1), :]
                    dve.tensor_tensor(tile, joined[par][:, 0:E], x_rows[:, bass.ds(t, 1), :], ALU.add
                                      ).then_inc(summed, 1)
                    dve.wait_ge(summed, t + 3)
                    dve.bn_stats(stats[:, bass.ds(t, 1), :], tile).then_inc(counted, 1)
            dve.wait_ge(counted, TILES)
            end = layernorm_params(dve, None, stats, mean[:], rstd[:], scratch[:], expo, step, 0)
            dve.wait_ge(step, end)
            normalise(dve, tokens, mean, rstd, normed)

def normalise(dve, tokens, mean, rstd, normed):
    with dve.Fori(0, TILES) as t:
        tile = tokens[:, bass.ds(t, 1), :]
        dve.tensor_scalar(tile, tile, mean[:, bass.ds(t, 1)], rstd[:, bass.ds(t, 1)],
                          ALU.subtract, ALU.mult).then_inc(normed, 1)

DEPTH = 2
LHEADS = 8
LD = 64
INNER = LHEADS * LD
KI = INNER // P
HID = 682
HT = -(-HID // P)
HTAIL = HID - (HT - 1) * P
RING = 4
BATCH = 4
BATCHES = TILES // BATCH
QK_SCALE = 8.0


def local_layers(nc, w_qkv, qk_rows, w_o, ln_gb, w_1, b_1, w_2, b_2, rotary, masks, ident, tokens, first_norm,
                 first_stored, out):
    with ExitStack() as ctx:
        sb = lambda name, shape, dt=F32: ctx.enter_context(nc.sbuf_tensor(name, shape, dt))
        sem = lambda name: ctx.enter_context(nc.semaphore(name))
        bank = [ctx.enter_context(nc.psum_tensor(f"bank{i}", [P, CH], F32)) for i in range(4, 8)]
        quad = ctx.enter_context(nc.psum_tensor("quad", [P, 4, CH], F32))
        wqkv = sb("wqkv", [P, KE, 3 * INNER])
        wo = sb("wo", [P, KI, E])
        w1 = sb("w1", [P, KE, 2 * HID])
        w2 = sb("w2", [P, HT, E])
        b2 = sb("b2", [P, 1, E])
        b1 = sb("b1", [P, 2, HT])
        gb = sb("ln_gb", [P, 2, KE])
        qk_row = sb("qk_row", [P, 4 * LD])
        rot = sb("rot", [P, TILES, 4 * LD])
        mask = sb("mask", [P, 2, SLAB])
        ident_f = sb("layer_ident", [P, P])
        tile_in = [sb(f"win_tile{i}", [P, E]) for i in range(2)]
        hT_a = [sb(f"hT_a{i}", [P, P]) for i in range(2)]
        hT_b = [sb(f"hT_b{i}", [P, P + 1]) for i in range(2)]
        v_kept = [sb(f"v_kept{i}", [P, INNER]) for i in range(RING)]
        k_T = [sb(f"k_T{i}", [P, KI, P]) for i in range(2)]
        q_T = sb("q_T", [P, KI, P])
        squares = sb("squares", [P, 2 * LHEADS, LD])
        norm = sb("norm", [P, 2 * LHEADS, 1])
        turn = sb("turn", [P, 4 * LD])
        rot_a = sb("rot_a", [P, 2 * LHEADS, LD])
        rot_b = sb("rot_b", [P, 2 * LHEADS, LD])
        sim = sb("sim", [P, LHEADS, SLAB])
        prob = sb("prob", [P, LHEADS, SLAB])
        top = sb("top", [P, LHEADS])
        shift = sb("shift", [P, LHEADS])
        total = sb("total", [P, LHEADS, 1])
        inv_total = sb("inv_total", [P, LHEADS, 1])
        prob_T = sb("prob_T", [P, 2 * LHEADS, P])
        o_tok = sb("o_tok", [P, LHEADS, LD])
        o_T = sb("o_T", [P, KI, P])
        half_in = sb("half_in", [P, BATCH, P])
        half_T = sb("half_T", [P, BATCH * P + 1])
        h_tok = sb("h_tok", [P, BATCH, E])
        h_T = [sb(f"h_T{i}", [P, KE, CH]) for i in range(2)]
        gate = sb("gate", [P, 2, CH])
        hidden = sb("hidden", [P, HT, CH])
        stats = sb("layer_stats", [P, BATCH, 6])
        mean, rstd, scratch = (sb(f"layer_{n}", [P, BATCH]) for n in ("mean", "rstd", "scratch"))
        expo = sb("layer_expo", [P, TILES])
        one = sb("one", [P, 1, 1])
        end_stats = sb("end_stats", [P, TILES, 6])
        end_mean, end_rstd, end_scratch = (sb(f"end_{n}", [P, TILES]) for n in ("mean", "rstd", "scratch"))

        fixed_in = sem("fixed_in")
        set_up = sem("set_up")
        attn_w_in = sem("attn_w_in")
        ffn_w_in = sem("ffn_w_in")
        tables_in = sem("tables_in")
        names = ("tile_ready hT_ready hT_kept qkv_ready squared v_taken turn_ready turned_a turned_b norm_guard "
                 "norm_ready rot_sum k_added rotated qk_T_ready qk_T_kept sim_ready sim_kept top_ready shift_ready "
                 "exp_done prob_T_ready prob_T_act prob_T_dve pv_ready total_inv o_ready o_T_ready o_T_kept "
                 "wo_ready win_done "
                 "half_ready half_T_ready carried half_T_kept half_back h_left h_right h_stats step h_normed "
                 "h_T_ready h_T_kept up_ready gate_ready hidden_ready down_ready batch_done "
                 "past_cleared bias_added first_in end_added end_counted end_step end_normed stored").split()
        S = type("Semaphores", (), {n: sem("l_" + n) for n in names})
        from_one = (S.batch_done, S.down_ready, S.exp_done, S.h_T_kept, S.h_T_ready, S.h_right, S.half_back,
                    S.norm_guard, S.o_ready, S.prob_T_act, S.prob_T_dve, S.prob_T_ready, S.qk_T_kept,
                    S.qk_T_ready, S.rotated, S.total_inv, S.turned_b, S.v_taken, S.win_done, S.half_T_ready)
        block = ctx.enter_context(nc.Block())
        qk_ps = (bank[1], bank[2])
        v_ps = bank[3]
        o_ps = bank[0]
        LAYER = TILES

        def slot(h):
            return h // 4 * 4 + (h % 2) * 2 + h // 2 % 2

        def windows(eng, l, step):
            for w in range(RING):
                step(w, l * LAYER + w, w, w > 0, True)
            with eng.Fori(1, LAYER // RING - 1) as m:
                for i in range(RING):
                    step(m * RING + i, l * LAYER + m * RING + i, i, True, True)
            for w in range(LAYER - RING, LAYER):
                step(w, l * LAYER + w, w % RING, True, w < LAYER - 1)

        def batches(eng, l, step):
            with eng.Fori(0, BATCHES // 2 - 1) as m:
                for par in range(2):
                    step(m * 2 + par, l * BATCHES + m * 2 + par, par, True)
            step(BATCHES - 2, l * BATCHES + BATCHES - 2, 0, True)
            step(BATCHES - 1, l * BATCHES + BATCHES - 1, 1, False)

        @block.sync
        def _(sp):
            for semaphore in from_one:
                sp.sem_inc(semaphore, 1)
            sp.dma_start(ident_f[:], ident).then_inc(fixed_in, 16)
            sp.dma_start(mask[:], masks.rearrange("m p n -> p m n")).then_inc(fixed_in, 16)
            tables = rotary.rearrange("(t p) n -> p t n", p=P)
            sp.dma_start(rot[:, 0:RING, :], tables[:, 0:RING, :]).then_inc(fixed_in, 16)
            with sp.Fori(0, DEPTH) as l:
                sp.wait_ge(S.win_done, l * LAYER + 1)
                one = bass.ds(l, 1)
                sp.dma_start(wqkv[:], w_qkv[one].rearrange("a (k p) n -> p (a k) n", p=P)).then_inc(attn_w_in, 16)
                sp.dma_start(wo[:], w_o[one].rearrange("a (k p) n -> p (a k) n", p=P)).then_inc(attn_w_in, 16)
                sp.dma_start(qk_row[:], qk_rows[one].partition_broadcast(P)).then_inc(attn_w_in, 16)
                sp.wait_ge(S.batch_done, l * BATCHES + 1)
                sp.dma_start(w1[:], w_1[one].rearrange("a (k p) n -> p (a k) n", p=P)).then_inc(ffn_w_in, 16)
                full = (HT - 1) * P
                sp.dma_start(w2[:, 0:HT - 1, :], w_2[one, 0:full].rearrange("a (k p) n -> p (a k) n", p=P)
                             ).then_inc(ffn_w_in, 16)
                sp.dma_start(w2[0:HTAIL, HT - 1, :], w_2[one, full:HID].rearrange("a p n -> p (a n)")
                             ).then_inc(ffn_w_in, 16)
                for side in range(2):
                    at = side * HID
                    sp.dma_start(b1[:, side, 0:HT - 1], b_1[one, at:at + full].rearrange("a (k p) -> p (a k)", p=P),
                                 allow_slow_non_contiguous=True).then_inc(ffn_w_in, 16)
                    sp.dma_start(b1[0:HTAIL, side, HT - 1:HT],
                                 b_1[one, at + full:at + HID].rearrange("a p -> p a"),
                                 allow_slow_non_contiguous=True).then_inc(ffn_w_in, 16)
                sp.dma_start(b2[:], b_2[one].partition_broadcast(P)).then_inc(ffn_w_in, 16)
                sp.dma_start(gb[:], ln_gb[one].rearrange("a g (k p) -> p (a g) k", p=P),
                             allow_slow_non_contiguous=True).then_inc(ffn_w_in, 16)
            sp.wait_ge(S.win_done, DEPTH * LAYER + 1)
            sp.wait_ge(first_stored, 16)
            sp.dma_start(rot[:], first_norm).then_inc(S.first_in, 16)
            QUARTER = TILES // 4
            for i in range(4):
                sp.wait_ge(S.end_normed, (i + 1) * QUARTER)
                sp.dma_start(out.rearrange("(t p) e -> p t e", p=P)[:, i * QUARTER:(i + 1) * QUARTER, :],
                             tokens[:, i * QUARTER:(i + 1) * QUARTER, :]).then_inc(S.stored, 16)
            sp.wait_ge(S.stored, 64)
        FFN_DMAS = 9 * 16

        @block.gpsimd
        def _(pool):
            pool.memset(expo[:], -0.5).then_inc(set_up, 1)
            pool.memset(one[:], 1.0).then_inc(set_up, 1)
            pool.memset(k_T[1][:], 0.0).then_inc(set_up, 1)
            pool.memset(v_kept[RING - 1][:], 0.0).then_inc(set_up, 1)
            pool.wait_ge(set_up, 5)

            def pick(w, g, par):
                pool.wait_ge(S.hT_ready, g + 1)
                same(pool, tile_in[par][:].rearrange("p (a n) -> p a n", a=1), tokens[:, bass.ds(w, 1), :], one
                     ).then_inc(S.tile_ready, 1)

            def load_tables():
                pool.wait_ge(attn_w_in, 48)
                pool.dma_start(rot[:, RING:, :], rotary.rearrange("(t p) n -> p t n", p=P)[:, RING:, :]
                               ).then_inc(tables_in, 16)

            def rotate(g):
                pool.wait_ge(S.norm_guard, g + 2)
                pool.tensor_tensor(norm[:], norm[:], expo[:, 0:2 * LHEADS].rearrange("p (h a) -> p h a", a=1),
                                   ALU.pow).then_inc(S.norm_ready, 1)
                pool.wait_ge(S.turned_b, g * 2 + 2)
                pool.tensor_tensor(rot_a[:, 0:LHEADS, :], rot_a[:, 0:LHEADS, :], rot_b[:, 0:LHEADS, :], ALU.add
                                   ).then_inc(S.rot_sum, 1)

            def window(w, g, at, before, more):
                if more:
                    pick(w + 1, g + 1, (at + 1) % 2)
                    rotate(g + 1)

            def take_half(b, g):
                pool.wait_ge(S.half_T_ready, g + 1)
                same(pool, half_in[:], tokens[:, bass.ds(b * BATCH, BATCH), P:E], one).then_inc(S.half_ready, 1)
                pool.wait_ge(S.h_T_ready, g * 2 + 1)
                same(pool, h_tok[:, :, 0:P], tokens[:, bass.ds(b * BATCH, BATCH), 0:P], one).then_inc(S.h_left, 1)
                layernorm_params(None, pool, stats, mean[:], rstd[:], scratch[:], expo, S.step, g * 8)

            load_tables()
            with pool.Fori(0, DEPTH) as l:
                pool.wait_ge(S.batch_done, l * BATCHES + 1)
                pick(0, l * LAYER, 0)
                rotate(l * LAYER)
                windows(pool, l, window)
                pool.wait_ge(S.win_done, l * LAYER + LAYER + 1)
                take_half(0, l * BATCHES)
                batches(pool, l, lambda b, g, par, more: take_half(b + 1, g + 1) if more else None)
            layernorm_params(None, pool, end_stats, end_mean[:], end_rstd[:], end_scratch[:], expo, S.end_step, 0)

        @block.tensor
        def _(pe):
            def turn_tile(g, par):
                pe.wait_ge(S.tile_ready, g + 1)
                pe.wait_ge(S.v_taken, g + 1)
                for k in range(KE):
                    mm = pe.transpose(v_ps[:, k * P:(k + 1) * P], tile_in[par][:, k * P:(k + 1) * P], ident_f[:])
                mm.then_inc(S.hT_ready, 1)

            def project(g, par):
                pe.wait_ge(S.hT_kept, g + 1)
                pe.wait_ge(S.qk_T_kept, g + 1)
                for j, ps in enumerate((*qk_ps, v_ps)):
                    for k, h in enumerate((hT_a[par][:], hT_b[par][:, 0:P])):
                        mm = pe.matmul(ps[:], h, wqkv[:, k, j * INNER:(j + 1) * INNER],
                                       start=k == 0, stop=k == KE - 1)
                    mm.then_inc(S.qkv_ready, 1)

            def turn_qk(g):
                pe.wait_ge(S.rotated, g + 2)
                for j in range(2):
                    for i in range(KI):
                        mm = pe.transpose(qk_ps[j][:, i * P:(i + 1) * P],
                                          rot_a[:].rearrange("p h d -> p (h d)")[:, (j * KI + i) * P:(j * KI + i + 1) * P],
                                          ident_f[:])
                mm.then_inc(S.qk_T_ready, 1)

            def similarities(g, par):
                pe.wait_ge(S.qk_T_kept, g + 2)
                pe.wait_ge(S.prob_T_act, g + 1)
                pe.wait_ge(S.prob_T_dve, g + 1)
                for pair in range(LHEADS // 2):
                    for c, keys, h in [(c, keys, 2 * pair + odd) for c, keys in enumerate((k_T[1 - par], k_T[par]))
                                       for odd in range(2)]:
                        rows = slice(LD * (h % 2), LD * (h % 2 + 1))
                        at = (slot(h) % 2) * SLAB + c * P
                        mm = pe.matmul(quad[:, slot(h) // 2, at:at + P], q_T[rows, h // 2, :], keys[rows, h // 2, :],
                                       start=True, stop=True)
                    if pair % 2 == 1:
                        mm.then_inc(S.sim_ready, 1)

            def turn_prob(g):
                for h in range(LHEADS):
                    if h % 4 == 0:
                        pe.wait_ge(S.exp_done, g * 2 + 1 + h // 4 + 1)
                    for c in range(2):
                        j = 2 * h + c
                        mm = pe.transpose(quad[:, j // 4, (j % 4) * P:(j % 4 + 1) * P],
                                          prob[:, h, c * P:(c + 1) * P], ident_f[:])
                    if h % 4 == 3:
                        mm.then_inc(S.prob_T_ready, 1)

            def weigh(g, at):
                pe.wait_ge(S.prob_T_act, g + 2)
                pe.wait_ge(S.prob_T_dve, g + 2)
                pe.wait_ge(S.win_done, g + 1)
                for h in range(LHEADS):
                    for c, v in enumerate((v_kept[at - 1], v_kept[at])):
                        j = slot(h)
                        mm = pe.matmul(o_ps[:, j * LD:(j + 1) * LD], prob_T[:, 2 * j + c, :],
                                       v[:, h * LD:(h + 1) * LD], start=c == 0, stop=c == 1)
                mm.then_inc(S.pv_ready, 1)

            def turn_o(g):
                pe.wait_ge(S.o_ready, g + 2)
                for i in range(KI):
                    mm = pe.transpose(o_ps[:, i * P:(i + 1) * P],
                                      o_tok[:].rearrange("p h d -> p (h d)")[:, i * P:(i + 1) * P], ident_f[:])
                mm.then_inc(S.o_T_ready, 1)

            def project_o(g):
                pe.wait_ge(S.o_T_kept, g + 1)
                for i in range(KI):
                    mm = pe.matmul(o_ps[:, 0:E], o_T[:, i, :], wo[:, i, :], start=i == 0, stop=i == KI - 1)
                mm.then_inc(S.wo_ready, 1)

            def window(w, g, at, before, more):
                par = at % 2
                if more:
                    turn_tile(g + 1, 1 - par)
                similarities(g, par)
                if more:
                    project(g + 1, 1 - par)
                if before:
                    weigh(g - 1, (at - 1) % RING)
                turn_prob(g)
                if before:
                    turn_o(g - 1)
                if more:
                    turn_qk(g + 1)
                if before:
                    project_o(g - 1)
                if not more:
                    weigh(g, at)
                    turn_o(g)
                    project_o(g)

            turned, back, h_ps = bank[0], bank[0], bank[1]
            down = (bank[2], bank[3])

            def turn_half(g):
                pe.wait_ge(S.half_ready, g + 1)
                pe.wait_ge(S.h_right, g + 1)
                for i in range(BATCH):
                    mm = pe.transpose(turned[:, i * P:(i + 1) * P], half_in[:, i, :], ident_f[:])
                mm.then_inc(S.half_T_ready, 1)

            def turn_back(g):
                pe.wait_ge(S.half_T_kept, g + 1)
                for i in range(BATCH):
                    mm = pe.transpose(back[:, i * P:(i + 1) * P], half_T[:, i * P:(i + 1) * P], ident_f[:])
                mm.then_inc(S.half_back, 1)

            def turn_h(g, k):
                if k == 0:
                    pe.wait_ge(S.h_normed, g + 1)
                pe.wait_ge(S.h_T_kept, g * 2 + k + 1)
                for i in range(BATCH):
                    mm = pe.transpose(h_ps[:, i * P:(i + 1) * P], h_tok[:, i, k * P:(k + 1) * P], ident_f[:])
                mm.then_inc(S.h_T_ready, 1)

            def up(g, par, i):
                rows = P if i < HT - 1 else HTAIL
                if i == 0:
                    pe.wait_ge(S.h_T_kept, g * 2 + 3)
                pe.wait_ge(S.hidden_ready, g * HT + i + 1)
                for side in range(2):
                    at = side * HID + i * P
                    for k in range(KE):
                        mm = pe.matmul(quad[0:rows, 2 * (i % 2) + side, :], w1[:, k, at:at + rows], h_T[par][:, k, :],
                                       start=k == 0, stop=k == KE - 1)
                mm.then_inc(S.up_ready, 1)

            def go_down(g):
                pe.wait_ge(S.hidden_ready, g * HT + HT + 1)
                pe.wait_ge(S.batch_done, g + 1)
                for w in range(BATCH):
                    res = down[w // 2][:, (w % 2) * E:(w % 2 + 1) * E]
                    for i in range(HT):
                        rows = P if i < HT - 1 else HTAIL
                        if w == 0 and i == HT - 1:
                            pe.wait_ge(S.hidden_ready, g * HT + HT + 2)
                        mm = pe.matmul(res, hidden[0:rows, i, w * P:(w + 1) * P], w2[0:rows, i, :],
                                       start=i == 0, stop=i == HT - 1)
                mm.then_inc(S.down_ready, 1)

            def batch(b, g, par, more):
                for i in range(HT):
                    up(g, par, i)
                    if more and i == 0:
                        turn_half(g + 1)
                    if more and i == 1:
                        turn_back(g + 1)
                    if more and i >= HT - 2:
                        turn_h(g + 1, i - (HT - 2))
                go_down(g)

            pe.wait_ge(fixed_in, 48)
            pe.wait_ge(set_up, 5)
            with pe.Fori(0, DEPTH) as l:
                pe.wait_ge(attn_w_in, l * 48 + 48)
                turn_tile(l * LAYER, 0)
                project(l * LAYER, 0)
                turn_qk(l * LAYER)
                windows(pe, l, window)
                pe.wait_ge(S.win_done, l * LAYER + LAYER + 1)
                pe.wait_ge(ffn_w_in, l * FFN_DMAS + FFN_DMAS)
                turn_half(l * BATCHES)
                turn_back(l * BATCHES)
                turn_h(l * BATCHES, 0)
                turn_h(l * BATCHES, 1)
                batches(pe, l, batch)
                pe.wait_ge(S.batch_done, l * BATCHES + BATCHES + 1)

        @block.scalar
        def _(act):
            def keep_hT(g, par):
                act.wait_ge(S.hT_ready, g + 3)
                act.activation(hT_a[par][:], v_ps[:, 0:P], ACT.Copy)
                act.activation(hT_b[1 - par][:, 0:1], v_ps[:, 2 * P - 1:2 * P], ACT.Copy)
                act.activation(hT_b[par][:, 1:P + 1], v_ps[:, P:2 * P], ACT.Copy).then_inc(S.hT_kept, 1)

            def square(g):
                act.wait_ge(S.norm_guard, g + 1)
                for j in range(2):
                    act.wait_ge(S.qkv_ready, g * 3 + j + 1)
                    act.activation(squares[:, j * LHEADS:(j + 1) * LHEADS, :],
                                   qk_ps[j][:].rearrange("p (h d) -> p h d", d=LD), ACT.Square
                                   ).then_inc(S.squared, 1)

            def take_v(g, at):
                act.wait_ge(S.qkv_ready, g * 3 + 3)
                act.activation(v_kept[at][:], v_ps[:], ACT.Copy).then_inc(S.v_taken, 1)

            def keep_qk(g, par):
                act.wait_ge(S.qk_T_ready, g + 2)
                act.activation(q_T[:].rearrange("p i n -> p (i n)"), qk_ps[0][:], ACT.Copy)
                act.activation(k_T[par][:].rearrange("p i n -> p (i n)"), qk_ps[1][:], ACT.Copy
                               ).then_inc(S.qk_T_kept, 1)

            def exps(g):
                act.wait_ge(S.shift_ready, g + 1)
                act.wait_ge(S.prob_T_ready, g * 2 + 1)
                act.wait_ge(S.total_inv, g + 1)
                for h in range(LHEADS):
                    ins = act.activation(prob[:, h, :], sim[:, h, :], ACT.Exp, bias=shift[:, h:h + 1],
                                         scale=QK_SCALE, accum_out=total[:, h, :])
                    if h % 4 == 3:
                        ins.then_inc(S.exp_done, 1)

            def keep_o(g):
                act.wait_ge(S.o_T_ready, g + 1)
                act.activation(o_T[:].rearrange("p i n -> p (i n)"), o_ps[:], ACT.Copy).then_inc(S.o_T_kept, 1)

            def window(w, g, at, before, more):
                par = at % 2
                if more:
                    keep_hT(g + 1, 1 - par)
                    square(g + 1)
                exps(g)
                if more:
                    take_v(g + 1, (at + 1) % RING)
                act.wait_ge(S.prob_T_ready, g * 2 + 2)
                act.activation(prob_T[:, 0:LHEADS, :].rearrange("p (a b) n -> p a (b n)", a=2), quad[:, 0:2, :],
                               ACT.Copy).then_inc(S.prob_T_act, 1)
                if before:
                    keep_o(g - 1)
                if more:
                    keep_qk(g + 1, 1 - par)
                else:
                    keep_o(g)

            def keep_half(g):
                act.wait_ge(S.half_T_ready, g + 2)
                act.wait_ge(S.half_back, g + 1)
                act.activation(half_T[:, 0:1], half_T[:, BATCH * P:BATCH * P + 1], ACT.Copy).then_inc(S.carried, 1)
                act.wait_ge(S.carried, g + 1)
                act.activation(half_T[:, 1:BATCH * P + 1], bank[0][:], ACT.Copy).then_inc(S.half_T_kept, 1)

            def keep_h(g, par, k):
                act.wait_ge(S.h_T_ready, g * 2 + k + 2)
                act.activation(h_T[par][:, k, :], bank[1][:], ACT.Identity, scale=gb[:, 0, k:k + 1],
                               bias=gb[:, 1, k:k + 1]).then_inc(S.h_T_kept, 1)

            def batch(b, g, par, more):
                for i in range(HT):
                    rows = P if i < HT - 1 else HTAIL
                    act.wait_ge(S.up_ready, g * HT + i + 1)
                    act.wait_ge(S.hidden_ready, g * HT + i + 1)
                    act.activation(gate[0:rows, i % 2, :], quad[0:rows, 2 * (i % 2) + 1, :], ACT.Gelu,
                                   bias=b1[0:rows, 1, i:i + 1]).then_inc(S.gate_ready, 1)
                    if more and i == 0:
                        keep_half(g + 1)
                    if more and i >= HT - 2:
                        keep_h(g + 1, 1 - par, i - (HT - 2))

            act.wait_ge(set_up, 5)
            with act.Fori(0, DEPTH) as l:
                act.preload_act_table(ACT.Exp)
                act.wait_ge(S.past_cleared, l + 1)
                keep_hT(l * LAYER, 0)
                square(l * LAYER)
                take_v(l * LAYER, 0)
                keep_qk(l * LAYER, 0)
                windows(act, l, window)
                act.preload_act_table(ACT.Gelu)
                keep_half(l * BATCHES)
                act.wait_ge(ffn_w_in, l * FFN_DMAS + FFN_DMAS)
                keep_h(l * BATCHES, 0, 0)
                keep_h(l * BATCHES, 0, 1)
                batches(act, l, batch)

        @block.vector
        def _(dve):
            dve.memset(squares[:], 0.0).then_inc(set_up, 1)
            dve.sem_inc(S.hT_ready, 2)
            dve.sem_inc(S.hidden_ready, 2)

            def scale_table(w, g):
                dve.wait_ge(S.turned_b, g * 2 + 1)
                if isinstance(w, int) and w == RING:
                    dve.wait_ge(tables_in, 16)
                dve.tensor_tensor(turn[:], rot[:, bass.ds(w, 1), :], qk_row[:], ALU.mult).then_inc(S.turn_ready, 1)

            def scale_rotate(g):
                dve.wait_ge(S.turn_ready, g + 1)
                dve.wait_ge(S.qk_T_ready, g + 1)
                LH = LD // 2
                for j in range(2):
                    dve.wait_ge(S.squared, g * 2 + j + 1)
                    qk = qk_ps[j][:].rearrange("p (h d) -> p h d", d=LD)
                    heads = slice(j * LHEADS, (j + 1) * LHEADS)
                    cos = turn[:, j * LD:(j + 1) * LD].rearrange("p (a d) -> p a d", a=1)
                    sin = turn[:, (2 + j) * LD:(3 + j) * LD].rearrange("p (a d) -> p a d", a=1)
                    dve.tensor_tensor(rot_a[:, heads, :], qk, cos.to_broadcast([P, LHEADS, LD]), ALU.mult)
                    dve.tensor_tensor(rot_b[:, heads, 0:LH], qk[:, :, LH:LD],
                                      sin[:, :, 0:LH].to_broadcast([P, LHEADS, LH]), ALU.mult)
                    dve.tensor_tensor(rot_b[:, heads, LH:LD], qk[:, :, 0:LH],
                                      sin[:, :, LH:LD].to_broadcast([P, LHEADS, LH]), ALU.mult
                                      ).then_inc(S.turned_b, 1)

            def sum_squares(g):
                dve.wait_ge(S.squared, g * 2 + 2)
                dve.wait_ge(S.rotated, g + 1)
                dve.tensor_reduce(norm[:, :, 0], squares[:], AX.X, ALU.add).then_inc(S.turned_a, 1)
                dve.wait_ge(S.turned_a, g + 1)
                dve.tensor_scalar(norm[:], norm[:], 1e-24, None, ALU.max).then_inc(S.norm_guard, 1)

            def add_k(g):
                dve.wait_ge(S.turned_b, g * 2 + 3)
                dve.tensor_tensor(rot_a[:, LHEADS:, :], rot_a[:, LHEADS:, :], rot_b[:, LHEADS:, :], ALU.add
                                  ).then_inc(S.k_added, 1)

            def divide_norm(g):
                dve.wait_ge(S.k_added, g + 1)
                dve.wait_ge(S.rot_sum, g + 1)
                dve.wait_ge(S.norm_ready, g + 1)
                dve.tensor_tensor(rot_a[:], rot_a[:], norm[:].to_broadcast([P, 2 * LHEADS, LD]), ALU.mult
                                  ).then_inc(S.rotated, 1)

            def divide_o(g):
                dve.wait_ge(S.pv_ready, g + 1)
                dve.wait_ge(S.total_inv, g + 2)
                for half in range(2):
                    heads = slice(4 * half, 4 * half + 4)
                    ins = dve.tensor_tensor(o_tok[:, heads, :].rearrange("p (a b) d -> p b a d", b=2),
                                            o_ps[:, half * 4 * LD:(half + 1) * 4 * LD]
                                            .rearrange("p (b a d) -> p b a d", b=2, d=LD),
                                            inv_total[:, heads, :].rearrange("p (b a) d -> p b a d", b=2)
                                            .to_broadcast([P, 2, 2, LD]), ALU.mult)
                ins.then_inc(S.o_ready, 1)

            def add_o(w, g):
                dve.wait_ge(S.wo_ready, g + 1)
                tile = tokens[:, bass.ds(w, 1), :]
                dve.tensor_tensor(tile, o_ps[:, 0:E], tile, ALU.add).then_inc(S.win_done, 1)

            def window(w, g, at, before, more):
                which = (w + TILES - 1) // TILES
                dve.wait_ge(S.exp_done, g * 2 + 1)
                for i in range(2):
                    dve.wait_ge(S.sim_ready, g * 2 + i + 1)
                    half = slice(2 * i, 2 * i + 2)
                    dve.tensor_tensor(sim[:].rearrange("p (a b) n -> p a b n", b=2)[:, half],
                                      quad[:].rearrange("p a (b n) -> p a b n", b=2)[:, half],
                                      mask[:, bass.ds(which, 1), :].rearrange("p (a b) n -> p a b n", b=1)
                                      .to_broadcast([P, 2, 2, SLAB]), ALU.add).then_inc(S.sim_kept, 1)
                dve.wait_ge(S.sim_kept, g * 2 + 2)
                dve.tensor_reduce(top[:], sim[:], AX.X, ALU.max).then_inc(S.top_ready, 1)
                dve.wait_ge(S.top_ready, g + 1)
                dve.tensor_scalar(shift[:], top[:], -QK_SCALE, None, ALU.mult).then_inc(S.shift_ready, 1)
                if more:
                    scale_table(w + 1, g + 1)
                    sum_squares(g + 1)
                    scale_rotate(g + 1)
                if before:
                    divide_o(g - 1)
                if more:
                    add_k(g + 1)
                    divide_norm(g + 1)
                dve.wait_ge(S.exp_done, g * 2 + 3)
                dve.wait_ge(S.o_ready, g + 1)
                dve.reciprocal(inv_total[:], total[:]).then_inc(S.total_inv, 1)
                dve.wait_ge(S.prob_T_ready, g * 2 + 3)
                dve.tensor_copy(prob_T[:, LHEADS:, :].rearrange("p (a b) n -> p a (b n)", a=2), quad[:, 2:4, :]
                                ).then_inc(S.prob_T_dve, 1)
                if before:
                    add_o(w - 1, g - 1)
                if not more:
                    divide_o(g)
                    add_o(w, g)

            def count_batch(g):
                dve.wait_ge(S.half_back, g + 2)
                dve.wait_ge(S.h_left, g + 1)
                dve.tensor_copy(h_tok[:, :, P:E], bank[0][:].rearrange("p (b n) -> p b n", n=P)).then_inc(S.h_right, 1)
                dve.wait_ge(S.h_right, g + 2)
                for i in range(BATCH):
                    ins = dve.bn_stats(stats[:, i, :], h_tok[:, i, :])
                ins.then_inc(S.h_stats, 1)
                dve.wait_ge(S.h_stats, g + 1)
                layernorm_params(dve, None, stats, mean[:], rstd[:], scratch[:], expo, S.step, g * 8)

            def norm_batch(g):
                dve.wait_ge(S.step, g * 8 + 8)
                for i in range(BATCH):
                    ins = dve.tensor_scalar(h_tok[:, i, :], h_tok[:, i, :], mean[:, i:i + 1], rstd[:, i:i + 1],
                                            ALU.subtract, ALU.mult)
                ins.then_inc(S.h_normed, 1)

            def batch(b, g, par, more):
                for i in range(HT):
                    rows = P if i < HT - 1 else HTAIL
                    dve.wait_ge(S.gate_ready, g * HT + i + 1)
                    if i == 0:
                        dve.wait_ge(S.down_ready, g + 1)
                    dve.scalar_tensor_tensor(out=hidden[0:rows, i, :], in0=quad[0:rows, 2 * (i % 2), :],
                                             scalar=b1[0:rows, 0, i:i + 1], in1=gate[0:rows, i % 2, :],
                                             op0=ALU.add, op1=ALU.mult).then_inc(S.hidden_ready, 1)
                    if more and i == 2:
                        count_batch(g + 1)
                    if more and i == 3:
                        norm_batch(g + 1)
                whole = tokens[:, bass.ds(b * BATCH, BATCH), :]
                dve.tensor_tensor(whole, whole, b2[:].to_broadcast([P, BATCH, E]), ALU.add).then_inc(S.bias_added, 1)
                dve.wait_ge(S.bias_added, g + 1)
                dve.wait_ge(S.down_ready, g + 2)
                for j in range(2):
                    tiles = tokens[:, bass.ds(b * BATCH + 2 * j, 2), :]
                    ins = dve.tensor_tensor(tiles, bank[2 + j][:].rearrange("p (b n) -> p b n", n=E), tiles, ALU.add)
                ins.then_inc(S.batch_done, 1)

            dve.wait_ge(fixed_in, 48)
            dve.wait_ge(first_stored, 16)
            with dve.Fori(0, DEPTH) as l:
                dve.memset(hT_b[0][:, 0:1], 0.0)
                dve.memset(half_T[:, BATCH * P:BATCH * P + 1], 0.0).then_inc(S.past_cleared, 1)
                dve.wait_ge(attn_w_in, l * 48 + 48)
                scale_table(0, l * LAYER)
                sum_squares(l * LAYER)
                scale_rotate(l * LAYER)
                add_k(l * LAYER)
                divide_norm(l * LAYER)
                windows(dve, l, window)
                dve.wait_ge(ffn_w_in, l * FFN_DMAS + FFN_DMAS)
                count_batch(l * BATCHES)
                norm_batch(l * BATCHES)
                batches(dve, l, batch)
            dve.wait_ge(S.batch_done, DEPTH * BATCHES + 1)
            dve.wait_ge(S.first_in, 16)
            with dve.Fori(0, TILES) as t:
                tile = tokens[:, bass.ds(t, 1), :]
                dve.tensor_tensor(tile, tile, rot[:, bass.ds(t, 1), :], ALU.add).then_inc(S.end_added, 1)
                dve.wait_ge(S.end_added, t + 1)
                dve.bn_stats(end_stats[:, bass.ds(t, 1), :], tokens[:, bass.ds(t, 1), :]).then_inc(S.end_counted, 1)
            dve.wait_ge(S.end_counted, TILES)
            end = layernorm_params(dve, None, end_stats, end_mean[:], end_rstd[:], end_scratch[:], expo,
                                   S.end_step, 0)
            dve.wait_ge(S.end_step, end)
            normalise(dve, tokens, end_mean, end_rstd, S.end_normed)

def build(nc, ins, out):
    q_stack = nc.dram_tensor("q_stack", [HEADS, ROWS, N], BF16, kind="Internal").ap()
    k_parts = nc.dram_tensor("k_parts", [HEADS, 3 * D, 2 * N], BF16, kind="Internal").ap()
    v_wide = nc.dram_tensor("v_wide", [HEADS, P, 2 * TILES * VW], F32, kind="Internal").ap()
    first_norm = nc.dram_tensor("first_norm", [P, TILES, E], F32, kind="Internal").ap()
    with ExitStack() as ctx:
        project_heads(nc, ins["x_T"], ins["w_in_T"], ins["b_in"], ins["pe_edges"], q_stack, k_parts, v_wide)
        first_stored = ctx.enter_context(nc.semaphore("first_stored"))
        tokens = ctx.enter_context(nc.sbuf_tensor("tokens", [P, TILES, E], F32))
        attend(nc, q_stack, k_parts, v_wide, ins["rel_T"], ins["ident"], ins["part_sum"], tokens)
        join_heads(nc, ins["x"], ins["w_out_T"], ins["b_out"], ins["ident"], tokens, first_norm,
                   first_stored)
        local_layers(nc, ins["w_qkv"], ins["qk_rows"], ins["w_o"], ins["ln_gb"], ins["w_1"], ins["b_1"],
                     ins["w_2"], ins["b_2"], ins["rotary"], ins["masks"], ins["ident"], tokens, first_norm,
                     first_stored, out)

def shape_constants():
    import numpy as np
    f = np.float32
    half = np.arange(0, LD, 2, dtype=f)
    inv_freq = f(1.0) / np.power(f(10000.0), half / f(LD), dtype=f)
    t = np.arange(N, dtype=f)
    freqs = t[:, None] * inv_freq[None, :]
    base = (half + f(0.4 * LD)) / f(1.4 * LD)
    power = (t - f(N // 2)) / f(P // 2)
    scale = np.power(base[None, :], power[:, None], dtype=f)
    cos, sin = np.cos(freqs), np.sin(freqs)
    both = lambda a, b: np.concatenate([a, b], axis=1)
    rotary = np.concatenate([both(cos * scale, cos * scale), both(cos / scale, cos / scale),
                             both(-sin * scale, sin * scale), both(-sin / scale, sin / scale)], axis=1)
    i, j = np.arange(P)[:, None], np.arange(SLAB)[None, :] - P
    hidden = (i < j) | (i > j + P)
    masks = np.stack([hidden | (j < 0), hidden]) * f(-3e37)
    part_sum = np.zeros((P, VW), f)
    for quadrant in range(0, P, 32):
        part_sum[quadrant:quadrant + VW] = np.eye(VW, dtype=f)
    return {"rotary": rotary.astype(f), "masks": masks.astype(f), "part_sum": part_sum,
            "ident": np.eye(P, dtype=f)}

def kernel(**inputs):
    import numpy as np
    import concourse.bacc as bacc
    from concourse.bass_utils import run_bass_kernel_spmd

    g = {k: np.asarray(v) for k, v in inputs.items()}
    x = g["L0_attn_q"].reshape(N, E)
    pe = g["L0_attn_rel_pe"]
    qs, ks = g["L0_ffn_q_scale"], g["L0_ffn_k_scale"]
    swap = lambda a: np.concatenate([a[:, LD // 2:], a[:, :LD // 2]], axis=1)
    arrays = {
        "x": x, "x_T": x.T, "w_in_T": g["L0_attn_in_proj_weight"].T, "b_in": g["L0_attn_in_proj_bias"],
        "pe_edges": np.tile(pe[::2 * CLIP], (1, GROUP)), "rel_T": pe.T,
        "w_out_T": g["L0_attn_out_w"].T, "b_out": g["L0_attn_out_b"],
        "w_qkv": g["L0_ffn_wqkv"], "qk_rows": np.concatenate([qs, ks, swap(qs), swap(ks)], axis=1),
        "w_o": g["L0_ffn_wo"], "ln_gb": np.stack([g["L0_ffn_ln_g"], g["L0_ffn_ln_b"]], axis=1),
        "w_1": g["L0_ffn_w1"], "b_1": g["L0_ffn_b1"], "w_2": g["L0_ffn_w2"], "b_2": g["L0_ffn_b2"],
        **shape_constants(),
    }
    nc = bacc.Bacc("TRN2", target_bir_lowering=False, num_devices=1)
    ins, feed = {}, {}
    for name, a in arrays.items():
        a = np.ascontiguousarray(a)
        feed[f"in_{name}"] = a
        ins[name] = nc.dram_tensor(f"in_{name}", a.shape, mybir.dt.from_np(a.dtype), kind="ExternalInput").ap()
    out = nc.dram_tensor("out_tokens", (N, E), F32, kind="ExternalOutput").ap()
    build(nc, ins, out)
    r = run_bass_kernel_spmd(nc, [feed], core_ids=[0])
    return r.results[0]["out_tokens"].reshape(1, N, E)
```
